# Optimizing a Trainium2 kernel written in Bass

```python
import numpy as np
import jax
import jax.numpy as jnp

def _softmax(x, axis=-1):
    return jax.nn.softmax(x, axis=axis)

def _gelu(x):
    return jax.nn.gelu(x, approximate=True)

def _silu(x):
    return jax.nn.silu(x)

def _sigmoid(x):
    return jax.nn.sigmoid(x)

def _layernorm(x, axis=-1, eps=1e-05):
    m = jnp.mean(x, axis=axis, keepdims=True)
    v = jnp.var(x, axis=axis, keepdims=True)
    return (x - m) / jnp.sqrt(v + eps)

def _scatter_add(tgt, idx, src, axis=0):
    return tgt.at[idx].add(src)

def _segment_sum(src, seg, n):
    return jax.ops.segment_sum(src, seg, n)
kernel_name = 'mk_decoder_postln_d1_seqx_r8_448005'

def setup_inputs(seed: int=0):
    np.random.seed(seed)
    _w = jnp.asarray

    def _rec_inputs():
        import jax
        import jax.numpy as jnp
        _rk = jax.random.key(seed)
        x = -0.0002928 + 1 * jax.random.normal(jax.random.fold_in(_rk, 1), (16, 64, 128), jnp.float32)
        _lenS = 64 - jax.random.randint(jax.random.fold_in(_rk, 7), (16,), 0, max(1, 64 // 4) + 1, jnp.int32)
        _lenS2 = 64 - jax.random.randint(jax.random.fold_in(_rk, 8), (16,), 0, max(1, 64 // 4) + 1, jnp.int32)
        _ctx_1024P = jax.random.normal(jax.random.fold_in(_rk, 11), (16, 16, 128), jnp.float32)
        _ctx_1024c = jax.random.dirichlet(jax.random.fold_in(_rk, 511), 0.3 * jnp.ones((16,), jnp.float32), (16, 64))
        _ctx_1024t = jnp.einsum('bsk,bkd->bsd', _ctx_1024c, _ctx_1024P)
        _ctx_1024t = _ctx_1024t * jax.lax.rsqrt(jnp.mean(jnp.square(_ctx_1024t)) + 1e-12) * 0.953939
        ctx_1024 = 4.13588e-05 + 0.999923 * (_ctx_1024t + 0.3 * jax.random.normal(jax.random.fold_in(_rk, 611), (16, 64, 128), jnp.float32))
        _validS = jnp.arange(64)[None, :] < _lenS[:, None]
        _validS2 = jnp.arange(64)[None, :] < _lenS2[:, None]
        _causal = jnp.tril(jnp.ones((64, 64), dtype=bool))
        mask_BxS2_bk0 = jnp.logical_not(jnp.broadcast_to(_validS2[:, :], (16, 64)))
        return (x, ctx_1024, mask_BxS2_bk0)
    x, ctx_1024, mask_BxS2_bk0 = _rec_inputs()

    def _L0_attn_setup():
        import jax, jax.numpy as jnp
        import numpy as np
        from jax import lax
        B, T, H = (4, 128, 128)
        NH, KD, VD = (4, 64, 128)
        DK, DV = (KD // NH, VD // NH)
        R, R5, G = (32, 160, 64)
        EPS = 1e-05

        def _forward(h, x_proj_mu, xl_w1, xl_w2, xl_b2, x_out_w, x_bias, r_w, w_w1, w_w2, w_b, k_w, v_w, g_w, bonus, gn_weight, gn_bias, o_w):
            B_, T_, H_ = h.shape
            shifted = jnp.pad(h, ((0, 0), (1, 0), (0, 0)))[:, :T_]
            delta = shifted - h
            x_lerp = h + delta * x_proj_mu
            x0 = jnp.tanh(x_lerp @ xl_w1.T) @ xl_w2.T + xl_b2
            x1 = jnp.tanh(x0).reshape(B_, T_, 5, R)
            x2 = jnp.einsum('btnr,hnr->btnh', x1, x_out_w.reshape(H_, 5, R))
            mus = x2 + x_bias
            r_mu, w_mu, k_mu, v_mu, g_mu = (mus[:, :, i] for i in range(5))
            r = (h + delta * r_mu) @ r_w.T
            w_in = h + delta * w_mu
            w = jnp.tanh(w_in @ w_w1.T) @ w_w2.T + w_b
            k = (h + delta * k_mu) @ k_w.T
            v = (h + delta * v_mu) @ v_w.T
            g = (h + delta * g_mu) @ g_w.T
            r = r.reshape(B_, T_, NH, DK)
            k = k.reshape(B_, T_, NH, DK)
            v = v.reshape(B_, T_, NH, DV)
            wd = jnp.exp(-jnp.exp(w.reshape(B_, T_, NH, DK)))

            def step(S, xs):
                r_t, k_t, v_t, w_t = xs
                o_t = jnp.einsum('bhk,bhkv->bhv', r_t, S) + jnp.sum(r_t * bonus * k_t, -1, keepdims=True) * v_t
                S = S * w_t[..., None] + k_t[..., None] * v_t[..., None, :]
                return (S, o_t)
            xs = tuple((jnp.swapaxes(a, 0, 1) for a in (r, k, v, wd)))
            S0 = jnp.zeros((B_, NH, DK, DV), jnp.float32)
            _, oT = lax.scan(step, S0, xs)
            o = jnp.swapaxes(oT, 0, 1)
            mean = o.mean(-1, keepdims=True)
            var = o.var(-1, keepdims=True)
            o = ((o - mean) * lax.rsqrt(var + EPS)).reshape(B_, T_, VD)
            o = (o * gn_weight + gn_bias) * jax.nn.silu(g)
            return o @ o_w.T
        key = jax.random.key(seed)
        ks = jax.random.split(key, 20)
        n = lambda k, s, sc=0.02: jax.random.normal(k, s, dtype=jnp.float32) * sc
        return {'hidden_states': jax.random.normal(ks[0], (B, T, H), dtype=jnp.float32), 'x_proj_mu': n(ks[1], (H,), 0.1), 'xl_w1': n(ks[2], (R, H)), 'xl_w2': n(ks[3], (R5, R)), 'xl_b2': jnp.zeros((R5,), jnp.float32), 'x_out_w': n(ks[4], (H, R5)), 'x_bias': n(ks[5], (5, H), 0.1), 'r_w': n(ks[6], (KD, H)), 'w_w1': n(ks[7], (G, H)), 'w_w2': n(ks[8], (KD, G)), 'w_b': n(ks[9], (KD,), 0.1), 'k_w': n(ks[10], (KD, H)), 'v_w': n(ks[11], (VD, H)), 'g_w': n(ks[12], (VD, H)), 'bonus': n(ks[13], (NH, DK), 0.1), 'gn_weight': jnp.ones((VD,), jnp.float32), 'gn_bias': jnp.zeros((VD,), jnp.float32), 'o_w': n(ks[14], (H, VD))}
    _L0_attn_all = _L0_attn_setup()
    _L0_attn_in = {k: v for k, v in _L0_attn_all.items() if k in ('x_proj_mu', 'xl_w1', 'xl_w2', 'xl_b2', 'x_out_w', 'x_bias', 'r_w', 'w_w1', 'w_w2', 'w_b', 'k_w', 'v_w', 'g_w', 'bonus', 'gn_weight', 'gn_bias', 'o_w')}
    del _L0_attn_all

    def _L0_xattn_setup():
        import jax, jax.numpy as jnp
        import numpy as np
        D_MODEL = 128
        N_HEAD = 16
        D_H = D_MODEL // N_HEAD
        key = jax.random.key(seed)
        ks = jax.random.split(key, 12)
        B, LQ, LK = (4, 128, 256)
        s = 1.0 / np.sqrt(D_MODEL)
        inp = {'q_input': jax.random.normal(ks[0], (B, LQ, D_MODEL), jnp.float32), 'kv_input': jax.random.normal(ks[1], (B, LK, D_MODEL), jnp.float32), 'key_padding_mask': jax.random.randint(ks[2], (B, LK), 0, 2) > 0, 'W_Q': jax.random.normal(ks[3], (D_MODEL, D_MODEL), jnp.float32) * s, 'b_Q': jnp.zeros((D_MODEL,), jnp.float32), 'W_K': jax.random.normal(ks[4], (D_MODEL, D_MODEL), jnp.float32) * s, 'b_K': jnp.zeros((D_MODEL,), jnp.float32), 'W_V': jax.random.normal(ks[5], (D_MODEL, D_MODEL), jnp.float32) * s, 'b_V': jnp.zeros((D_MODEL,), jnp.float32), 'W_O': jax.random.normal(ks[6], (D_MODEL, D_MODEL), jnp.float32) * s, 'b_O': jnp.zeros((D_MODEL,), jnp.float32)}
        return inp
    _L0_xattn_all = _L0_xattn_setup()
    _L0_xattn_in = {k: v for k, v in _L0_xattn_all.items() if k in ('W_Q', 'b_Q', 'W_K', 'b_K', 'W_V', 'b_V', 'W_O', 'b_O')}
    del _L0_xattn_all

    def _L0_ffn_setup():
        import jax, jax.numpy as jnp
        import numpy as np
        import math
        B, S, D = (4, 256, 128)
        E, DFF = (16, 256)
        CAP_FACTOR = 2.0
        ROUTER_HIDDEN = 128
        CAPACITY = int(math.ceil(S * CAP_FACTOR / E))
        key = jax.random.key(seed)
        ks = jax.random.split(key, 6)

        def uinit(k, shape, fan_in):
            bound = math.sqrt(3.0) * math.sqrt(1.0 / 3.0) / math.sqrt(fan_in)
            return jax.random.uniform(k, shape, jnp.float32, -bound, bound)
        return {'hidden_states': jax.random.normal(ks[0], (B, S, D), jnp.float32), 'router_w1': jax.random.normal(ks[1], (D, ROUTER_HIDDEN), jnp.float32) / math.sqrt(D), 'router_w2': jax.random.normal(ks[2], (ROUTER_HIDDEN, E), jnp.float32) / math.sqrt(ROUTER_HIDDEN), 'w1': uinit(ks[3], (E, D, DFF), D), 'w2': uinit(ks[4], (E, D, DFF), D), 'w3': uinit(ks[5], (E, DFF, D), DFF)}
    _L0_ffn_all = _L0_ffn_setup()
    _L0_ffn_in = {k: v for k, v in _L0_ffn_all.items() if k in ('router_w1', 'router_w2', 'w1', 'w2', 'w3')}
    del _L0_ffn_all
    return {'x': x, 'ctx_1024': ctx_1024, 'mask_BxS2_bk0': mask_BxS2_bk0, 'L0_attn_x_proj_mu': _L0_attn_in['x_proj_mu'], 'L0_attn_xl_w1': _L0_attn_in['xl_w1'], 'L0_attn_xl_w2': _L0_attn_in['xl_w2'], 'L0_attn_xl_b2': _L0_attn_in['xl_b2'], 'L0_attn_x_out_w': _L0_attn_in['x_out_w'], 'L0_attn_x_bias': _L0_attn_in['x_bias'], 'L0_attn_r_w': _L0_attn_in['r_w'], 'L0_attn_w_w1': _L0_attn_in['w_w1'], 'L0_attn_w_w2': _L0_attn_in['w_w2'], 'L0_attn_w_b': _L0_attn_in['w_b'], 'L0_attn_k_w': _L0_attn_in['k_w'], 'L0_attn_v_w': _L0_attn_in['v_w'], 'L0_attn_g_w': _L0_attn_in['g_w'], 'L0_attn_bonus': _L0_attn_in['bonus'], 'L0_attn_gn_weight': _L0_attn_in['gn_weight'], 'L0_attn_gn_bias': _L0_attn_in['gn_bias'], 'L0_attn_o_w': _L0_attn_in['o_w'], 'L0_xattn_W_Q': _L0_xattn_in['W_Q'], 'L0_xattn_b_Q': _L0_xattn_in['b_Q'], 'L0_xattn_W_K': _L0_xattn_in['W_K'], 'L0_xattn_b_K': _L0_xattn_in['b_K'], 'L0_xattn_W_V': _L0_xattn_in['W_V'], 'L0_xattn_b_V': _L0_xattn_in['b_V'], 'L0_xattn_W_O': _L0_xattn_in['W_O'], 'L0_xattn_b_O': _L0_xattn_in['b_O'], 'L0_ffn_router_w1': _L0_ffn_in['router_w1'], 'L0_ffn_router_w2': _L0_ffn_in['router_w2'], 'L0_ffn_w1': _L0_ffn_in['w1'], 'L0_ffn_w2': _L0_ffn_in['w2'], 'L0_ffn_w3': _L0_ffn_in['w3']}

def reference(x, ctx_1024, mask_BxS2_bk0, L0_attn_x_proj_mu, L0_attn_xl_w1, L0_attn_xl_w2, L0_attn_xl_b2, L0_attn_x_out_w, L0_attn_x_bias, L0_attn_r_w, L0_attn_w_w1, L0_attn_w_w2, L0_attn_w_b, L0_attn_k_w, L0_attn_v_w, L0_attn_g_w, L0_attn_bonus, L0_attn_gn_weight, L0_attn_gn_bias, L0_attn_o_w, L0_xattn_W_Q, L0_xattn_b_Q, L0_xattn_W_K, L0_xattn_b_K, L0_xattn_W_V, L0_xattn_b_V, L0_xattn_W_O, L0_xattn_b_O, L0_ffn_router_w1, L0_ffn_router_w2, L0_ffn_w1, L0_ffn_w2, L0_ffn_w3):
    import jax
    import jax.numpy as jnp

    def _L0_attn_ref(hidden_states, x_proj_mu, xl_w1, xl_w2, xl_b2, x_out_w, x_bias, r_w, w_w1, w_w2, w_b, k_w, v_w, g_w, bonus, gn_weight, gn_bias, o_w):
        import jax, jax.numpy as jnp
        import numpy as np
        from jax import lax
        B, T, H = (4, 128, 128)
        NH, KD, VD = (4, 64, 128)
        DK, DV = (KD // NH, VD // NH)
        R, R5, G = (32, 160, 64)
        EPS = 1e-05

        def _forward(h, x_proj_mu, xl_w1, xl_w2, xl_b2, x_out_w, x_bias, r_w, w_w1, w_w2, w_b, k_w, v_w, g_w, bonus, gn_weight, gn_bias, o_w):
            B_, T_, H_ = h.shape
            shifted = jnp.pad(h, ((0, 0), (1, 0), (0, 0)))[:, :T_]
            delta = shifted - h
            x_lerp = h + delta * x_proj_mu
            x0 = jnp.tanh(x_lerp @ xl_w1.T) @ xl_w2.T + xl_b2
            x1 = jnp.tanh(x0).reshape(B_, T_, 5, R)
            x2 = jnp.einsum('btnr,hnr->btnh', x1, x_out_w.reshape(H_, 5, R))
            mus = x2 + x_bias
            r_mu, w_mu, k_mu, v_mu, g_mu = (mus[:, :, i] for i in range(5))
            r = (h + delta * r_mu) @ r_w.T
            w_in = h + delta * w_mu
            w = jnp.tanh(w_in @ w_w1.T) @ w_w2.T + w_b
            k = (h + delta * k_mu) @ k_w.T
            v = (h + delta * v_mu) @ v_w.T
            g = (h + delta * g_mu) @ g_w.T
            r = r.reshape(B_, T_, NH, DK)
            k = k.reshape(B_, T_, NH, DK)
            v = v.reshape(B_, T_, NH, DV)
            wd = jnp.exp(-jnp.exp(w.reshape(B_, T_, NH, DK)))

            def step(S, xs):
                r_t, k_t, v_t, w_t = xs
                o_t = jnp.einsum('bhk,bhkv->bhv', r_t, S) + jnp.sum(r_t * bonus * k_t, -1, keepdims=True) * v_t
                S = S * w_t[..., None] + k_t[..., None] * v_t[..., None, :]
                return (S, o_t)
            xs = tuple((jnp.swapaxes(a, 0, 1) for a in (r, k, v, wd)))
            S0 = jnp.zeros((B_, NH, DK, DV), jnp.float32)
            _, oT = lax.scan(step, S0, xs)
            o = jnp.swapaxes(oT, 0, 1)
            mean = o.mean(-1, keepdims=True)
            var = o.var(-1, keepdims=True)
            o = ((o - mean) * lax.rsqrt(var + EPS)).reshape(B_, T_, VD)
            o = (o * gn_weight + gn_bias) * jax.nn.silu(g)
            return o @ o_w.T
        return _forward(hidden_states, x_proj_mu, xl_w1, xl_w2, xl_b2, x_out_w, x_bias, r_w, w_w1, w_w2, w_b, k_w, v_w, g_w, bonus, gn_weight, gn_bias, o_w)

    def _L0_xattn_ref(q_input, kv_input, key_padding_mask, W_Q, b_Q, W_K, b_K, W_V, b_V, W_O, b_O):
        import jax, jax.numpy as jnp
        import numpy as np
        D_MODEL = 128
        N_HEAD = 16
        D_H = D_MODEL // N_HEAD
        B, LQ, _ = q_input.shape
        LK = kv_input.shape[1]
        q = q_input @ W_Q + b_Q
        k = kv_input @ W_K + b_K
        v = kv_input @ W_V + b_V
        q = q.reshape(B, LQ, N_HEAD, D_H).transpose(0, 2, 1, 3)
        k = k.reshape(B, LK, N_HEAD, D_H).transpose(0, 2, 1, 3)
        v = v.reshape(B, LK, N_HEAD, D_H).transpose(0, 2, 1, 3)
        sim = jnp.einsum('bhqd,bhkd->bhqk', q, k) / jnp.sqrt(jnp.float32(D_H))
        neg_inf = jnp.finfo(sim.dtype).min
        mask = key_padding_mask[:, None, None, :]
        sim = jnp.where(mask, neg_inf, sim)
        attn = jax.nn.softmax(sim, axis=-1)
        out = jnp.einsum('bhqk,bhkd->bhqd', attn, v)
        out = out.transpose(0, 2, 1, 3).reshape(B, LQ, D_MODEL)
        return out @ W_O + b_O

    def _L0_ffn_ref(hidden_states, router_w1, router_w2, w1, w2, w3):
        import jax, jax.numpy as jnp
        import numpy as np
        import math
        B, S, D = (4, 256, 128)
        E, DFF = (16, 256)
        CAP_FACTOR = 2.0
        ROUTER_HIDDEN = 128
        CAPACITY = int(math.ceil(S * CAP_FACTOR / E))
        b, s, d = hidden_states.shape
        e = w1.shape[0]
        cap = CAPACITY
        router_logits = jax.nn.silu(hidden_states @ router_w1) @ router_w2
        expert_probs = jax.nn.softmax(router_logits.transpose(0, 2, 1), axis=-1)
        expert_weights, token_indices = jax.lax.top_k(expert_probs, cap)
        expert_weights = expert_weights / (expert_weights.sum(-1, keepdims=True) + 1e-09)
        expert_inputs = jax.vmap(lambda h, i: h[i])(hidden_states, token_indices)
        gate = jax.nn.silu(jnp.einsum('becd,edf->becf', expert_inputs, w1))
        value = jnp.einsum('becd,edf->becf', expert_inputs, w2)
        expert_out = jnp.einsum('becf,efd->becd', gate * value, w3)
        weighted = expert_out * expert_weights[..., None]

        def combine(idx, vals):
            return jnp.zeros((s, d), vals.dtype).at[idx.reshape(-1)].add(vals.reshape(-1, d))
        output = jax.vmap(combine)(token_indices, weighted)
        return output
    x = _layernorm(x + _L0_attn_ref(x, L0_attn_x_proj_mu, L0_attn_xl_w1, L0_attn_xl_w2, L0_attn_xl_b2, L0_attn_x_out_w, L0_attn_x_bias, L0_attn_r_w, L0_attn_w_w1, L0_attn_w_w2, L0_attn_w_b, L0_attn_k_w, L0_attn_v_w, L0_attn_g_w, L0_attn_bonus, L0_attn_gn_weight, L0_attn_gn_bias, L0_attn_o_w), axis=-1)
    x = _layernorm(x + _L0_xattn_ref(x, ctx_1024, mask_BxS2_bk0, L0_xattn_W_Q, L0_xattn_b_Q, L0_xattn_W_K, L0_xattn_b_K, L0_xattn_W_V, L0_xattn_b_V, L0_xattn_W_O, L0_xattn_b_O), axis=-1)
    x = _layernorm(x + _L0_ffn_ref(x, L0_ffn_router_w1, L0_ffn_router_w2, L0_ffn_w1, L0_ffn_w2, L0_ffn_w3), axis=-1)
    return x

_drawn_inputs = setup_inputs


def setup_inputs(seed=0):
    import zlib

    import numpy as np

    out = dict(_drawn_inputs(seed))
    spreads = {'L0_attn_xl_b2': (0.0, 0.8),
     'L0_attn_gn_weight': (1.0, 0.6),
     'L0_attn_gn_bias': (0.0, 0.8),
     'L0_xattn_b_Q': (0.0, 0.411),
     'L0_xattn_b_K': (0.0, 0.8),
     'L0_xattn_b_V': (0.0, 0.1),
     'L0_xattn_b_O': (0.0, 0.1)}
    factors = {'L0_attn_x_proj_mu': 8.0,
     'L0_attn_xl_w1': 8.0,
     'L0_attn_xl_w2': 8.0,
     'L0_attn_x_out_w': 8.0,
     'L0_attn_x_bias': 6.903,
     'L0_attn_w_w1': 8.0,
     'L0_attn_w_w2': 8.0,
     'L0_attn_w_b': 8.0,
     'L0_attn_bonus': 8.0,
     'L0_ffn_router_w1': 7.659,
     'L0_ffn_router_w2': 7.532,
     'L0_ffn_w1': 5.905,
     'L0_ffn_w2': 5.716,
     'L0_ffn_w3': 5.696}
    for name, (base, spread) in spreads.items():
        noise = np.random.default_rng([zlib.crc32(name.encode()), seed]).standard_normal(out[name].shape)
        drawn = base * np.exp(spread * noise) if base else spread * noise
        out[name] = jnp.asarray(drawn.astype(out[name].dtype))
    for name, factor in factors.items():
        out[name] = (out[name] * factor).astype(out[name].dtype)
    return out
```

```python
from contextlib import ExitStack

import concourse.bass as bass
from concourse import mybir

F32 = mybir.dt.float32
BF16 = mybir.dt.bfloat16
U8 = mybir.dt.uint8
U32 = mybir.dt.uint32
ALU = mybir.AluOpType
ACT = mybir.ActivationFunctionType
AX_X = mybir.AxisListType.X

P = 128
B, S, D = 16, 64, 128
NPAIR = B // 2
HP = NPAIR // 2
HT = HP * P
NH, DK, DV = 4, 16, 32
XH, XD = 16, 8
R = 32
E, DFF, CAP = 16, 256, 32
EG = 4
EPS = 1e-5
MASKED = -1e30
KRING = 2
WRING = 8
LEVELS = [1, 2, 4, 8, 16, 32]


def decoder_kernel(nc, ap, cols, out):
    with ExitStack() as ctx:
        def sb(name, shape, dt=F32):
            return ctx.enter_context(nc.sbuf_tensor(name, shape, dt))

        def sem(name):
            return ctx.enter_context(nc.semaphore(name))

        shared = sb("shared", [P, 26 * 1024 + 256])
        used = {"early": 0, "late": 0}

        def part_of(when, shape):
            n = 1
            for d in shape[1:]:
                n *= d
            at = used[when]
            used[when] += n
            view = shared[0:shape[0], at:at + n]
            names = "abcdef"[:len(shape) - 1]
            if len(shape) == 2:
                return view
            return view.rearrange(f"p ({' '.join(names)}) -> p {' '.join(names)}", **dict(zip(names, shape[1:])))

        def early(shape):
            return part_of("early", shape)

        def late(shape):
            return part_of("late", shape)

        def over(flat, shape):
            names = "abcdef"[:len(shape) - 1]
            return flat.rearrange(f"p ({' '.join(names)}) -> p {' '.join(names)}", **dict(zip(names, shape[1:])))

        wa = sb("wa", [P, ap["wa"].shape[1]])
        wb = sb("wb", [P, ap["wb"].shape[1]])
        cb = sb("cb", [P, ap["cb"].shape[1]], BF16)
        key_mask = sb("key_mask", [2, NPAIR, S], U8)
        xT = sb("xT", [P, B, S])
        x_tm = sb("x_tm", [P, NPAIR, D])
        ew1 = sb("ew1", [P, WRING, DFF])
        ew2 = sb("ew2", [P, WRING, DFF])
        ew3 = sb("ew3", [P, WRING, 2, D])

        def const(name):
            pack, rows, at, n = cols[name]
            return {"wa": wa, "wb": wb, "cb": cb}[pack][0:rows, at:at + n]

        ident = const("ident")

        shiftd = early([P, 2, 5, HT])
        ctxT = early([P, NPAIR, 2, S])
        delta = early([P, B, S])
        lerp = early([P, 2, HT])
        low_full = early([P, 2, HT])
        low1 = low_full[0:R]
        mixA = early([P, 2, HT])
        mixB = early([R, 2, HT])
        wlow_full = early([P, 2, HT])
        wlow = wlow_full[0:64]
        expw = early([P, 2, HP * S])
        v_tm = early([P, 2, HP, D])
        kbonus = early([P, 2, HP, P])
        kdecay = early([P, 2, HP, P])
        rdecay = early([P, 2, HP * NH, S])
        total = [early([P, 2, HP * NH, S // n]) for n in LEVELS]
        attT = early([P, 2, HP * NH, S])
        gsum = sb("gsum", [P, 2, HP * NH])
        gvar = sb("gvar", [P, 2, HP * NH])
        grstd = sb("grstd", [P, 2, HP * NH])
        oT = sb("oT", [P, 2, HT])
        gate_t = lerp
        gsq = over(low_full.rearrange("p a b -> p (a b)"), [P, 2, HP * NH, DV])
        gcen = over(mixA.rearrange("p a b -> p (a b)"), [P, 2, HP * NH, DV])
        gout = over(wlow_full.rearrange("p a b -> p (a b)"), [P, 2, HP, D])
        gate = over(delta.rearrange("p a b -> p (a b)"), [P, 2, HT])
        minus_half = sb("minus_half", [P, HP * NH])
        res = sb("res", [P, 2, HP, D])
        stats = sb("stats", [P, 2, HP, 6])
        mv = sb("mv", [P, 2, HP, 2])
        veps = sb("veps", [P, 2, HP])
        rstd = sb("rstd", [P, 2, HP])
        x1 = sb("x1", [P, 2, HP, D])
        x2 = sb("x2", [P, 2, HP, D])
        x3 = x1
        xTn = sb("xTn", [P, 2, HT])
        bqs = sb("bqs", [P, 2])
        mask_row = sb("mask_row", [2, NPAIR, S], BF16)
        kc = sb("kc", [P, 2, 2, HP, S])
        khead = sb("khead", [P, 2, KRING, XH // 2, S])
        qdiag = late([P, 2, NPAIR, P])
        vhead = sb("vhead", [P, NPAIR, 2, XH // 2, 2, XD + 1])
        smax = sb("smax", [P, 2, 8])
        scen = late([P, 2, 8, S])
        prob = late([P, 2, 512])
        probT = late([P, 2, 4, P])
        oden = sb("oden", [P, 2, 2, XH])
        oatt = late([P, NPAIR, XH, XD])
        hr = late([P, 2, HT])
        lmax = sb("lmax", [P, 2])
        lexp = late([P, 2, S])
        lsum = sb("lsum", [P, 2])
        lrec = sb("lrec", [P, 2])
        pr = late([P, 2, 2, S])
        topv = sb("topv", [P, 2, CAP])
        topi = sb("topi", [P, 2, CAP], U32)
        topf = sb("topf", [P, 2, CAP])
        tsum = sb("tsum", [P, 2])
        topw = sb("topw", [P, 2, CAP])
        didx = sb("didx", [P, 2, E, CAP], BF16)
        dwgt = late([P, 2, E, CAP])
        pick = late([P, 2, E * CAP])
        pcol = sb("pcol", [P, 2, 2, 4, 8])
        place = late([P, E // EG, B, S])
        used["late"] = max(used["late"], E * B * CAP)
        xg = over(shared[:, 0:E * B * CAP], [P, E, B, CAP])
        sg = late([P, 2, 512])
        hid = late([P, 2, 2, 512])
        yT = late([P, 2, B, EG, CAP])
        y = late([P, 2, 4, D])
        moeT = late([P, 2, HT])

        ps = ctx.enter_context(nc.psum_tensor("ps", [P, 8, 512], F32))

        def bank(hf, i):
            return ps[:, 4 * hf + i, :]

        ld_x, ld_wa, ld_xtm, ld_ctx, ld_wb = sem("ld_x"), sem("ld_wa"), sem("ld_xtm"), sem("ld_ctx"), sem("ld_wb")
        ld_c, ld_e = sem("ld_c"), [sem(f"ld_e{q}") for q in range(4)]
        stored = sem("stored")
        dve_chain, pool_chain, act_chain = sem("dve_chain"), sem("pool_chain"), sem("act_chain")
        names = """zeroed delta_done lerp_done low1_mm low1_done mix_mm mixA_done mixB_done x2_mm muls_done shifted
            r_mm k_mm w1_mm wlow_done w2_mm expw_done tot_ready v_mm g_mm v_done gate_t_done gate_done
            kbonus_done kmix_done kdecay_done rx_ready lvl_mm att_done upd_r upd_k upd_t o_mm gcen_done gsq_done gvar_done
            grstd_done gn_done gw_done gout_done oT_mm oT_done proj_mm veps_done rstd_done x1_done x1T_mm x1T_done
            kv_mm kc_done vhead_done khead_done const_done q_mm qdiag_done s_mm scen_done smax_done prob_done pT_mm
            pT_done pv_mm oatt_done x2_done x2T_mm x2T_done hr_mm hr_done lg_mm lmax_done lexp_done top_done
            didx_done dwgt_done row_mm pick_done xg_mm xg_done col_mm pcol_done eq_done place_done
            up_mm sg_done hid_done y_mm yT_done yTT_mm y_done moe_mm moeT_done fin_mm x3_done""".split()
        s = {n: sem(n) for n in names}
        block = ctx.enter_context(nc.Block())

        @block.sync
        def _(sp):
            sp.dma_start(xT[:].rearrange("p b s -> p (b s)"), ap["xT"]).then_inc(ld_x, 16)
            sp.dma_start(wa[:], ap["wa"]).then_inc(ld_wa, 16)
            sp.dma_start(cb[:], ap["cb"]).then_inc(ld_c, 16)
            sp.dma_start(key_mask[:], ap["key_mask"]).then_inc(ld_c, 16)
            sp.dma_start(ctxT[:].rearrange("p a b s -> p (a b s)"), ap["ctxT"]).then_inc(ld_ctx, 16)
            sp.dma_start(wb[:], ap["wb"]).then_inc(ld_wb, 16)
            sp.dma_start(x_tm[:], ap["x"].rearrange("(n a) s d -> (a s) n d", a=2)).then_inc(ld_xtm, 16)
            for q in range(4):
                es = slice(4 * q, 4 * q + 4)
                ws = slice(4 * q % WRING, 4 * q % WRING + 4)
                if 4 * q >= WRING:
                    sp.wait_ge(s["y_mm"], 4 * q - WRING + 4)
                sp.dma_start(ew1[:, ws, :], ap["w1"][es].rearrange("e d f -> d e f")).then_inc(ld_e[q], 16)
                sp.dma_start(ew2[:, ws, :], ap["w2"][es].rearrange("e d f -> d e f")).then_inc(ld_e[q], 16)
                for f in range(2):
                    sp.dma_start(ew3[:, ws, f, :], ap["w3"][es, f * P:(f + 1) * P, :].rearrange("e f d -> f e d")).then_inc(ld_e[q], 16)
            for hf in range(2):
                sp.wait_ge(s["x3_done"], hf + 1)
                sp.dma_start(out[8 * hf:8 * hf + 8].rearrange("(n a) s d -> (a s) n d", a=2), x3[:, hf]).then_inc(stored, 16)
            sp.wait_ge(stored, 32)

        @block.tensor
        def _(pe):
            pe.wait_ge(ld_wa, 16)
            for hf in range(2):
                pe.wait_ge(s["lerp_done"], hf + 1)
                pe.matmul(bank(hf, 0)[0:R, :], const("xl_w1T"), lerp[:, hf, :], start=True, stop=True).then_inc(s["low1_mm"], 1)
            for hf in range(2):
                pe.wait_ge(s["low1_done"], hf + 1)
                pe.matmul(bank(hf, 1), const("xl_w2T")[:, 0:P], low1[:, hf, :], start=True, stop=True).then_inc(s["mix_mm"], 1)
                pe.matmul(bank(hf, 2)[0:R, :], const("xl_w2T")[:, P:], low1[:, hf, :], start=True, stop=True).then_inc(s["mix_mm"], 1)
            slot = [0, 3, 1, 2, 0]
            for n in range(5):
                for hf in range(2):
                    if n == 0:
                        pe.wait_ge(s["mixA_done"], hf + 1)
                    if n == 3:
                        pe.wait_ge(s["mixB_done"], hf + 1)
                    if n == 4:
                        pe.wait_ge(s["muls_done"], hf + 1)
                    if n < 4:
                        pe.matmul(bank(hf, slot[n]), const("xout")[n * R:(n + 1) * R, :], mixA[n * R:(n + 1) * R, hf, :],
                                  start=True, stop=True).then_inc(s["x2_mm"], 1)
                    else:
                        pe.matmul(bank(hf, slot[n]), const("xout4"), mixB[:, hf, :], start=True, stop=True).then_inc(s["x2_mm"], 1)

            def split(n, hf, w, b, at):
                src = shiftd[:, hf, n, :].rearrange("p (n a s) -> p a n s", a=2, s=S)
                for par in range(2):
                    mm = pe.matmul(bank(hf, b)[64 * par:64 * par + 64, at:at + HP * S], w, src[:, par],
                                   start=True, stop=True)
                return mm

            for hf in range(2):
                pe.wait_ge(s["shifted"], 0 * 2 + hf + 1)
                pe.wait_ge(s["muls_done"], 2 + hf + 1)
                split(0, hf, const("r_wT"), 3, 0).then_inc(s["r_mm"], 1)
            for hf in range(2):
                pe.wait_ge(s["shifted"], 2 + hf + 1)
                pe.wait_ge(s["muls_done"], 4 + hf + 1)
                pe.matmul(bank(hf, 1)[0:64, :], const("w_w1T"), shiftd[:, hf, 1, :], start=True, stop=True).then_inc(s["w1_mm"], 1)
            for hf in range(2):
                pe.wait_ge(s["shifted"], 4 + hf + 1)
                pe.wait_ge(s["rx_ready"], hf + 1)
                split(2, hf, const("k_wT"), 3, HP * S).then_inc(s["k_mm"], 1)
            for hf in range(2):
                pe.wait_ge(s["wlow_done"], hf + 1)
                src = wlow[:, hf, :].rearrange("p (n a s) -> p a n s", a=2, s=S)
                for par in range(2):
                    mm = pe.matmul(bank(hf, 1)[64 * par:64 * par + 64, 0:HP * S], const("w_w2T"), src[:, par],
                                   start=True, stop=True)
                mm.then_inc(s["w2_mm"], 1)
            for hf in range(2):
                pe.wait_ge(s["shifted"], 6 + hf + 1)
                pe.wait_ge(s["muls_done"], 6 + hf + 1)
                for n in range(HP):
                    mm = pe.matmul(bank(hf, 2)[:, n * D:(n + 1) * D], shiftd[:, hf, 3, n * P:(n + 1) * P], const("v_wT"),
                                   start=True, stop=True)
                mm.then_inc(s["v_mm"], 1)
            for hf in range(2):
                pe.wait_ge(s["shifted"], 8 + hf + 1)
                for n in range(HP):
                    mm = pe.matmul(bank(hf, 0)[:, n * D:(n + 1) * D], shiftd[:, hf, 4, n * P:(n + 1) * P], const("g_wT"),
                                   start=True, stop=True)
                mm.then_inc(s["g_mm"], 1)
            pe.wait_ge(ld_ctx, 16)
            pe.wait_ge(ld_wb, 16)
            for hf in range(2):
                pe.wait_ge(s["expw_done"], hf + 1)
                for g in range(2):
                    for par in range(2):
                        mm = pe.matmul(bank(hf, 1)[64 * par:64 * par + 64, g * 256:(g + 1) * 256], const("W_K")[:, 64 * g:64 * g + 64],
                                       ctxT[:, HP * hf:HP * hf + HP, par, :], start=True, stop=True)
                mm.then_inc(s["kv_mm"], 1)
            for hf in range(2):
                pe.wait_ge(s["gate_done"], hf + 1)
                for hh in range(2):
                    for b in range(8):
                        mm = pe.matmul(bank(hf, 0)[64 * hh:64 * hh + 64, b * 64:b * 64 + 64], ctxT[:, HP * hf + b // 2, b % 2, :],
                                       const("W_V2")[:, hh * 64:hh * 64 + 64], start=True, stop=True)
                mm.then_inc(s["kv_mm"], 1)
            for step in range(7):
                n = LEVELS[max(step - 1, 0)]
                for hf in range(2):
                    if step == 0:
                        pe.wait_ge(s["kbonus_done"], hf + 1)
                        pe.wait_ge(s["rx_ready"], hf + 1)
                        pe.wait_ge(s["v_done"], hf + 1)
                    elif step == 1:
                        pe.wait_ge(s["kmix_done"], hf + 1)
                        pe.wait_ge(s["kdecay_done"], hf + 1)
                    else:
                        pe.wait_ge(s["upd_r"], 2 * (step - 2) + hf + 1)
                        pe.wait_ge(s["upd_k"], 2 * (step - 2) + hf + 1)
                        pe.wait_ge(s["att_done"], 2 * (step - 2) + hf + 1)
                    stat = kbonus if step < 2 else kdecay
                    for q in range(HP):
                        rd = rdecay[:, hf, q * NH:(q + 1) * NH, :].rearrange("p h (b two n) -> p h b two n", two=2, n=n)[:, :, :, min(step, 1), :]
                        mm = pe.matmul(bank(hf, 2 + step % 2)[:, q * P:(q + 1) * P], stat[:, hf, q, :], rd, start=True, stop=True)
                    mm.then_inc(s["lvl_mm"], 1)
            for hf in range(2):
                pe.wait_ge(s["att_done"], 12 + hf + 1)
                pe.wait_ge(s["vhead_done"], hf + 1)
                for q in range(HP):
                    for par in range(2):
                        rows = slice(64 * par, 64 * par + 64)
                        for h in range(NH):
                            mm = pe.matmul(bank(hf, 0)[rows, q * D + h * DV:q * D + (h + 1) * DV], attT[rows, hf, q * NH + h, :],
                                           v_tm[rows, hf, q, h * DV:(h + 1) * DV], start=True, stop=True)
                mm.then_inc(s["o_mm"], 1)

            def transposes(hf, b, src, signal):
                for q in range(HP):
                    mm = pe.transpose(bank(hf, b)[:, q * P:(q + 1) * P], src[:, q, :], ident)
                mm.then_inc(s[signal], 1)

            for hf in range(2):
                pe.wait_ge(s["gout_done"], hf + 1)
                transposes(hf, 2, gout[:, hf], "oT_mm")
            for hf in range(2):
                pe.wait_ge(s["oT_done"], hf + 1)
                for q in range(HP):
                    mm = pe.matmul(bank(hf, 3)[:, q * P:(q + 1) * P], oT[:, hf, q * P:(q + 1) * P], const("o_wT"), start=True, stop=True)
                mm.then_inc(s["proj_mm"], 1)
            for hf in range(2):
                pe.wait_ge(s["x1_done"], hf + 1)
                transposes(hf, 2, x1[:, hf], "x1T_mm")
            for hf in range(2):
                pe.wait_ge(s["x1T_done"], hf + 1)
                src = xTn[:, hf, :].rearrange("p (n a s) -> p a n s", a=2, s=S)
                for g in range(2):
                    for par in range(2):
                        mm = pe.matmul(bank(hf, 0)[64 * par:64 * par + 64, g * 256:(g + 1) * 256], const("W_Q")[:, 64 * g:64 * g + 64],
                                       src[:, par], start=True, stop=True)
                mm.then_inc(s["q_mm"], 1)
            pe.wait_ge(s["qdiag_done"], 2)
            pe.wait_ge(s["vhead_done"], 2)
            pe.wait_ge(s["kc_done"], 2)
            N2 = 2 * NPAIR

            def scores(i):
                q, g = i // 2, i % 2
                if g == 0:
                    pe.wait_ge(s["khead_done"], q + 1)
                if i >= 2:
                    pe.wait_ge(s["scen_done"], i - 1)
                pe.matmul(ps[:, i % 2, :], qdiag[:, g, q, :], khead[:, g, q % KRING], start=True, stop=False)
                pe.matmul(ps[:, i % 2, :], const("parsel"), mask_row[:, q, None, :].broadcast_to([2, 8, S]),
                          start=False, stop=True).then_inc(s["s_mm"], 1)

            def weigh(i):
                q, g = i // 2, i % 2
                if i >= 2:
                    pe.wait_ge(s["pT_done"], i - 1)
                pe.wait_ge(s["prob_done"], i + 1)
                for c in range(4):
                    mm = pe.transpose(ps[:, 2 + i % 2, c * P:(c + 1) * P], prob[:, i % 2, c * P:(c + 1) * P], ident)
                mm.then_inc(s["pT_mm"], 1)

            def values(i):
                q, g = i // 2, i % 2
                pe.wait_ge(s["pT_done"], i + 1)
                if q >= 4 and g == 0:
                    pe.wait_ge(s["oatt_done"], q // 2 - 1)
                o = ps[:, 4 + q % 4, 0:288].rearrange("p (a c x) -> p a c x", a=2, c=8)
                for c in range(4):
                    mm = pe.matmul(o[:, :, 4 * g + c, :], probT[:, i % 2, c, :],
                                   vhead[:, q, :, 4 * g + c].rearrange("p a h x -> p a (h x)"), start=True, stop=True)
                mm.then_inc(s["pv_mm"], 1)

            for i in range(N2 + 2):
                if i < N2:
                    scores(i)
                if 1 <= i < N2 + 1:
                    weigh(i - 1)
                if i >= 2:
                    values(i - 2)
            for hf in range(2):
                if hf == 0:
                    pe.wait_ge(s["oatt_done"], 2)
                    pe.wait_ge(s["pT_done"], 2 * NPAIR)
                else:
                    pe.wait_ge(s["oatt_done"], 4)
                transposes(hf, 2, oatt[:, HP * hf:HP * hf + HP].rearrange("p n h d -> p n (h d)"), "oT_mm")
            for hf in range(2):
                pe.wait_ge(s["oT_done"], 2 + hf + 1)
                for q in range(HP):
                    mm = pe.matmul(bank(hf, 3)[:, q * P:(q + 1) * P], oT[:, hf, q * P:(q + 1) * P], const("W_O"), start=True, stop=True)
                mm.then_inc(s["proj_mm"], 1)
            for hf in range(2):
                pe.wait_ge(s["x2_done"], hf + 1)
                transposes(hf, 2, x2[:, hf], "x2T_mm")
            for hf in range(2):
                pe.wait_ge(s["x2T_done"], hf + 1)
                pe.matmul(bank(hf, 0), const("router_w1"), xTn[:, hf, :], start=True, stop=True).then_inc(s["hr_mm"], 1)
            for hf in range(2):
                pe.wait_ge(s["hr_done"], hf + 1)
                for b in range(8):
                    mm = pe.matmul(bank(hf, 1)[:, 0:S], const("router_w2")[:, (7 - b) * E:(7 - b) * E + P], hr[:, hf, b * S:(b + 1) * S],
                                   start=(b == 0), stop=(b == 7))
                mm.then_inc(s["lg_mm"], 1)
            for hf in range(2):
                pe.wait_ge(s["didx_done"], hf + 1)
                pe.wait_ge(s["dwgt_done"], hf + 1)
                for eg in range(4):
                    pe.matmul(bank(hf, 1)[:, 128 + eg * 8:136 + eg * 8], didx[:, hf, EG * eg:EG * eg + EG, :].rearrange("p e j -> p (e j)"),
                              const("bsel8b"), start=True, stop=True)
                    mm = pe.matmul(bank(hf, 1)[:, 192 + eg * 8:200 + eg * 8], dwgt[:, hf, EG * eg:EG * eg + EG, :].rearrange("p e j -> p (e j)"),
                                   const("bsel8"), start=True, stop=True)
                mm.then_inc(s["col_mm"], 1)
            for q in range(NPAIR):
                hf = q // HP
                if q >= 2:
                    pe.wait_ge(s["pick_done"], q - 1)
                pe.matmul(bank(q % 2, 2), const("bsel")[:, (q % HP) * P:(q % HP + 1) * P],
                          didx[:, hf].rearrange("p e j -> p (e j)"), start=True, stop=True).then_inc(s["row_mm"], 1)
                pe.wait_ge(s["pick_done"], q + 1)
                if q >= 1:
                    pe.wait_ge(s["xg_done"], 2 * q)
                for par in range(2):
                    rows = slice(64 * par, 64 * par + 64)
                    pe.matmul(bank(par, 3), x2[rows, hf, q % HP, :], pick[rows, q % 2, :], start=True, stop=True).then_inc(s["xg_mm"], 1)
            pe.wait_ge(s["pcol_done"], 2)
            pe.wait_ge(s["xg_done"], B)

            def up(e):
                if e % 4 == 0:
                    pe.wait_ge(ld_e[e // 4], 64)
                for f in range(2):
                    if e >= 1:
                        pe.wait_ge(s["hid_done"], 2 * (e - 1) + f + 1)
                    pe.matmul(ps[:, 2 * f, :], ew1[:, e % WRING, f * P:(f + 1) * P], xg[:, e].rearrange("p b j -> p (b j)"), start=True, stop=True)
                    pe.matmul(ps[:, 2 * f + 1, :], ew2[:, e % WRING, f * P:(f + 1) * P], xg[:, e].rearrange("p b j -> p (b j)"),
                              start=True, stop=True).then_inc(s["up_mm"], 1)

            def down(e):
                pe.wait_ge(s["hid_done"], 2 * e + 2)
                if e >= 1:
                    pe.wait_ge(s["yT_done"], e)
                pe.matmul(ps[:, 4, :], ew3[:, e % WRING, 0, :], hid[:, e % 2, 0, :], start=True, stop=False)
                pe.matmul(ps[:, 4, :], ew3[:, e % WRING, 1, :], hid[:, e % 2, 1, :], start=False, stop=True).then_inc(s["y_mm"], 1)

            def scatter(eg, t):
                k = 4 * eg + t
                pe.wait_ge(s["yT_done"], EG * eg + EG)
                if k >= 1:
                    pe.wait_ge(s["y_done"], k)
                for b in range(4):
                    mm = pe.transpose(ps[:, 5, b * P:(b + 1) * P], yT[:, eg % 2, 4 * t + b].rearrange("p e j -> p (e j)"), ident)
                mm.then_inc(s["yTT_mm"], 1)
                pe.wait_ge(s["y_done"], k + 1)
                if k == 0:
                    pe.wait_ge(s["place_done"], 1)
                for b in range(4):
                    bb = 4 * t + b
                    mm = pe.matmul(ps[:, 6 + bb // 8, (bb % 8) * S:(bb % 8 + 1) * S], y[:, k % 2, b, :], place[:, eg, bb, :],
                                   start=(eg == 0 and bb % 8 == 0), stop=(eg == 3), skip_group_check=True)
                mm.then_inc(s["moe_mm"], 1)

            for e in range(E + 1):
                if e < E:
                    up(e)
                if e >= 1:
                    down(e - 1)
                if e >= 5:
                    scatter((e - 5) // 4, (e - 5) % 4)
            for t in range(4):
                scatter(3, t)
            for hf in range(2):
                pe.wait_ge(s["moeT_done"], hf + 1)
                transposes(hf, 0, moeT[:, hf, :].rearrange("p (q t) -> p q t", q=HP), "fin_mm")

        @block.gpsimd
        def _(pool):
            done = [0]

            def link(ins):
                done[0] += 1
                ins.then_inc(pool_chain, 1)
                pool.wait_ge(pool_chain, done[0])

            pool.wait_ge(ld_x, 16)
            link(pool.tensor_tensor(delta[:, :, 1:S], xT[:, :, 0:S - 1], xT[:, :, 1:S], ALU.subtract))
            pool.tensor_scalar(delta[:, :, 0:1], xT[:, :, 0:1], -1.0, None, ALU.mult).then_inc(s["delta_done"], 1)
            for t in (kbonus, kdecay):
                pool.memset(t[:], 0.0).then_inc(s["zeroed"], 1)
            pool.memset(minus_half[:], -0.5).then_inc(s["const_done"], 1)
            xh = xT[:].rearrange("p (f b) s -> p f (b s)", f=2)
            for n in range(5):
                for hf in range(2):
                    pool.wait_ge(s["muls_done"], 2 * n + hf + 1)
                    pool.tensor_tensor(shiftd[:, hf, n, :], shiftd[:, hf, n, :], xh[:, hf, :], ALU.add).then_inc(s["shifted"], 1)
            pool.memset(vhead[:], 0.0).then_inc(s["zeroed"], 1)
            pool.wait_ge(s["zeroed"], 3)
            for hh in range(2):
                link(pool.memset(vhead[64 * hh:64 * hh + 64, :, :, :, hh, XD:XD + 1].rearrange("p n a c x -> p (n a c) x"), 1.0))
            pool.wait_ge(s["g_mm"], 2)
            pool.memset(qdiag[:], 0.0).then_inc(s["zeroed"], 1)
            pool.wait_ge(s["kdecay_done"], 2)
            for lv in range(5):
                n = LEVELS[lv]
                for hf in range(2):
                    if lv == 0:
                        pool.wait_ge(s["tot_ready"], hf + 1)
                    if lv >= 1:
                        pool.wait_ge(s["upd_t"], 2 * (lv - 1) + hf + 1)
                        pool.wait_ge(s["lvl_mm"], 2 * (lv + 1) + hf + 1)
                        pool.wait_ge(s["upd_k"], 2 * (lv - 1) + hf + 1)
                    if 2 * lv + hf >= 1:
                        pool.wait_ge(s["upd_k"], 2 * lv + hf)
                    tot = total[lv][:, hf].rearrange("p g (b two) -> p g b two", two=2)
                    pool.tensor_tensor(total[lv + 1][:, hf], tot[:, :, :, 0], tot[:, :, :, 1], ALU.mult).then_inc(s["upd_t"], 1)
                    pool.wait_ge(s["upd_t"], 2 * lv + hf + 1)
                    for par in range(2):
                        rows = slice(64 * par, 64 * par + 64)
                        kd = kdecay[rows, hf, :, 64 * par:64 * par + 64].rearrange("p q (b two n) -> p q b two n", two=2, n=n)[:, :, :, 0, :]
                        tk = tot[rows].rearrange("p (q h) b two -> p q h b two", h=NH)[:, :, 0, :, 1]
                        mm = pool.tensor_tensor(kd, kd, tk[:, :, :, None].broadcast_to([64, HP, S // (2 * n), n]), ALU.mult)
                        if par == 0:
                            link(mm)
                    mm.then_inc(s["upd_k"], 1)
            pool.wait_ge(s["upd_k"], 10)
            for hf in range(2):
                if hf == 0:
                    pool.wait_ge(s["const_done"], 1)
                pool.wait_ge(s["gvar_done"], hf + 1)
                pool.tensor_tensor(grstd[:, hf], gvar[:, hf], minus_half[:], ALU.pow).then_inc(s["grstd_done"], 1)
            for hf in range(2):
                pool.wait_ge(s["gn_done"], hf + 1)
                g3 = gout[:, hf]
                link(pool.tensor_tensor(g3, g3, const("gnw")[:, None, :].broadcast_to([P, HP, D]), ALU.mult))
                pool.tensor_tensor(g3, g3, const("gnb")[:, None, :].broadcast_to([P, HP, D]), ALU.add).then_inc(s["gw_done"], 1)

            def inverse_deviation(k):
                for hf in range(2):
                    pool.wait_ge(s["veps_done"], 2 * k + hf + 1)
                    pool.tensor_tensor(rstd[:, hf], veps[:, hf], minus_half[:, 0:HP], ALU.pow).then_inc(s["rstd_done"], 1)

            for hf in range(2):
                pool.wait_ge(s["kc_done"], hf + 1)
                for q in range(HP):
                    if hf == 0 and q == KRING:
                        inverse_deviation(0)
                    if HP * hf + q >= KRING:
                        pool.wait_ge(s["s_mm"], 2 * (HP * hf + q - KRING) + 2)
                    for g in range(2):
                        kq = kc[:, hf, g, q, None, :].broadcast_to([P, 8, S])
                        mm = pool.tensor_tensor(khead[:, g, q % KRING], kq, const("hm8")[:, :, None].broadcast_to([P, 8, S]), ALU.mult)
                    mm.then_inc(s["khead_done"], 1)
            inverse_deviation(1)
            for hf in range(2):
                pool.wait_ge(s["eq_done"], hf + 1)
                pl = place[:, :, 8 * hf:8 * hf + 8, :]
                for eg in range(4):
                    mm = pool.tensor_tensor(pl[:, eg], pl[:, eg], pcol[:, hf, 1, eg, :, None].broadcast_to([P, 8, S]), ALU.mult)
            mm.then_inc(s["place_done"], 1)
            inverse_deviation(2)

        @block.scalar
        def _(act):
            done = [0]

            def link(ins):
                done[0] += 1
                ins.then_inc(act_chain, 1)
                act.wait_ge(act_chain, done[0])

            act.wait_ge(ld_wa, 16)
            for hf in range(2):
                act.wait_ge(s["low1_mm"], hf + 1)
                act.activation(low1[:, hf, :], bank(hf, 0)[0:R, :], ACT.Tanh).then_inc(s["low1_done"], 1)
            for hf in range(2):
                act.wait_ge(s["mix_mm"], 2 * hf + 1)
                act.activation(mixA[:, hf, :], bank(hf, 1), ACT.Tanh, bias=const("xl_b2")).then_inc(s["mixA_done"], 1)
                act.wait_ge(s["mix_mm"], 2 * hf + 2)
                act.activation(mixB[:, hf, :], bank(hf, 2)[0:R, :], ACT.Tanh, bias=const("xl_b24")).then_inc(s["mixB_done"], 1)
            for hf in range(2):
                act.wait_ge(s["w1_mm"], hf + 1)
                act.activation(wlow[:, hf, :], bank(hf, 1)[0:64, :], ACT.Tanh).then_inc(s["wlow_done"], 1)
            for hf in range(2):
                act.wait_ge(s["k_mm"], hf + 1)
                if hf == 0:
                    act.wait_ge(s["zeroed"], 2)
                kps = bank(hf, 3)[:, HP * S:].rearrange("p (q s) -> p q s", s=S)
                for par in range(2):
                    rows = slice(64 * par, 64 * par + 64)
                    kb = kbonus[rows, hf, :, 64 * par:64 * par + 64]
                    mm = act.activation(kb, kps[rows], ACT.Copy, scale=const("bonus")[rows])
                mm.then_inc(s["kbonus_done"], 1)
                for par in range(2):
                    rows = slice(64 * par, 64 * par + 64)
                    mm = act.activation(kdecay[rows, hf, :, 64 * par:64 * par + 64], kps[rows], ACT.Copy)
                mm.then_inc(s["kdecay_done"], 1)
            for hf in range(2):
                act.wait_ge(s["w2_mm"], hf + 1)
                act.activation(expw[:, hf, :], bank(hf, 1)[:, 0:HP * S], ACT.Exp, bias=const("w_b")).then_inc(s["expw_done"], 1)
                act.wait_ge(s["expw_done"], hf + 1)
                for h in range(NH):
                    tt = total[0][:, hf].rearrange("p (q h) s -> p q h s", h=NH)[:, :, h, :]
                    mm = act.activation(tt, expw[:, hf, :].rearrange("p (q s) -> p q s", s=S), ACT.Exp, scale=-1.0)
                mm.then_inc(s["tot_ready"], 1)
            for hf in range(2):
                act.wait_ge(s["v_mm"], hf + 1)
                act.activation(v_tm[:, hf].rearrange("p q d -> p (q d)"), bank(hf, 2), ACT.Copy).then_inc(s["v_done"], 1)
            for hf in range(2):
                act.wait_ge(s["g_mm"], hf + 1)
                act.activation(gate_t[:, hf, :], bank(hf, 0), ACT.Tanh, scale=0.5).then_inc(s["gate_t_done"], 1)
            for hf in range(2):
                act.wait_ge(s["lvl_mm"], hf + 1)
                kps = bank(hf, 3)[:, HP * S:].rearrange("p (q s two) -> p q s two", two=2, q=HP)
                for par in range(2):
                    rows = slice(64 * par, 64 * par + 64)
                    ke = kbonus[rows, hf, :, 64 * par:64 * par + 64].rearrange("p q (s two) -> p q s two", two=2)
                    mm = act.activation(ke[:, :, :, 0], kps[rows][:, :, :, 0], ACT.Copy)
                mm.then_inc(s["kmix_done"], 1)
            act.wait_ge(ld_wb, 16)
            for hf in range(2):
                act.wait_ge(s["kv_mm"], hf + 1)
                for g in range(2):
                    mm = act.activation(kc[:, hf, g].rearrange("p q s -> p (q s)"), bank(hf, 1)[:, 256 * g:256 * g + 256], ACT.Identity,
                                        bias=const("b_K")[:, g:g + 1])
                mm.then_inc(s["kc_done"], 1)
            for g in range(2):
                mm = act.activation(bqs[:, g:g + 1], const("b_Q")[:, g:g + 1], ACT.Copy, scale=XD ** -0.5)
            mm.then_inc(s["const_done"], 1)
            for hf in range(2):
                act.wait_ge(s["gcen_done"], hf + 1)
                act.activation(gsq[:, hf], gcen[:, hf], ACT.Square).then_inc(s["gsq_done"], 1)

            def copy_T(dst, b, mm_sem, k, done_sem):
                for hf in range(2):
                    act.wait_ge(s[mm_sem], k + hf + 1)
                    act.activation(dst[:, hf, :], bank(hf, b), ACT.Copy).then_inc(s[done_sem], 1)

            copy_T(oT, 2, "oT_mm", 0, "oT_done")
            copy_T(xTn, 2, "x1T_mm", 0, "x1T_done")
            act.wait_ge(s["const_done"], 2)
            act.wait_ge(s["zeroed"], 4)
            for hf in range(2):
                act.wait_ge(s["q_mm"], hf + 1)
                for g in range(2):
                    for par in range(2):
                        rows = slice(64 * par, 64 * par + 64)
                        mm = act.activation(qdiag[rows, g, HP * hf:HP * hf + HP, 64 * par:64 * par + 64],
                                            bank(hf, 0)[rows, 256 * g:256 * g + 256].rearrange("p (q s) -> p q s", s=S),
                                            ACT.Identity, bias=bqs[rows, g:g + 1], scale=XD ** -0.5)
                mm.then_inc(s["qdiag_done"], 1)
            N2 = 2 * NPAIR
            for i in range(N2 + 1):
                if i < N2:
                    act.wait_ge(s["scen_done"], i + 1)
                    if i >= 2:
                        act.wait_ge(s["pT_mm"], i - 1)
                    act.activation(prob[:, i % 2, :], scen[:, i % 2].rearrange("p h s -> p (h s)"), ACT.Exp).then_inc(s["prob_done"], 1)
                if i >= 1:
                    act.wait_ge(s["pT_mm"], i)
                    if i >= 3:
                        act.wait_ge(s["pv_mm"], i - 2)
                    act.activation(probT[:, (i - 1) % 2].rearrange("p c q -> p (c q)"), ps[:, 2 + (i - 1) % 2, :], ACT.Copy).then_inc(s["pT_done"], 1)
            copy_T(oT, 2, "oT_mm", 2, "oT_done")
            copy_T(xTn, 2, "x2T_mm", 0, "x2T_done")
            for hf in range(2):
                act.wait_ge(s["hr_mm"], hf + 1)
                act.activation(hr[:, hf, :], bank(hf, 0), ACT.Silu).then_inc(s["hr_done"], 1)
            for hf in range(2):
                act.wait_ge(s["lmax_done"], hf + 1)
                act.activation(lexp[:, hf, :], bank(hf, 1)[:, 0:S], ACT.Exp, bias=lmax[:, hf:hf + 1], accum_out=lsum[:, hf:hf + 1]).then_inc(s["lexp_done"], 1)
            for b in range(B):
                act.wait_ge(s["xg_mm"], b + 1)
                act.activation(xg[:, :, b, :], bank(b % 2, 3).rearrange("p (e j) -> p e j", e=E), ACT.Copy).then_inc(s["xg_done"], 1)
            for e in range(E + 1):
                if e < E:
                    for f in range(2):
                        k = 2 * e + f
                        act.wait_ge(s["up_mm"], k + 1)
                        if k >= 2:
                            act.wait_ge(s["hid_done"], k - 1)
                        act.activation(sg[:, f, :], ps[:, 2 * f, :], ACT.Silu).then_inc(s["sg_done"], 1)
                if e >= 1:
                    d = e - 1
                    act.wait_ge(s["y_mm"], d + 1)
                    if d >= 8 and d % 4 == 0:
                        act.wait_ge(s["yTT_mm"], 4 * (d // 4 - 1))
                    act.activation(yT[:, (d // 4) % 2, :, d % 4, :], ps[:, 4, :].rearrange("p (b j) -> p b j", b=B), ACT.Copy).then_inc(s["yT_done"], 1)
            for hf in range(2):
                act.wait_ge(s["moe_mm"], 4 * 3 + 2 * hf + 2)
                act.activation(moeT[:, hf, :], ps[:, 6 + hf, :], ACT.Copy).then_inc(s["moeT_done"], 1)

        @block.vector
        def _(dve):
            done = [0]

            def link(ins):
                done[0] += 1
                ins.then_inc(dve_chain, 1)
                dve.wait_ge(dve_chain, done[0])

            dve.wait_ge(ld_wa, 16)
            dve.wait_ge(s["delta_done"], 1)
            dve.wait_ge(pool_chain, 1)
            xh = xT[:].rearrange("p (f b) s -> p f (b s)", f=2)
            dh = delta[:].rearrange("p (f b) s -> p f (b s)", f=2)
            for hf in range(2):
                dve.scalar_tensor_tensor(lerp[:, hf, :], dh[:, hf], const("mu"), xh[:, hf], ALU.mult, ALU.add).then_inc(s["lerp_done"], 1)
            link(dve.memset(attT[:], 0.0))
            dve.wait_ge(ld_c, 32)
            link(dve.tensor_scalar(mask_row[:], key_mask[:], MASKED, None, ALU.mult))
            slot = [0, 3, 1, 2, 0]
            for n in range(5):
                for hf in range(2):
                    dve.wait_ge(s["x2_mm"], 2 * n + hf + 1)
                    dve.scalar_tensor_tensor(shiftd[:, hf, n, :], bank(hf, slot[n]), const("x_bias")[:, n:n + 1], dh[:, hf],
                                             ALU.add, ALU.mult).then_inc(s["muls_done"], 1)
            for hf in range(2):
                dve.wait_ge(s["r_mm"], hf + 1)
                rps = bank(hf, 3)[:, 0:HP * S].rearrange("p (q s) -> p q s", s=S)
                dve.tensor_tensor(rdecay[:, hf].rearrange("p (q h) s -> p q h s", h=NH), rps[:, :, None, :].broadcast_to([P, HP, NH, S]),
                                  const("hm4")[:, None, :, None].broadcast_to([P, HP, NH, S]), ALU.mult).then_inc(s["rx_ready"], 1)
            for hf in range(2):
                dve.wait_ge(s["gate_t_done"], hf + 1)
                dve.scalar_tensor_tensor(gate[:, hf, :], gate_t[:, hf, :], 1.0, bank(hf, 0), ALU.add, ALU.mult).then_inc(s["gate_done"], 1)
            dve.wait_ge(ld_wb, 16)
            masks = const("masks").bitcast(U32).rearrange("p (l n) -> p l n", l=7)
            for step in range(7):
                n = LEVELS[max(step - 1, 0)]
                for hf in range(2):
                    dve.wait_ge(s["lvl_mm"], 2 * step + hf + 1)
                    dst = attT[:, hf].rearrange("p g (b two n) -> p g b two n", two=2, n=n)[:, :, :, min(step, 1), :]
                    msk = masks[:, step].rearrange("p (b n) -> p b n", n=n)[:, None].broadcast_to([P, HP * NH, S // (2 * n), n])
                    src = bank(hf, 2 + step % 2).rearrange("p (g b n) -> p g b n", g=HP * NH, n=n)
                    dve.copy_predicated(dst, msk, src).then_inc(s["att_done"], 1)
                    if 1 <= step <= 5:
                        lv = step - 1
                        if lv == 0:
                            dve.wait_ge(s["tot_ready"], hf + 1)
                            dve.wait_ge(s["rx_ready"], hf + 1)
                        else:
                            dve.wait_ge(s["upd_t"], 2 * (lv - 1) + hf + 1)
                            dve.wait_ge(s["upd_r"], 2 * (lv - 1) + hf + 1)
                        rd = rdecay[:, hf].rearrange("p g (b two n) -> p g b two n", two=2, n=n)[:, :, :, 1, :]
                        tt = total[lv][:, hf].rearrange("p g (b two) -> p g b two", two=2)[:, :, :, 0]
                        dve.tensor_tensor(rd, rd, tt[:, :, :, None].broadcast_to([P, HP * NH, S // (2 * n), n]), ALU.mult).then_inc(s["upd_r"], 1)
            dve.wait_ge(ld_wb, 16)
            dve.wait_ge(pool_chain, 3)
            for hf in range(2):
                dve.wait_ge(s["kv_mm"], 2 + hf + 1)
                for hh in range(2):
                    rows = slice(64 * hh, 64 * hh + 64)
                    dst = vhead[rows, HP * hf:HP * hf + HP, :, :, hh, 0:XD].rearrange("p n a c x -> p (n a) c x")
                    mm = dve.tensor_tensor(dst, bank(hf, 0)[rows].rearrange("p (b c x) -> p b c x", c=8, x=XD),
                                           const("b_V")[rows].rearrange("p (c x) -> p c x", c=8)[:, None].broadcast_to([64, 8, 8, XD]), ALU.add)
                mm.then_inc(s["vhead_done"], 1)
            for hf in range(2):
                dve.wait_ge(s["o_mm"], hf + 1)
                o = bank(hf, 0).rearrange("p (g v) -> p g v", v=DV)
                link(dve.reduce_sum(gsum[:, hf], o, AX_X))
                link(dve.tensor_scalar(gsum[:, hf], gsum[:, hf], 1.0 / DV, None, ALU.mult))
                dve.tensor_tensor(gcen[:, hf], o, gsum[:, hf, :, None].broadcast_to([P, HP * NH, DV]), ALU.subtract).then_inc(s["gcen_done"], 1)
            for hf in range(2):
                dve.wait_ge(s["gsq_done"], hf + 1)
                link(dve.reduce_sum(gvar[:, hf], gsq[:, hf], AX_X))
                dve.tensor_scalar(gvar[:, hf], gvar[:, hf], 1.0 / DV, EPS, ALU.mult, ALU.add).then_inc(s["gvar_done"], 1)
            for hf in range(2):
                dve.wait_ge(s["grstd_done"], hf + 1)
                dve.tensor_tensor(gout[:, hf].rearrange("p q (h v) -> p (q h) v", v=DV), gcen[:, hf],
                                  grstd[:, hf, :, None].broadcast_to([P, HP * NH, DV]), ALU.mult).then_inc(s["gn_done"], 1)
            for hf in range(2):
                dve.wait_ge(s["gw_done"], hf + 1)
                g2 = gout[:, hf].rearrange("p q d -> p (q d)")
                dve.scalar_tensor_tensor(g2, g2, 0.5, gate[:, hf, :], ALU.mult, ALU.mult).then_inc(s["gout_done"], 1)

            def layer_norm(k, add_projection, dst, signal):
                for hf in range(2):
                    add_projection(hf)
                    for q in range(HP):
                        mm = dve.bn_stats(stats[:, hf, q, :], res[:, hf, q, :])
                    link(mm)
                    for q in range(HP):
                        mm = dve.bn_aggr(mv[:, hf, q, :], stats[:, hf, q, :])
                    link(mm)
                    dve.tensor_scalar(veps[:, hf], mv[:, hf, :, 1], EPS, None, ALU.add).then_inc(s["veps_done"], 1)
                for hf in range(2):
                    dve.wait_ge(s["rstd_done"], 2 * k + hf + 1)
                    for q in range(HP):
                        mm = dve.tensor_scalar(dst[:, hf, q, :], res[:, hf, q, :], mv[:, hf, q, 0:1], rstd[:, hf, q:q + 1],
                                               ALU.subtract, ALU.mult)
                    mm.then_inc(s[signal], 1)

            def add_x(hf):
                if hf == 0:
                    dve.wait_ge(ld_xtm, 16)
                dve.wait_ge(s["proj_mm"], hf + 1)
                link(dve.tensor_tensor(res[:, hf], bank(hf, 3).rearrange("p (q d) -> p q d", q=HP), x_tm[:, HP * hf:HP * hf + HP, :], ALU.add))

            layer_norm(0, add_x, x1, "x1_done")
            for i in range(2 * NPAIR):
                q = i // 2
                dve.wait_ge(s["s_mm"], i + 1)
                sc = ps[:, i % 2, :].rearrange("p (h s) -> p h s", s=S)
                dve.tensor_reduce(smax[:, i % 2], sc, AX_X, ALU.max).then_inc(s["smax_done"], 1)
                dve.wait_ge(s["smax_done"], i + 1)
                if i >= 2:
                    dve.wait_ge(s["prob_done"], i - 1)
                dve.tensor_tensor(scen[:, i % 2], sc, smax[:, i % 2, :, None].broadcast_to([P, 8, S]), ALU.subtract).then_inc(s["scen_done"], 1)
                norm = [u for u in range(4) if i == min(4 * u + 6, 2 * NPAIR - 1)]
                if i == 2 * NPAIR - 1:
                    norm = [3]
                for u in norm:
                    dve.wait_ge(s["pv_mm"], 4 * u + 4)
                    for par in range(2):
                        rows = slice(64 * par, 64 * par + 64)
                        o = ps[rows, 4 + 2 * (u % 2):6 + 2 * (u % 2), 144 * par:144 * par + 144].rearrange("p n (h x) -> p n h x", x=XD + 1)
                        link(dve.reciprocal(oden[rows, u % 2], o[:, :, :, XD]))
                        mm = dve.tensor_tensor(oatt[rows, 2 * u:2 * u + 2].rearrange("p n h x -> p n h x"), o[:, :, :, 0:XD],
                                               oden[rows, u % 2, :, :, None].broadcast_to([64, 2, XH, XD]), ALU.mult)
                    mm.then_inc(s["oatt_done"], 1)

            def add_x1(hf):
                dve.wait_ge(s["proj_mm"], 2 + hf + 1)
                link(dve.tensor_tensor(res[:, hf], bank(hf, 3).rearrange("p (q d) -> p q d", q=HP), x1[:, hf], ALU.add))
                link(dve.tensor_tensor(res[:, hf], res[:, hf], const("b_O")[:, None, :].broadcast_to([P, HP, D]), ALU.add))

            layer_norm(1, add_x1, x2, "x2_done")
            for hf in range(2):
                dve.wait_ge(s["lg_mm"], hf + 1)
                link(dve.tensor_reduce(lmax[:, hf:hf + 1], bank(hf, 1)[:, 0:S], AX_X, ALU.max))
                dve.tensor_scalar(lmax[:, hf:hf + 1], lmax[:, hf:hf + 1], -1.0, None, ALU.mult).then_inc(s["lmax_done"], 1)
            for hf in range(2):
                dve.wait_ge(s["lexp_done"], hf + 1)
                link(dve.reciprocal(lrec[:, hf:hf + 1], lsum[:, hf:hf + 1]))
                link(dve.tensor_scalar(pr[:, hf, 0], lexp[:, hf, :], lrec[:, hf:hf + 1], None, ALU.mult))
                for k in range(CAP // 8):
                    k8 = slice(8 * k, 8 * k + 8)
                    link(dve.max(topv[:, hf, k8], pr[:, hf, k % 2]))
                    link(dve.max_index(topi[:, hf, k8], topv[:, hf, k8], pr[:, hf, k % 2]))
                    if k < CAP // 8 - 1:
                        link(dve.match_replace(pr[:, hf, (k + 1) % 2], topv[:, hf, k8], pr[:, hf, k % 2], -1.0))
                link(dve.reduce_sum(tsum[:, hf:hf + 1], topv[:, hf], AX_X))
                link(dve.tensor_scalar(tsum[:, hf:hf + 1], tsum[:, hf:hf + 1], 1e-9, None, ALU.add))
                link(dve.reciprocal(tsum[:, hf:hf + 1], tsum[:, hf:hf + 1]))
                link(dve.tensor_scalar(topw[:, hf], topv[:, hf], tsum[:, hf:hf + 1], None, ALU.mult))
                link(dve.tensor_copy(topf[:, hf], topi[:, hf]))
                he = const("hme")[:, :, None].broadcast_to([P, E, CAP])
                dve.tensor_tensor(didx[:, hf], topf[:, hf, None, :].broadcast_to([P, E, CAP]), he, ALU.mult).then_inc(s["didx_done"], 1)
                dve.tensor_tensor(dwgt[:, hf], topw[:, hf, None, :].broadcast_to([P, E, CAP]), he, ALU.mult).then_inc(s["dwgt_done"], 1)
            for hf in range(2):
                dve.wait_ge(s["col_mm"], hf + 1)
                dve.tensor_copy(pcol[:, hf].rearrange("p a g b -> p a (g b)"), bank(hf, 1)[:, 128:256].rearrange("p (a x) -> p a x", a=2)[:, :, 0:32]).then_inc(s["pcol_done"], 1)
            for q in range(NPAIR):
                dve.wait_ge(s["row_mm"], q + 1)
                if q >= 2:
                    dve.wait_ge(s["xg_mm"], 2 * (q - 1))
                dve.tensor_scalar(pick[:, q % 2, :], bank(q % 2, 2), const("tcol"), None, ALU.is_equal).then_inc(s["pick_done"], 1)
            dve.wait_ge(s["pcol_done"], 2)
            for hf in range(2):
                for eg in range(4):
                    mm = dve.tensor_tensor(place[:, eg, 8 * hf:8 * hf + 8, :], const("trow")[:, None, :].broadcast_to([P, 8, S]),
                                           pcol[:, hf, 0, eg, :, None].broadcast_to([P, 8, S]), ALU.is_equal)
                mm.then_inc(s["eq_done"], 1)
            def copy_y(k):
                dve.wait_ge(s["yTT_mm"], k + 1)
                if k >= 2:
                    dve.wait_ge(s["moe_mm"], k - 1)
                dve.tensor_copy(y[:, k % 2].rearrange("p b d -> p (b d)"), ps[:, 5, :]).then_inc(s["y_done"], 1)

            for e in range(E):
                for f in range(2):
                    dve.wait_ge(s["sg_done"], 2 * e + f + 1)
                    if e >= 2:
                        dve.wait_ge(s["y_mm"], e - 1)
                    dve.tensor_tensor(hid[:, e % 2, f, :], sg[:, f, :], ps[:, 2 * f + 1, :], ALU.mult).then_inc(s["hid_done"], 1)
                if e >= 5:
                    copy_y(e - 5)
            for k in range(E - 5, E):
                copy_y(k)

            def add_x2(hf):
                dve.wait_ge(s["fin_mm"], hf + 1)
                link(dve.tensor_tensor(res[:, hf], bank(hf, 0).rearrange("p (q d) -> p q d", q=HP), x2[:, hf], ALU.add))

            layer_norm(2, add_x2, x3, "x3_done")


def kernel(**inputs):
    import numpy as np
    import concourse.bacc as bacc
    from concourse.bass_utils import run_bass_kernel_spmd

    i = {k.removeprefix("L0_"): np.asarray(v) for k, v in inputs.items()}
    packs = {"wa": [], "wb": [], "cb": []}
    cols = {}

    def put(pack, name, a):
        a = np.asarray(a)
        a = a.reshape(a.shape[0], -1)
        full = np.zeros((P, a.shape[1]), a.dtype)
        full[:a.shape[0]] = a
        cols[name] = (pack, a.shape[0], sum(x.shape[1] for x in packs[pack]), a.shape[1])
        packs[pack].append(full)

    f32 = np.float32
    import ml_dtypes
    bf = ml_dtypes.bfloat16
    part = np.arange(P)
    tok = part % S
    put("wa", "mu", i["attn_x_proj_mu"][:, None])
    put("wa", "xl_w1T", i["attn_xl_w1"].T)
    put("wa", "xl_w2T", i["attn_xl_w2"].T)
    put("wa", "xl_b2", i["attn_xl_b2"][:P, None])
    put("wa", "xl_b24", i["attn_xl_b2"][P:, None])
    put("wa", "xout", i["attn_x_out_w"].T[:P])
    put("wa", "xout4", i["attn_x_out_w"].T[P:])
    put("wa", "x_bias", i["attn_x_bias"].T)
    put("wa", "r_wT", i["attn_r_w"].T)
    put("wa", "k_wT", i["attn_k_w"].T)
    put("wa", "w_w1T", i["attn_w_w1"].T)
    put("wa", "w_w2T", i["attn_w_w2"].T)
    put("wa", "v_wT", i["attn_v_w"].T)
    put("wa", "g_wT", i["attn_g_w"].T)
    put("wa", "w_b", np.concatenate([i["attn_w_b"]] * 2)[:, None])
    put("wa", "bonus", np.concatenate([i["attn_bonus"].reshape(-1)] * 2)[:, None])
    put("wa", "hm4", (part[:, None] % 64 // DK == np.arange(NH)).astype(f32))
    put("wa", "ident", np.eye(P, dtype=f32))
    put("wb", "o_wT", i["attn_o_w"].T)
    put("wb", "gnw", np.broadcast_to(i["attn_gn_weight"], (P, D)))
    put("wb", "gnb", np.broadcast_to(i["attn_gn_bias"], (P, D)))
    put("wb", "W_Q", i["xattn_W_Q"])
    put("wb", "W_K", i["xattn_W_K"])
    even_odd = lambda a: a.reshape(-1, XH // 2, 2, XD).transpose(0, 2, 1, 3).reshape(-1, D)
    put("wb", "W_V2", even_odd(i["xattn_W_V"]))
    put("wb", "W_O", i["xattn_W_O"])
    put("wb", "b_Q", np.tile(i["xattn_b_Q"].reshape(2, 64), (1, 2)).T)
    put("wb", "b_K", np.tile(i["xattn_b_K"].reshape(2, 64), (1, 2)).T)
    put("wb", "b_V", np.repeat(even_odd(i["xattn_b_V"]).reshape(2, 64), 64, axis=0))
    put("wb", "b_O", np.broadcast_to(i["xattn_b_O"], (P, D)))
    put("wb", "hm8", (part[:, None] % 64 // XD == np.arange(8)).astype(f32))
    put("wb", "router_w1", i["ffn_router_w1"])
    rw2 = np.zeros((P, 15 * E), f32)
    rw2[:, 7 * E:8 * E] = i["ffn_router_w2"]
    put("wb", "router_w2", rw2)
    put("wb", "hme", (part[:, None] % E == np.arange(E)).astype(f32))
    put("wb", "bsel8", (part[:, None] // E == np.arange(8)).astype(f32))
    put("wb", "tcol", tok[:, None].astype(f32))
    put("wb", "trow", np.broadcast_to(np.arange(S).astype(f32), (P, S)))
    put("cb", "bsel8b", (part[:, None] // E == np.arange(8)).astype(bf))
    put("cb", "bsel", np.stack([part[:, None] // E == 2 * q + part[None, :] // S for q in range(HP)], 1).astype(bf))
    put("cb", "parsel", (np.arange(2)[:, None] == part[None, :] // S).astype(bf))
    masks = []
    t = np.arange(S)
    for step in range(7):
        n = LEVELS[max(step - 1, 0)]
        ts = t.reshape(-1, 2, n)[:, min(step, 1), :].reshape(-1)
        src = tok[:, None]
        if step == 0:
            m = src == ts
        elif step == 1:
            m = (src == ts) | (src == ts - 1)
        else:
            m = src // n == ts // n - 1
        masks.append(m)
    put("wb", "masks", np.concatenate(masks, 1).astype(f32))

    arrays = {k: np.ascontiguousarray(np.concatenate(v, 1)) for k, v in packs.items()}
    arrays["x"] = np.ascontiguousarray(i["x"])
    arrays["xT"] = np.ascontiguousarray(i["x"].reshape(B * S, D).T)
    arrays["ctxT"] = np.ascontiguousarray(i["ctx_1024"].reshape(B * S, D).T)
    arrays["key_mask"] = np.ascontiguousarray(i["mask_BxS2_bk0"].reshape(NPAIR, 2, S).transpose(1, 0, 2))
    arrays["w1"] = np.ascontiguousarray(i["ffn_w1"])
    arrays["w2"] = np.ascontiguousarray(i["ffn_w2"])
    arrays["w3"] = np.ascontiguousarray(i["ffn_w3"])

    nc = bacc.Bacc("TRN2", target_bir_lowering=False, num_devices=1)
    ap = {k: nc.dram_tensor("in_" + k, v.shape, mybir.dt.from_np(v.dtype), kind="ExternalInput").ap() for k, v in arrays.items()}
    out = nc.dram_tensor("out_0", (B, S, D), F32, kind="ExternalOutput").ap()
    decoder_kernel(nc, ap, cols, out)
    r = run_bass_kernel_spmd(nc, [{"in_" + k: v for k, v in arrays.items()}], core_ids=[0])
    return r.results[0]["out_0"]
```

```python
from contextlib import ExitStack

import concourse.bass as bass
from concourse import mybir

F32 = mybir.dt.float32
BF16 = mybir.dt.bfloat16
U8 = mybir.dt.uint8
U32 = mybir.dt.uint32
F32R = mybir.dt.float32r
ALU = mybir.AluOpType
ACT = mybir.ActivationFunctionType
AX_X = mybir.AxisListType.X

P = 128
B, S, D = 16, 64, 128
NPAIR = B // 2
HP = NPAIR // 2
HT = HP * P
NH, DK, DV = 4, 16, 32
XH, XD = 16, 8
R = 32
E, DFF, CAP = 16, 256, 32
EG = 4
EPS = 1e-5
MASKED = -1e30
KRING = 2
WRING = 4
ROWS = [2, 6]
GATHER = [(0, 0), (1, 0), (0, 1), (1, 1)]
GBANK = [3, 7, 0, 4]
TURN = [5] * 13 + [0, 1, 2]
LEVELS = [1, 2, 4, 8, 16, 32]


def decoder_kernel(nc, ap, cols, out):
    with ExitStack() as ctx:
        def sb(name, shape, dt=F32):
            return ctx.enter_context(nc.sbuf_tensor(name, shape, dt))

        def sem(name):
            return ctx.enter_context(nc.semaphore(name))

        def sbuf(stack):
            return lambda name, shape, dt=F32: stack.enter_context(nc.sbuf_tensor(name, shape, dt))

        wb = sb("wb", [P, ap["wb"].shape[1]])
        cb = sb("cb", [P, ap["cb"].shape[1]], BF16)
        minus_half = sb("minus_half", [P, HP * NH])
        res = sb("res", [P, 2, HP, D])
        stats = sb("stats", [P, 2, HP, 6])
        mv = sb("mv", [P, 2, HP, 2])
        veps = sb("veps", [P, 2, HP])
        rstd = sb("rstd", [P, 2, HP])
        x1 = sb("x1", [P, 2, HP, D])
        x2 = sb("x2", [P, 2, HP, D])
        x3 = x1
        ew = sb("ew", [P, WRING, 3, DFF])
        topf = sb("topf", [P, 2, CAP])
        topw = sb("topw", [P, 2, CAP])
        didx = sb("didx", [P, 2, E, CAP], BF16)
        pcol = sb("pcol", [P, 2, 2, 4, 8])

        with ExitStack() as attention:
            sa = sbuf(attention)
            wa = sa("wa", [P, ap["wa"].shape[1]])
            key_mask = sa("key_mask", [2, NPAIR, S], U8)
            mask_row = sa("mask_row", [2, NPAIR, S], BF16)
            bqs = sa("bqs", [P, 2])
            kc = sa("kc", [P, 2, 2, HP, S])
            khead = sa("khead", [P, 2, KRING, XH // 2, S])
            vhead = sa("vhead", [P, NPAIR, 2, XH // 2, 2, XD + 1])
            x_tm = sa("x_tm", [P, NPAIR, D])
            oT = sa("oT", [P, 2, HT])
            xTn = sa("xTn", [P, 2, HT])
            with ExitStack() as recurrent:
                se = sbuf(recurrent)
                shiftd = se("shiftd", [P, 2, 5, HT])
                xT = se("xT", [P, B, S])
                ctxT = se("ctxT", [P, NPAIR, 2, S])
                delta = se("delta", [P, B, S])
                lerp = se("lerp", [P, 2, HT])
                low1 = se("low1", [R, 2, HT])
                mixA = se("mixA", [P, 2, HT])
                mixB = se("mixB", [R, 2, HT])
                wlow = se("wlow", [64, 2, HT])
                expw = se("expw", [P, 2, HP * S])
                v_tm = se("v_tm", [P, 2, HP, D])
                gate_t = se("gate_t", [P, 2, HT])
                gate = se("gate", [P, 2, HT])
                kbonus = se("kbonus", [P, 2, HP, P])
                kdecay = se("kdecay", [P, 2, HP, P])
                rdecay = se("rdecay", [P, 2, HP * NH, S])
                total = [se(f"total{n}", [P, 2, HP * NH, S // n]) for n in LEVELS]
                attT = se("attT", [P, 2, HP * NH, S])
                gsum = se("gsum", [P, 2, HP * NH])
                gvar = se("gvar", [P, 2, HP * NH])
                grstd = se("grstd", [P, 2, HP * NH])
                gcen = se("gcen", [P, 2, HP * NH, DV])
                gsq = se("gsq", [P, 2, HP * NH, DV])
                gout = se("gout", [P, 2, HP, D])
            qdiag = sa("qdiag", [P, 2, NPAIR, P])
            smax = sa("smax", [P, 2, 8])
            scen = sa("scen", [P, 2, 8, S])
            prob = sa("prob", [P, 2, 512])
            probT = sa("probT", [P, 2, 4, P])
            oden = sa("oden", [P, 2, 2, XH])
            oatt = sa("oatt", [P, NPAIR, XH, XD])
            hr = sa("hr", [P, 2, HT])
            lmax = sa("lmax", [P, 2])
            lexp = sa("lexp", [P, 2, S])
            lsum = sa("lsum", [P, 2])
            lrec = sa("lrec", [P, 2])
            pr = sa("pr", [P, 2, 2, S])
            topv = sa("topv", [P, 2, CAP])
            topi = sa("topi", [P, 2, CAP], U32)
            tsum = sa("tsum", [P, 2])
            dwgt = sa("dwgt", [P, 2, E, CAP])

        xh = sb("xh", [P, E, B, CAP], F32R)
        xl = sb("xl", [P, E, B, CAP], F32R)
        wh = sb("wh", [P, 3, 3, DFF], F32R)
        wl = sb("wl", [P, 3, 3, DFF], F32R)
        hid_h = sb("hid_h", [P, 2, 2, 512], F32R)
        hid_l = sb("hid_l", [P, 2, 2, 512], F32R)
        x2h = sb("x2h", [P, 2, HP, D], F32R)
        x2l = sb("x2l", [P, 2, HP, D], F32R)
        pick = sb("pick", [P, 2, E * CAP], F32R)
        place = sb("place", [P, E // EG, B, S])
        sg = sb("sg", [P, 2, 512])
        hid = sb("hid", [P, 2, 512])
        yT = sb("yT", [P, 2, B, EG, CAP])
        y = sb("y", [P, 4, 4, D])
        moeT = sb("moeT", [P, 2, HT])

        def const(name):
            pack, rows, at, n = cols[name]
            return {"wa": wa, "wb": wb, "cb": cb}[pack][0:rows, at:at + n]

        ident = const("ident")

        ps = ctx.enter_context(nc.psum_tensor("ps", [P, 8, 512], F32))

        def bank(hf, i):
            return ps[:, 4 * hf + i, :]

        ld_x, ld_wa, ld_xtm, ld_ctx, ld_wb = sem("ld_x"), sem("ld_wa"), sem("ld_xtm"), sem("ld_ctx"), sem("ld_wb")
        ld_c, ld_e = sem("ld_c"), [sem(f"ld_e{q}") for q in range(2)]
        stored = sem("stored")
        dve_chain, pool_chain, act_chain = sem("dve_chain"), sem("pool_chain"), sem("act_chain")
        names = """zeroed delta_done lerp_done low1_mm low1_done mix_mm mixA_done mixB_done x2_mm muls_done shifted
            r_mm k_mm w1_mm wlow_done w2_mm expw_done tot_ready v_mm g_mm v_done gate_t_done gate_done
            kbonus_done kmix_done kdecay_done rx_ready lvl_mm att_done upd_r upd_k upd_t o_mm gcen_done gsq_done gvar_done
            grstd_done gn_done gw_done gout_done oT_mm oT_done proj_mm veps_done rstd_done x1_done x1T_mm x1T_done
            kv_mm kc_done vhead_done khead_done const_done q_mm qdiag_done s_mm scen_done smax_done prob_done pT_mm
            pT_done pv_mm oatt_done x2_done x2T_mm x2T_done hr_mm hr_done lg_mm lmax_done lexp_done top_done
            didx_done dwgt_done row_mm pick_done xg_mm xg_done col_mm pcol_done eq_done place_done
            gate_mm wh_done wl_done hh_done hl_done x2h_done x2l_done y_act xg_act xg_dve up_mm sg_done hid_done y_mm yT_done yTT_mm y_done moe_mm moeT_done fin_mm x3_done""".split()
        s = {n: sem(n) for n in names}
        block = ctx.enter_context(nc.Block())

        @block.sync
        def _(sp):
            sp.dma_start(xT[:].rearrange("p b s -> p (b s)"), ap["xT"]).then_inc(ld_x, 16)
            sp.dma_start(ctxT[:].rearrange("p a b s -> p (a b s)"), ap["ctxT"]).then_inc(ld_ctx, 16)
            sp.dma_start(wb[:], ap["wb"]).then_inc(ld_wb, 16)
            sp.dma_start(cb[:], ap["cb"]).then_inc(ld_c, 16)
            sp.dma_start(key_mask[:], ap["key_mask"]).then_inc(ld_c, 16)
            sp.dma_start(x_tm[:], ap["x"].rearrange("(n a) s d -> (a s) n d", a=2)).then_inc(ld_xtm, 16)
            for k in range(E // 2):
                if 2 * k >= WRING:
                    sp.wait_ge(s["wl_done"], 2 * k - WRING + 2)
                at = 2 * k % WRING
                sp.dma_start(ew[:, at:at + 2].rearrange("p e w f -> p (e w f)"), ap["ew"][:, 2 * k * 3 * DFF:(2 * k + 2) * 3 * DFF]).then_inc(ld_e[k % 2], 16)
            for hf in range(2):
                sp.wait_ge(s["x3_done"], hf + 1)
                sp.dma_start(out[8 * hf:8 * hf + 8].rearrange("(n a) s d -> (a s) n d", a=2), x3[:, hf]).then_inc(stored, 16)
            sp.wait_ge(stored, 32)

        @block.tensor
        def _(pe):
            pe.wait_ge(ld_wa, 16)
            for hf in range(2):
                pe.wait_ge(s["lerp_done"], hf + 1)
                pe.matmul(bank(hf, 0)[0:R, :], const("xl_w1T"), lerp[:, hf, :], start=True, stop=True).then_inc(s["low1_mm"], 1)
            for hf in range(2):
                pe.wait_ge(s["low1_done"], hf + 1)
                pe.matmul(bank(hf, 1), const("xl_w2T")[:, 0:P], low1[:, hf, :], start=True, stop=True).then_inc(s["mix_mm"], 1)
                pe.matmul(bank(hf, 2)[0:R, :], const("xl_w2T")[:, P:], low1[:, hf, :], start=True, stop=True).then_inc(s["mix_mm"], 1)
            slot = [0, 3, 1, 2, 0]
            for n in range(5):
                for hf in range(2):
                    if n == 0:
                        pe.wait_ge(s["mixA_done"], hf + 1)
                    if n == 3:
                        pe.wait_ge(s["mixB_done"], hf + 1)
                    if n == 4:
                        pe.wait_ge(s["muls_done"], hf + 1)
                    if n < 4:
                        pe.matmul(bank(hf, slot[n]), const("xout")[:, n * D:(n + 1) * D], mixA[:, hf, :],
                                  start=True, stop=True).then_inc(s["x2_mm"], 1)
                    else:
                        pe.matmul(bank(hf, slot[n]), const("xout4"), mixB[:, hf, :], start=True, stop=True).then_inc(s["x2_mm"], 1)

            def split(n, hf, w, b, at):
                src = shiftd[:, hf, n, :].rearrange("p (n a s) -> p a n s", a=2, s=S)
                for par in range(2):
                    mm = pe.matmul(bank(hf, b)[64 * par:64 * par + 64, at:at + HP * S], w, src[:, par],
                                   start=True, stop=True)
                return mm

            for hf in range(2):
                pe.wait_ge(s["shifted"], hf + 1)
                pe.wait_ge(s["muls_done"], 2 + hf + 1)
                split(0, hf, const("r_wT"), 3, 0).then_inc(s["r_mm"], 1)
            for hf in range(2):
                pe.wait_ge(s["shifted"], 2 + hf + 1)
                pe.wait_ge(s["muls_done"], 4 + hf + 1)
                pe.matmul(bank(hf, 1)[0:64, :], const("w_w1T"), shiftd[:, hf, 1, :], start=True, stop=True).then_inc(s["w1_mm"], 1)
            for hf in range(2):
                pe.wait_ge(s["shifted"], 4 + hf + 1)
                pe.wait_ge(s["rx_ready"], hf + 1)
                split(2, hf, const("k_wT"), 3, HP * S).then_inc(s["k_mm"], 1)
            for hf in range(2):
                pe.wait_ge(s["wlow_done"], hf + 1)
                src = wlow[:, hf, :].rearrange("p (n a s) -> p a n s", a=2, s=S)
                for par in range(2):
                    mm = pe.matmul(bank(hf, 1)[64 * par:64 * par + 64, 0:HP * S], const("w_w2T"), src[:, par],
                                   start=True, stop=True)
                mm.then_inc(s["w2_mm"], 1)
            for hf in range(2):
                pe.wait_ge(s["shifted"], 6 + hf + 1)
                pe.wait_ge(s["muls_done"], 6 + hf + 1)
                for n in range(HP):
                    mm = pe.matmul(bank(hf, 2)[:, n * D:(n + 1) * D], shiftd[:, hf, 3, n * P:(n + 1) * P], const("v_wT"),
                                   start=True, stop=True)
                mm.then_inc(s["v_mm"], 1)
            for hf in range(2):
                pe.wait_ge(s["shifted"], 8 + hf + 1)
                for n in range(HP):
                    mm = pe.matmul(bank(hf, 0)[:, n * D:(n + 1) * D], shiftd[:, hf, 4, n * P:(n + 1) * P], const("g_wT"),
                                   start=True, stop=True)
                mm.then_inc(s["g_mm"], 1)
            pe.wait_ge(ld_ctx, 16)
            pe.wait_ge(ld_wb, 16)
            for hf in range(2):
                pe.wait_ge(s["expw_done"], hf + 1)
                for g in range(2):
                    for par in range(2):
                        mm = pe.matmul(bank(hf, 1)[64 * par:64 * par + 64, g * 256:(g + 1) * 256], const("W_K")[:, 64 * g:64 * g + 64],
                                       ctxT[:, HP * hf:HP * hf + HP, par, :], start=True, stop=True)
                mm.then_inc(s["kv_mm"], 1)
            for hf in range(2):
                pe.wait_ge(s["gate_done"], hf + 1)
                for hh in range(2):
                    for b in range(8):
                        mm = pe.matmul(bank(hf, 0)[64 * hh:64 * hh + 64, b * 64:b * 64 + 64], ctxT[:, HP * hf + b // 2, b % 2, :],
                                       const("W_V2")[:, hh * 64:hh * 64 + 64], start=True, stop=True)
                mm.then_inc(s["kv_mm"], 1)
            for step in range(7):
                n = LEVELS[max(step - 1, 0)]
                for hf in range(2):
                    if step == 0:
                        pe.wait_ge(s["kbonus_done"], hf + 1)
                        pe.wait_ge(s["rx_ready"], hf + 1)
                        pe.wait_ge(s["v_done"], hf + 1)
                    elif step == 1:
                        pe.wait_ge(s["kmix_done"], hf + 1)
                        pe.wait_ge(s["kdecay_done"], hf + 1)
                    else:
                        pe.wait_ge(s["upd_r"], 2 * (step - 2) + hf + 1)
                        pe.wait_ge(s["upd_k"], 2 * (step - 2) + hf + 1)
                        pe.wait_ge(s["att_done"], 2 * (step - 2) + hf + 1)
                    stat = kbonus if step < 2 else kdecay
                    for q in range(HP):
                        rd = rdecay[:, hf, q * NH:(q + 1) * NH, :].rearrange("p h (b two n) -> p h b two n", two=2, n=n)[:, :, :, min(step, 1), :]
                        mm = pe.matmul(bank(hf, 2 + step % 2)[:, q * P:(q + 1) * P], stat[:, hf, q, :], rd, start=True, stop=True)
                    mm.then_inc(s["lvl_mm"], 1)
            for hf in range(2):
                pe.wait_ge(s["att_done"], 12 + hf + 1)
                pe.wait_ge(s["vhead_done"], hf + 1)
                for q in range(HP):
                    for par in range(2):
                        rows = slice(64 * par, 64 * par + 64)
                        for h in range(NH):
                            mm = pe.matmul(bank(hf, 0)[rows, q * D + h * DV:q * D + (h + 1) * DV], attT[rows, hf, q * NH + h, :],
                                           v_tm[rows, hf, q, h * DV:(h + 1) * DV], start=True, stop=True)
                mm.then_inc(s["o_mm"], 1)

            def transposes(hf, b, src, signal):
                for q in range(HP):
                    mm = pe.transpose(bank(hf, b)[:, q * P:(q + 1) * P], src[:, q, :], ident)
                mm.then_inc(s[signal], 1)

            for hf in range(2):
                pe.wait_ge(s["gout_done"], hf + 1)
                transposes(hf, 2, gout[:, hf], "oT_mm")
            for hf in range(2):
                pe.wait_ge(s["oT_done"], hf + 1)
                for q in range(HP):
                    mm = pe.matmul(bank(hf, 3)[:, q * P:(q + 1) * P], oT[:, hf, q * P:(q + 1) * P], const("o_wT"), start=True, stop=True)
                mm.then_inc(s["proj_mm"], 1)
            for hf in range(2):
                pe.wait_ge(s["x1_done"], hf + 1)
                transposes(hf, 2, x1[:, hf], "x1T_mm")
            for hf in range(2):
                pe.wait_ge(s["x1T_done"], hf + 1)
                src = xTn[:, hf, :].rearrange("p (n a s) -> p a n s", a=2, s=S)
                for g in range(2):
                    for par in range(2):
                        mm = pe.matmul(bank(hf, 0)[64 * par:64 * par + 64, g * 256:(g + 1) * 256], const("W_Q")[:, 64 * g:64 * g + 64],
                                       src[:, par], start=True, stop=True)
                mm.then_inc(s["q_mm"], 1)
            pe.wait_ge(s["qdiag_done"], 2)
            pe.wait_ge(s["vhead_done"], 2)
            pe.wait_ge(s["kc_done"], 2)
            N2 = 2 * NPAIR

            def scores(i):
                q, g = i // 2, i % 2
                if g == 0:
                    pe.wait_ge(s["khead_done"], q + 1)
                if i >= 2:
                    pe.wait_ge(s["scen_done"], i - 1)
                pe.matmul(ps[:, i % 2, :], qdiag[:, g, q, :], khead[:, g, q % KRING], start=True, stop=False)
                pe.matmul(ps[:, i % 2, :], const("parsel"), mask_row[:, q, None, :].broadcast_to([2, 8, S]),
                          start=False, stop=True).then_inc(s["s_mm"], 1)

            def weigh(i):
                q, g = i // 2, i % 2
                if i >= 2:
                    pe.wait_ge(s["pT_done"], i - 1)
                pe.wait_ge(s["prob_done"], i + 1)
                for c in range(4):
                    mm = pe.transpose(ps[:, 2 + i % 2, c * P:(c + 1) * P], prob[:, i % 2, c * P:(c + 1) * P], ident)
                mm.then_inc(s["pT_mm"], 1)

            def values(i):
                q, g = i // 2, i % 2
                pe.wait_ge(s["pT_done"], i + 1)
                if q >= 4 and g == 0:
                    pe.wait_ge(s["oatt_done"], q // 2 - 1)
                o = ps[:, 4 + q % 4, 0:288].rearrange("p (a c x) -> p a c x", a=2, c=8)
                for c in range(4):
                    mm = pe.matmul(o[:, :, 4 * g + c, :], probT[:, i % 2, c, :],
                                   vhead[:, q, :, 4 * g + c].rearrange("p a h x -> p a (h x)"), start=True, stop=True)
                mm.then_inc(s["pv_mm"], 1)

            for i in range(N2 + 2):
                if i < N2:
                    scores(i)
                if 1 <= i < N2 + 1:
                    weigh(i - 1)
                if i >= 2:
                    values(i - 2)
            for hf in range(2):
                if hf == 0:
                    pe.wait_ge(s["oatt_done"], 2)
                    pe.wait_ge(s["pT_done"], 2 * NPAIR)
                else:
                    pe.wait_ge(s["oatt_done"], 4)
                transposes(hf, 2, oatt[:, HP * hf:HP * hf + HP].rearrange("p n h d -> p n (h d)"), "oT_mm")
            for hf in range(2):
                pe.wait_ge(s["oT_done"], 2 + hf + 1)
                for q in range(HP):
                    mm = pe.matmul(bank(hf, 3)[:, q * P:(q + 1) * P], oT[:, hf, q * P:(q + 1) * P], const("W_O"), start=True, stop=True)
                mm.then_inc(s["proj_mm"], 1)
            for hf in range(2):
                pe.wait_ge(s["x2_done"], hf + 1)
                transposes(hf, 2, x2[:, hf], "x2T_mm")
            for hf in range(2):
                pe.wait_ge(s["x2T_done"], hf + 1)
                pe.matmul(bank(hf, 0), const("router_w1"), xTn[:, hf, :], start=True, stop=True).then_inc(s["hr_mm"], 1)
            for hf in range(2):
                pe.wait_ge(s["hr_done"], hf + 1)
                for b in range(8):
                    mm = pe.matmul(bank(hf, 1)[:, 0:S], const("router_w2")[:, (7 - b) * E:(7 - b) * E + P], hr[:, hf, b * S:(b + 1) * S],
                                   start=(b == 0), stop=(b == 7))
                mm.then_inc(s["lg_mm"], 1)
            for hf in range(2):
                pe.wait_ge(s["didx_done"], hf + 1)
                pe.wait_ge(s["dwgt_done"], hf + 1)
                for eg in range(4):
                    pe.matmul(bank(hf, 1)[:, 128 + eg * 8:136 + eg * 8], didx[:, hf, EG * eg:EG * eg + EG, :].rearrange("p e j -> p (e j)"),
                              const("bsel8b"), start=True, stop=True)
                    mm = pe.matmul(bank(hf, 1)[:, 192 + eg * 8:200 + eg * 8], dwgt[:, hf, EG * eg:EG * eg + EG, :].rearrange("p e j -> p (e j)"),
                                   const("bsel8"), start=True, stop=True)
                mm.then_inc(s["col_mm"], 1)

            def row(q):
                if q >= 2:
                    pe.wait_ge(s["pick_done"], q - 1)
                pe.matmul(ps[:, ROWS[q % 2], :], const("bsel")[:, (q % HP) * P:(q % HP + 1) * P],
                          didx[:, q // HP].rearrange("p e j -> p (e j)"), start=True, stop=True).then_inc(s["row_mm"], 1)

            def gather(q):
                hf = q // HP
                if q % HP == 0:
                    pe.wait_ge(s["x2l_done"], hf + 1)
                pe.wait_ge(s["pick_done"], q + 1)
                for k, (par, part) in enumerate(GATHER):
                    rows = slice(64 * par, 64 * par + 64)
                    if q >= 1:
                        if k < 3:
                            pe.wait_ge(s["xg_act"], 3 * (q - 1) + k + 1)
                        else:
                            pe.wait_ge(s["xg_dve"], q)
                    pe.matmul(ps[:, GBANK[k], :], (x2h, x2l)[part][rows, hf, q % HP, :], pick[rows, q % 2, :],
                              start=True, stop=True).then_inc(s["xg_mm"], 1)

            row(0)
            for q in range(NPAIR):
                if q + 1 < NPAIR:
                    row(q + 1)
                gather(q)
            pe.wait_ge(s["pcol_done"], 2)
            pe.wait_ge(s["xg_act"], 3 * NPAIR)
            pe.wait_ge(s["xg_dve"], NPAIR)

            def three(out_ps, w_at, rhs_h, rhs_l, first, last):
                w_h, w_l = wh[:, w_at[0], w_at[1], w_at[2]], wl[:, w_at[0], w_at[1], w_at[2]]
                pe.matmul(out_ps, w_h, rhs_h, start=first, stop=False)
                pe.matmul(out_ps, w_h, rhs_l, start=False, stop=False)
                return pe.matmul(out_ps, w_l, rhs_h, start=False, stop=last)

            def up(e):
                pe.wait_ge(s["wl_done"], e + 1)
                for f in range(2):
                    fs = slice(f * P, (f + 1) * P)
                    r_h, r_l = (x[:, e].rearrange("p b j -> p (b j)") for x in (xh, xl))
                    if e >= 1:
                        pe.wait_ge(s["sg_done"], 2 * (e - 1) + f + 1)
                    three(ps[:, 2 * f, :], (e % 3, 0, fs), r_h, r_l, True, True).then_inc(s["gate_mm"], 1)
                    if e >= 1:
                        pe.wait_ge(s["hid_done"], 2 * (e - 1) + f + 1)
                    three(ps[:, 2 * f + 1, :], (e % 3, 1, fs), r_h, r_l, True, True).then_inc(s["up_mm"], 1)

            def down(e):
                if e >= 1:
                    pe.wait_ge(s["yT_done"], e)
                for f in range(2):
                    pe.wait_ge(s["hl_done"], 2 * e + f + 1)
                    mm = three(ps[:, 4, :], (e % 3, 2, slice(f * P, (f + 1) * P)), hid_h[:, e % 2, f, :], hid_l[:, e % 2, f, :], f == 0, f == 1)
                mm.then_inc(s["y_mm"], 1)

            def turn(k):
                eg, t = k // 4, k % 4
                pe.wait_ge(s["yT_done"], EG * eg + EG)
                if 1 <= k <= 12:
                    pe.wait_ge(s["y_done"], k)
                for b in range(4):
                    mm = pe.transpose(ps[:, TURN[k], b * P:(b + 1) * P],
                                      yT[:, eg % 2, 4 * t + b].rearrange("p e j -> p (e j)"), ident)
                mm.then_inc(s["yTT_mm"], 1)

            def put(k):
                eg, t = k // 4, k % 4
                if k < 12:
                    pe.wait_ge(s["y_done"], k + 1)
                elif k % 2 == 0:
                    pe.wait_ge(s["y_done"], 13 + (k - 12) // 2)
                else:
                    pe.wait_ge(s["y_act"], 1 + (k - 12) // 2)
                if k % 2 == 0:
                    pe.wait_ge(s["place_done"], k // 2 + 1)
                for b in range(4):
                    bb = 4 * t + b
                    mm = pe.matmul(ps[:, 6 + bb // 8, (bb % 8) * S:(bb % 8 + 1) * S], y[:, k % 4, b, :], place[:, eg, bb, :],
                                   start=(eg == 0 and bb % 8 == 0), stop=(eg == 3), skip_group_check=True)
                mm.then_inc(s["moe_mm"], 1)

            for e in range(E + 1):
                if e < E:
                    up(e)
                if e >= 6:
                    put(e - 6)
                if e >= 5:
                    turn(e - 5)
                if e >= 1:
                    down(e - 1)
            for k in range(12, 16):
                turn(k)
            for k in range(11, 16):
                put(k)
            for hf in range(2):
                pe.wait_ge(s["moeT_done"], hf + 1)
                transposes(hf, 0, moeT[:, hf, :].rearrange("p (q t) -> p q t", q=HP), "fin_mm")

        @block.gpsimd
        def _(pool):
            done = [0]

            def link(ins):
                done[0] += 1
                ins.then_inc(pool_chain, 1)
                pool.wait_ge(pool_chain, done[0])

            pool.wait_ge(ld_x, 16)
            link(pool.tensor_tensor(delta[:, :, 1:S], xT[:, :, 0:S - 1], xT[:, :, 1:S], ALU.subtract))
            pool.tensor_scalar(delta[:, :, 0:1], xT[:, :, 0:1], -1.0, None, ALU.mult).then_inc(s["delta_done"], 1)
            for t in (kbonus, kdecay):
                pool.memset(t[:], 0.0).then_inc(s["zeroed"], 1)
            pool.memset(minus_half[:], -0.5).then_inc(s["const_done"], 1)
            xh = xT[:].rearrange("p (f b) s -> p f (b s)", f=2)
            for n in range(5):
                for hf in range(2):
                    pool.wait_ge(s["muls_done"], 2 * n + hf + 1)
                    pool.tensor_tensor(shiftd[:, hf, n, :], shiftd[:, hf, n, :], xh[:, hf, :], ALU.add).then_inc(s["shifted"], 1)
            pool.memset(vhead[:], 0.0).then_inc(s["zeroed"], 1)
            pool.wait_ge(s["zeroed"], 3)
            for hh in range(2):
                link(pool.memset(vhead[64 * hh:64 * hh + 64, :, :, :, hh, XD:XD + 1].rearrange("p n a c x -> p (n a c) x"), 1.0))
            pool.wait_ge(s["g_mm"], 2)
            pool.memset(qdiag[:], 0.0).then_inc(s["zeroed"], 1)
            pool.wait_ge(s["kdecay_done"], 2)
            for lv in range(5):
                n = LEVELS[lv]
                for hf in range(2):
                    if lv == 0:
                        pool.wait_ge(s["tot_ready"], hf + 1)
                    if lv >= 1:
                        pool.wait_ge(s["upd_t"], 2 * (lv - 1) + hf + 1)
                        pool.wait_ge(s["lvl_mm"], 2 * (lv + 1) + hf + 1)
                        pool.wait_ge(s["upd_k"], 2 * (lv - 1) + hf + 1)
                    if 2 * lv + hf >= 1:
                        pool.wait_ge(s["upd_k"], 2 * lv + hf)
                    tot = total[lv][:, hf].rearrange("p g (b two) -> p g b two", two=2)
                    pool.tensor_tensor(total[lv + 1][:, hf], tot[:, :, :, 0], tot[:, :, :, 1], ALU.mult).then_inc(s["upd_t"], 1)
                    pool.wait_ge(s["upd_t"], 2 * lv + hf + 1)
                    for par in range(2):
                        rows = slice(64 * par, 64 * par + 64)
                        kd = kdecay[rows, hf, :, 64 * par:64 * par + 64].rearrange("p q (b two n) -> p q b two n", two=2, n=n)[:, :, :, 0, :]
                        tk = tot[rows].rearrange("p (q h) b two -> p q h b two", h=NH)[:, :, 0, :, 1]
                        mm = pool.tensor_tensor(kd, kd, tk[:, :, :, None].broadcast_to([64, HP, S // (2 * n), n]), ALU.mult)
                        if par == 0:
                            link(mm)
                    mm.then_inc(s["upd_k"], 1)
            pool.wait_ge(s["upd_k"], 10)
            for hf in range(2):
                if hf == 0:
                    pool.wait_ge(s["const_done"], 1)
                pool.wait_ge(s["gvar_done"], hf + 1)
                pool.tensor_tensor(grstd[:, hf], gvar[:, hf], minus_half[:], ALU.pow).then_inc(s["grstd_done"], 1)
            for hf in range(2):
                pool.wait_ge(s["gn_done"], hf + 1)
                g3 = gout[:, hf]
                link(pool.tensor_tensor(g3, g3, const("gnw")[:, None, :].broadcast_to([P, HP, D]), ALU.mult))
                pool.tensor_tensor(g3, g3, const("gnb")[:, None, :].broadcast_to([P, HP, D]), ALU.add).then_inc(s["gw_done"], 1)

            def inverse_deviation(k):
                for hf in range(2):
                    pool.wait_ge(s["veps_done"], 2 * k + hf + 1)
                    pool.tensor_tensor(rstd[:, hf], veps[:, hf], minus_half[:, 0:HP], ALU.pow).then_inc(s["rstd_done"], 1)

            for hf in range(2):
                pool.wait_ge(s["kc_done"], hf + 1)
                for q in range(HP):
                    if hf == 0 and q == KRING:
                        inverse_deviation(0)
                    if HP * hf + q >= KRING:
                        pool.wait_ge(s["s_mm"], 2 * (HP * hf + q - KRING) + 2)
                    for g in range(2):
                        kq = kc[:, hf, g, q, None, :].broadcast_to([P, 8, S])
                        mm = pool.tensor_tensor(khead[:, g, q % KRING], kq, const("hm8")[:, :, None].broadcast_to([P, 8, S]), ALU.mult)
                    mm.then_inc(s["khead_done"], 1)
            inverse_deviation(1)
            for hf in range(2):
                pool.wait_ge(s["x2h_done"], hf + 1)
                pool.tensor_tensor(x2l[:, hf], x2[:, hf], x2h[:, hf].bitcast(F32), ALU.subtract).then_inc(s["x2l_done"], 1)

            def rest_of_weights(e):
                pool.wait_ge(s["wh_done"], e + 1)
                pool.tensor_tensor(wl[:, e % 3], ew[:, e % WRING], wh[:, e % 3].bitcast(F32), ALU.subtract).then_inc(s["wl_done"], 1)

            for e in range(E):
                rest_of_weights(e)
                if 2 <= e < 10:
                    eg, hf = (e - 2) // 2, e % 2
                    pool.wait_ge(s["eq_done"], e - 1)
                    pl = place[:, eg, 8 * hf:8 * hf + 8, :]
                    pool.tensor_tensor(pl, pl, pcol[:, hf, 1, eg, :, None].broadcast_to([P, 8, S]), ALU.mult).then_inc(s["place_done"], 1)
            inverse_deviation(2)

        @block.scalar
        def _(act):
            done = [0]

            def link(ins):
                done[0] += 1
                ins.then_inc(act_chain, 1)
                act.wait_ge(act_chain, done[0])

            act.dma_start(wa[:], ap["wa"]).then_inc(ld_wa, 16)
            act.wait_ge(ld_wa, 16)
            for hf in range(2):
                act.wait_ge(s["low1_mm"], hf + 1)
                act.activation(low1[:, hf, :], bank(hf, 0)[0:R, :], ACT.Tanh).then_inc(s["low1_done"], 1)
            for hf in range(2):
                act.wait_ge(s["mix_mm"], 2 * hf + 1)
                act.activation(mixA[:, hf, :], bank(hf, 1), ACT.Tanh, bias=const("xl_b2")).then_inc(s["mixA_done"], 1)
                act.wait_ge(s["mix_mm"], 2 * hf + 2)
                act.activation(mixB[:, hf, :], bank(hf, 2)[0:R, :], ACT.Tanh, bias=const("xl_b24")).then_inc(s["mixB_done"], 1)
            for hf in range(2):
                act.wait_ge(s["w1_mm"], hf + 1)
                act.activation(wlow[:, hf, :], bank(hf, 1)[0:64, :], ACT.Tanh).then_inc(s["wlow_done"], 1)
            for hf in range(2):
                act.wait_ge(s["k_mm"], hf + 1)
                if hf == 0:
                    act.wait_ge(s["zeroed"], 2)
                kps = bank(hf, 3)[:, HP * S:].rearrange("p (q s) -> p q s", s=S)
                for par in range(2):
                    rows = slice(64 * par, 64 * par + 64)
                    kb = kbonus[rows, hf, :, 64 * par:64 * par + 64]
                    mm = act.activation(kb, kps[rows], ACT.Copy, scale=const("bonus")[rows])
                mm.then_inc(s["kbonus_done"], 1)
                for par in range(2):
                    rows = slice(64 * par, 64 * par + 64)
                    mm = act.activation(kdecay[rows, hf, :, 64 * par:64 * par + 64], kps[rows], ACT.Copy)
                mm.then_inc(s["kdecay_done"], 1)
            for hf in range(2):
                act.wait_ge(s["w2_mm"], hf + 1)
                act.activation(expw[:, hf, :], bank(hf, 1)[:, 0:HP * S], ACT.Exp, bias=const("w_b")).then_inc(s["expw_done"], 1)
                act.wait_ge(s["expw_done"], hf + 1)
                for h in range(NH):
                    tt = total[0][:, hf].rearrange("p (q h) s -> p q h s", h=NH)[:, :, h, :]
                    mm = act.activation(tt, expw[:, hf, :].rearrange("p (q s) -> p q s", s=S), ACT.Exp, scale=-1.0)
                mm.then_inc(s["tot_ready"], 1)
            for hf in range(2):
                act.wait_ge(s["v_mm"], hf + 1)
                act.activation(v_tm[:, hf].rearrange("p q d -> p (q d)"), bank(hf, 2), ACT.Copy).then_inc(s["v_done"], 1)
            for hf in range(2):
                act.wait_ge(s["g_mm"], hf + 1)
                act.activation(gate_t[:, hf, :], bank(hf, 0), ACT.Tanh, scale=0.5).then_inc(s["gate_t_done"], 1)
            for hf in range(2):
                act.wait_ge(s["lvl_mm"], hf + 1)
                kps = bank(hf, 3)[:, HP * S:].rearrange("p (q s two) -> p q s two", two=2, q=HP)
                for par in range(2):
                    rows = slice(64 * par, 64 * par + 64)
                    ke = kbonus[rows, hf, :, 64 * par:64 * par + 64].rearrange("p q (s two) -> p q s two", two=2)
                    mm = act.activation(ke[:, :, :, 0], kps[rows][:, :, :, 0], ACT.Copy)
                mm.then_inc(s["kmix_done"], 1)
            act.wait_ge(ld_wb, 16)
            for hf in range(2):
                act.wait_ge(s["kv_mm"], hf + 1)
                for g in range(2):
                    mm = act.activation(kc[:, hf, g].rearrange("p q s -> p (q s)"), bank(hf, 1)[:, 256 * g:256 * g + 256], ACT.Identity,
                                        bias=const("b_K")[:, g:g + 1])
                mm.then_inc(s["kc_done"], 1)
            for g in range(2):
                mm = act.activation(bqs[:, g:g + 1], const("b_Q")[:, g:g + 1], ACT.Copy, scale=XD ** -0.5)
            mm.then_inc(s["const_done"], 1)
            for hf in range(2):
                act.wait_ge(s["gcen_done"], hf + 1)
                act.activation(gsq[:, hf], gcen[:, hf], ACT.Square).then_inc(s["gsq_done"], 1)

            def copy_T(dst, b, mm_sem, k, done_sem):
                for hf in range(2):
                    act.wait_ge(s[mm_sem], k + hf + 1)
                    act.activation(dst[:, hf, :], bank(hf, b), ACT.Copy).then_inc(s[done_sem], 1)

            copy_T(oT, 2, "oT_mm", 0, "oT_done")
            copy_T(xTn, 2, "x1T_mm", 0, "x1T_done")
            act.wait_ge(s["const_done"], 2)
            act.wait_ge(s["zeroed"], 4)
            for hf in range(2):
                act.wait_ge(s["q_mm"], hf + 1)
                for g in range(2):
                    for par in range(2):
                        rows = slice(64 * par, 64 * par + 64)
                        mm = act.activation(qdiag[rows, g, HP * hf:HP * hf + HP, 64 * par:64 * par + 64],
                                            bank(hf, 0)[rows, 256 * g:256 * g + 256].rearrange("p (q s) -> p q s", s=S),
                                            ACT.Identity, bias=bqs[rows, g:g + 1], scale=XD ** -0.5)
                mm.then_inc(s["qdiag_done"], 1)
            N2 = 2 * NPAIR
            for i in range(N2 + 1):
                if i < N2:
                    act.wait_ge(s["scen_done"], i + 1)
                    if i >= 2:
                        act.wait_ge(s["pT_mm"], i - 1)
                    act.activation(prob[:, i % 2, :], scen[:, i % 2].rearrange("p h s -> p (h s)"), ACT.Exp).then_inc(s["prob_done"], 1)
                if i >= 1:
                    act.wait_ge(s["pT_mm"], i)
                    if i >= 3:
                        act.wait_ge(s["pv_mm"], i - 2)
                    act.activation(probT[:, (i - 1) % 2].rearrange("p c q -> p (c q)"), ps[:, 2 + (i - 1) % 2, :], ACT.Copy).then_inc(s["pT_done"], 1)
            copy_T(oT, 2, "oT_mm", 2, "oT_done")
            copy_T(xTn, 2, "x2T_mm", 0, "x2T_done")
            for hf in range(2):
                act.wait_ge(s["hr_mm"], hf + 1)
                act.activation(hr[:, hf, :], bank(hf, 0), ACT.Silu).then_inc(s["hr_done"], 1)
            for hf in range(2):
                act.wait_ge(s["lmax_done"], hf + 1)
                act.activation(lexp[:, hf, :], bank(hf, 1)[:, 0:S], ACT.Exp, bias=lmax[:, hf:hf + 1], accum_out=lsum[:, hf:hf + 1]).then_inc(s["lexp_done"], 1)
            for hf in range(2):
                act.wait_ge(s["x2_done"], hf + 1)
                act.activation(x2h[:, hf], x2[:, hf], ACT.Copy).then_inc(s["x2h_done"], 1)

            def round_weights(e):
                act.wait_ge(ld_e[e // 2 % 2], 16 * (e // 4 + 1))
                if e >= 3:
                    act.wait_ge(s["y_mm"], e - 2)
                act.activation(wh[:, e % 3], ew[:, e % WRING], ACT.Copy).then_inc(s["wh_done"], 1)

            for q in range(NPAIR):
                for k in range(3):
                    par, part = GATHER[k]
                    act.wait_ge(s["xg_mm"], 4 * q + k + 1)
                    act.activation((xh, xl)[part][:, :, 2 * q + par, :], ps[:, GBANK[k], :].rearrange("p (e j) -> p e j", e=E),
                                   ACT.Copy).then_inc(s["xg_act"], 1)
                if q < 2:
                    round_weights(q)
            for e in range(E + 1):
                if e < E:
                    for f in range(2):
                        k = 2 * e + f
                        act.wait_ge(s["gate_mm"], k + 1)
                        if k >= 2:
                            act.wait_ge(s["hid_done"], k - 1)
                        act.activation(sg[:, f, :], ps[:, 2 * f, :], ACT.Silu).then_inc(s["sg_done"], 1)
                    for f in range(2):
                        act.wait_ge(s["hid_done"], 2 * e + f + 1)
                        if e >= 2:
                            act.wait_ge(s["y_mm"], e - 1)
                        act.activation(hid_h[:, e % 2, f, :], hid[:, f, :], ACT.Copy).then_inc(s["hh_done"], 1)
                if e >= 1:
                    d = e - 1
                    act.wait_ge(s["y_mm"], d + 1)
                    if d >= 8 and d % 4 == 0:
                        act.wait_ge(s["yTT_mm"], 4 * (d // 4 - 1))
                    act.activation(yT[:, (d // 4) % 2, :, d % 4, :], ps[:, 4, :].rearrange("p (b j) -> p b j", b=B), ACT.Copy).then_inc(s["yT_done"], 1)
                if e + 2 < E:
                    round_weights(e + 2)
            act.wait_ge(s["yTT_mm"], 14)
            act.wait_ge(s["moe_mm"], 10)
            act.activation(y[:, 1].rearrange("p b d -> p (b d)"), ps[:, TURN[13], :], ACT.Copy).then_inc(s["y_act"], 1)
            act.wait_ge(s["yTT_mm"], 16)
            act.wait_ge(s["moe_mm"], 12)
            act.activation(y[:, 3].rearrange("p b d -> p (b d)"), ps[:, TURN[15], :], ACT.Copy).then_inc(s["y_act"], 1)
            for hf in range(2):
                act.wait_ge(s["moe_mm"], 4 * 3 + 2 * hf + 2)
                act.activation(moeT[:, hf, :], ps[:, 6 + hf, :], ACT.Copy).then_inc(s["moeT_done"], 1)

        @block.vector
        def _(dve):
            done = [0]

            def link(ins):
                done[0] += 1
                ins.then_inc(dve_chain, 1)
                dve.wait_ge(dve_chain, done[0])

            dve.wait_ge(ld_wa, 16)
            dve.wait_ge(s["delta_done"], 1)
            dve.wait_ge(pool_chain, 1)
            xh = xT[:].rearrange("p (f b) s -> p f (b s)", f=2)
            dh = delta[:].rearrange("p (f b) s -> p f (b s)", f=2)
            for hf in range(2):
                dve.scalar_tensor_tensor(lerp[:, hf, :], dh[:, hf], const("mu"), xh[:, hf], ALU.mult, ALU.add).then_inc(s["lerp_done"], 1)
            link(dve.memset(attT[:], 0.0))
            dve.wait_ge(ld_c, 32)
            link(dve.tensor_scalar(mask_row[:], key_mask[:], MASKED, None, ALU.mult))
            slot = [0, 3, 1, 2, 0]
            for n in range(5):
                for hf in range(2):
                    dve.wait_ge(s["x2_mm"], 2 * n + hf + 1)
                    dve.scalar_tensor_tensor(shiftd[:, hf, n, :], bank(hf, slot[n]), const("x_bias")[:, n:n + 1], dh[:, hf],
                                             ALU.add, ALU.mult).then_inc(s["muls_done"], 1)
            for hf in range(2):
                dve.wait_ge(s["r_mm"], hf + 1)
                rps = bank(hf, 3)[:, 0:HP * S].rearrange("p (q s) -> p q s", s=S)
                dve.tensor_tensor(rdecay[:, hf].rearrange("p (q h) s -> p q h s", h=NH), rps[:, :, None, :].broadcast_to([P, HP, NH, S]),
                                  const("hm4")[:, None, :, None].broadcast_to([P, HP, NH, S]), ALU.mult).then_inc(s["rx_ready"], 1)
            for hf in range(2):
                dve.wait_ge(s["gate_t_done"], hf + 1)
                dve.scalar_tensor_tensor(gate[:, hf, :], gate_t[:, hf, :], 1.0, bank(hf, 0), ALU.add, ALU.mult).then_inc(s["gate_done"], 1)
            dve.wait_ge(ld_wb, 16)
            masks = const("masks").bitcast(U32).rearrange("p (l n) -> p l n", l=7)
            for step in range(7):
                n = LEVELS[max(step - 1, 0)]
                for hf in range(2):
                    dve.wait_ge(s["lvl_mm"], 2 * step + hf + 1)
                    dst = attT[:, hf].rearrange("p g (b two n) -> p g b two n", two=2, n=n)[:, :, :, min(step, 1), :]
                    msk = masks[:, step].rearrange("p (b n) -> p b n", n=n)[:, None].broadcast_to([P, HP * NH, S // (2 * n), n])
                    src = bank(hf, 2 + step % 2).rearrange("p (g b n) -> p g b n", g=HP * NH, n=n)
                    dve.copy_predicated(dst, msk, src).then_inc(s["att_done"], 1)
                    if 1 <= step <= 5:
                        lv = step - 1
                        if lv == 0:
                            dve.wait_ge(s["tot_ready"], hf + 1)
                            dve.wait_ge(s["rx_ready"], hf + 1)
                        else:
                            dve.wait_ge(s["upd_t"], 2 * (lv - 1) + hf + 1)
                            dve.wait_ge(s["upd_r"], 2 * (lv - 1) + hf + 1)
                        rd = rdecay[:, hf].rearrange("p g (b two n) -> p g b two n", two=2, n=n)[:, :, :, 1, :]
                        tt = total[lv][:, hf].rearrange("p g (b two) -> p g b two", two=2)[:, :, :, 0]
                        dve.tensor_tensor(rd, rd, tt[:, :, :, None].broadcast_to([P, HP * NH, S // (2 * n), n]), ALU.mult).then_inc(s["upd_r"], 1)
            dve.wait_ge(ld_wb, 16)
            dve.wait_ge(pool_chain, 3)
            for hf in range(2):
                dve.wait_ge(s["kv_mm"], 2 + hf + 1)
                for hh in range(2):
                    rows = slice(64 * hh, 64 * hh + 64)
                    dst = vhead[rows, HP * hf:HP * hf + HP, :, :, hh, 0:XD].rearrange("p n a c x -> p (n a) c x")
                    mm = dve.tensor_tensor(dst, bank(hf, 0)[rows].rearrange("p (b c x) -> p b c x", c=8, x=XD),
                                           const("b_V")[rows].rearrange("p (c x) -> p c x", c=8)[:, None].broadcast_to([64, 8, 8, XD]), ALU.add)
                mm.then_inc(s["vhead_done"], 1)
            for hf in range(2):
                dve.wait_ge(s["o_mm"], hf + 1)
                o = bank(hf, 0).rearrange("p (g v) -> p g v", v=DV)
                link(dve.reduce_sum(gsum[:, hf], o, AX_X))
                link(dve.tensor_scalar(gsum[:, hf], gsum[:, hf], 1.0 / DV, None, ALU.mult))
                dve.tensor_tensor(gcen[:, hf], o, gsum[:, hf, :, None].broadcast_to([P, HP * NH, DV]), ALU.subtract).then_inc(s["gcen_done"], 1)
            for hf in range(2):
                dve.wait_ge(s["gsq_done"], hf + 1)
                link(dve.reduce_sum(gvar[:, hf], gsq[:, hf], AX_X))
                dve.tensor_scalar(gvar[:, hf], gvar[:, hf], 1.0 / DV, EPS, ALU.mult, ALU.add).then_inc(s["gvar_done"], 1)
            for hf in range(2):
                dve.wait_ge(s["grstd_done"], hf + 1)
                dve.tensor_tensor(gout[:, hf].rearrange("p q (h v) -> p (q h) v", v=DV), gcen[:, hf],
                                  grstd[:, hf, :, None].broadcast_to([P, HP * NH, DV]), ALU.mult).then_inc(s["gn_done"], 1)
            for hf in range(2):
                dve.wait_ge(s["gw_done"], hf + 1)
                g2 = gout[:, hf].rearrange("p q d -> p (q d)")
                dve.scalar_tensor_tensor(g2, g2, 0.5, gate[:, hf, :], ALU.mult, ALU.mult).then_inc(s["gout_done"], 1)

            def layer_norm(k, add_projection, dst, signal):
                for hf in range(2):
                    add_projection(hf)
                    for q in range(HP):
                        mm = dve.bn_stats(stats[:, hf, q, :], res[:, hf, q, :])
                    link(mm)
                    for q in range(HP):
                        mm = dve.bn_aggr(mv[:, hf, q, :], stats[:, hf, q, :])
                    link(mm)
                    dve.tensor_scalar(veps[:, hf], mv[:, hf, :, 1], EPS, None, ALU.add).then_inc(s["veps_done"], 1)
                for hf in range(2):
                    dve.wait_ge(s["rstd_done"], 2 * k + hf + 1)
                    for q in range(HP):
                        mm = dve.tensor_scalar(dst[:, hf, q, :], res[:, hf, q, :], mv[:, hf, q, 0:1], rstd[:, hf, q:q + 1],
                                               ALU.subtract, ALU.mult)
                    mm.then_inc(s[signal], 1)

            def add_x(hf):
                if hf == 0:
                    dve.wait_ge(ld_xtm, 16)
                dve.wait_ge(s["proj_mm"], hf + 1)
                link(dve.tensor_tensor(res[:, hf], bank(hf, 3).rearrange("p (q d) -> p q d", q=HP), x_tm[:, HP * hf:HP * hf + HP, :], ALU.add))

            layer_norm(0, add_x, x1, "x1_done")
            for i in range(2 * NPAIR):
                q = i // 2
                dve.wait_ge(s["s_mm"], i + 1)
                sc = ps[:, i % 2, :].rearrange("p (h s) -> p h s", s=S)
                dve.tensor_reduce(smax[:, i % 2], sc, AX_X, ALU.max).then_inc(s["smax_done"], 1)
                dve.wait_ge(s["smax_done"], i + 1)
                if i >= 2:
                    dve.wait_ge(s["prob_done"], i - 1)
                dve.tensor_tensor(scen[:, i % 2], sc, smax[:, i % 2, :, None].broadcast_to([P, 8, S]), ALU.subtract).then_inc(s["scen_done"], 1)
                norm = [u for u in range(4) if i == min(4 * u + 6, 2 * NPAIR - 1)]
                if i == 2 * NPAIR - 1:
                    norm = [3]
                for u in norm:
                    dve.wait_ge(s["pv_mm"], 4 * u + 4)
                    for par in range(2):
                        rows = slice(64 * par, 64 * par + 64)
                        o = ps[rows, 4 + 2 * (u % 2):6 + 2 * (u % 2), 144 * par:144 * par + 144].rearrange("p n (h x) -> p n h x", x=XD + 1)
                        link(dve.reciprocal(oden[rows, u % 2], o[:, :, :, XD]))
                        mm = dve.tensor_tensor(oatt[rows, 2 * u:2 * u + 2].rearrange("p n h x -> p n h x"), o[:, :, :, 0:XD],
                                               oden[rows, u % 2, :, :, None].broadcast_to([64, 2, XH, XD]), ALU.mult)
                    mm.then_inc(s["oatt_done"], 1)

            def add_x1(hf):
                dve.wait_ge(s["proj_mm"], 2 + hf + 1)
                link(dve.tensor_tensor(res[:, hf], bank(hf, 3).rearrange("p (q d) -> p q d", q=HP), x1[:, hf], ALU.add))
                link(dve.tensor_tensor(res[:, hf], res[:, hf], const("b_O")[:, None, :].broadcast_to([P, HP, D]), ALU.add))

            layer_norm(1, add_x1, x2, "x2_done")
            for hf in range(2):
                dve.wait_ge(s["lg_mm"], hf + 1)
                link(dve.tensor_reduce(lmax[:, hf:hf + 1], bank(hf, 1)[:, 0:S], AX_X, ALU.max))
                dve.tensor_scalar(lmax[:, hf:hf + 1], lmax[:, hf:hf + 1], -1.0, None, ALU.mult).then_inc(s["lmax_done"], 1)
            for hf in range(2):
                dve.wait_ge(s["lexp_done"], hf + 1)
                link(dve.reciprocal(lrec[:, hf:hf + 1], lsum[:, hf:hf + 1]))
                link(dve.tensor_scalar(pr[:, hf, 0], lexp[:, hf, :], lrec[:, hf:hf + 1], None, ALU.mult))
                for k in range(CAP // 8):
                    k8 = slice(8 * k, 8 * k + 8)
                    link(dve.max(topv[:, hf, k8], pr[:, hf, k % 2]))
                    link(dve.max_index(topi[:, hf, k8], topv[:, hf, k8], pr[:, hf, k % 2]))
                    if k < CAP // 8 - 1:
                        link(dve.match_replace(pr[:, hf, (k + 1) % 2], topv[:, hf, k8], pr[:, hf, k % 2], -1.0))
                link(dve.reduce_sum(tsum[:, hf:hf + 1], topv[:, hf], AX_X))
                link(dve.tensor_scalar(tsum[:, hf:hf + 1], tsum[:, hf:hf + 1], 1e-9, None, ALU.add))
                link(dve.reciprocal(tsum[:, hf:hf + 1], tsum[:, hf:hf + 1]))
                link(dve.tensor_scalar(topw[:, hf], topv[:, hf], tsum[:, hf:hf + 1], None, ALU.mult))
                link(dve.tensor_copy(topf[:, hf], topi[:, hf]))
                he = const("hme")[:, :, None].broadcast_to([P, E, CAP])
                dve.tensor_tensor(didx[:, hf], topf[:, hf, None, :].broadcast_to([P, E, CAP]), he, ALU.mult).then_inc(s["didx_done"], 1)
                dve.tensor_tensor(dwgt[:, hf], topw[:, hf, None, :].broadcast_to([P, E, CAP]), he, ALU.mult).then_inc(s["dwgt_done"], 1)
            for hf in range(2):
                dve.wait_ge(s["col_mm"], hf + 1)
                dve.tensor_copy(pcol[:, hf].rearrange("p a g b -> p a (g b)"), bank(hf, 1)[:, 128:256].rearrange("p (a x) -> p a x", a=2)[:, :, 0:32]).then_inc(s["pcol_done"], 1)

            def gathered(q):
                par, part = GATHER[3]
                dve.wait_ge(s["xg_mm"], 4 * q + 4)
                dve.tensor_copy((xh, xl)[part][:, :, 2 * q + par, :], ps[:, GBANK[3], :].rearrange("p (e j) -> p e j", e=E)).then_inc(s["xg_dve"], 1)

            def make_pick(q):
                dve.wait_ge(s["row_mm"], q + 1)
                if q >= 2:
                    dve.wait_ge(s["xg_mm"], 4 * (q - 1))
                dve.tensor_scalar(pick[:, q % 2, :], ps[:, ROWS[q % 2], :], const("tcol"), None, ALU.is_equal).then_inc(s["pick_done"], 1)

            make_pick(0)
            for q in range(NPAIR):
                if q + 1 < NPAIR:
                    make_pick(q + 1)
                gathered(q)
            dve.wait_ge(s["pcol_done"], 2)
            def copy_y(k):
                dve.wait_ge(s["yTT_mm"], k + 1)
                if k >= 4:
                    dve.wait_ge(s["moe_mm"], k - 3)
                dve.tensor_copy(y[:, k % 4].rearrange("p b d -> p (b d)"), ps[:, TURN[k], :]).then_inc(s["y_done"], 1)

            for e in range(E):
                for f in range(2):
                    dve.wait_ge(s["sg_done"], 2 * e + f + 1)
                    dve.wait_ge(s["up_mm"], 2 * e + f + 1)
                    if e >= 1:
                        dve.wait_ge(s["hl_done"], 2 * (e - 1) + f + 1)
                    dve.tensor_tensor(hid[:, f, :], sg[:, f, :], ps[:, 2 * f + 1, :], ALU.mult).then_inc(s["hid_done"], 1)
                for f in range(2):
                    dve.wait_ge(s["hh_done"], 2 * e + f + 1)
                    dve.tensor_tensor(hid_l[:, e % 2, f, :], hid[:, f, :], hid_h[:, e % 2, f, :].bitcast(F32), ALU.subtract).then_inc(s["hl_done"], 1)
                if e < 8:
                    eg, hf = e // 2, e % 2
                    dve.tensor_tensor(place[:, eg, 8 * hf:8 * hf + 8, :], const("trow")[:, None, :].broadcast_to([P, 8, S]),
                                      pcol[:, hf, 0, eg, :, None].broadcast_to([P, 8, S]), ALU.is_equal).then_inc(s["eq_done"], 1)
                if e >= 5:
                    copy_y(e - 5)
            copy_y(11)
            copy_y(12)
            copy_y(14)

            def add_x2(hf):
                dve.wait_ge(s["fin_mm"], hf + 1)
                link(dve.tensor_tensor(res[:, hf], bank(hf, 0).rearrange("p (q d) -> p q d", q=HP), x2[:, hf], ALU.add))

            layer_norm(2, add_x2, x3, "x3_done")


def kernel(**inputs):
    import numpy as np
    import concourse.bacc as bacc
    from concourse.bass_utils import run_bass_kernel_spmd

    i = {k.removeprefix("L0_"): np.asarray(v) for k, v in inputs.items()}
    packs = {"wa": [], "wb": [], "cb": []}
    cols = {}

    def put(pack, name, a):
        a = np.asarray(a)
        a = a.reshape(a.shape[0], -1)
        full = np.zeros((P, a.shape[1]), a.dtype)
        full[:a.shape[0]] = a
        cols[name] = (pack, a.shape[0], sum(x.shape[1] for x in packs[pack]), a.shape[1])
        packs[pack].append(full)

    f32 = np.float32
    import ml_dtypes
    bf = ml_dtypes.bfloat16
    part = np.arange(P)
    tok = part % S
    put("wa", "mu", i["attn_x_proj_mu"][:, None])
    put("wa", "xl_w1T", i["attn_xl_w1"].T)
    put("wa", "xl_w2T", i["attn_xl_w2"].T)
    put("wa", "xl_b2", i["attn_xl_b2"][:P, None])
    put("wa", "xl_b24", i["attn_xl_b2"][P:, None])
    mixers = np.zeros((P, 4, D), f32)
    for n in range(4):
        mixers[n * R:(n + 1) * R, n] = i["attn_x_out_w"].T[n * R:(n + 1) * R]
    put("wa", "xout", mixers)
    put("wa", "xout4", i["attn_x_out_w"].T[P:])
    put("wa", "x_bias", i["attn_x_bias"].T)
    put("wa", "r_wT", i["attn_r_w"].T)
    put("wa", "k_wT", i["attn_k_w"].T)
    put("wa", "w_w1T", i["attn_w_w1"].T)
    put("wa", "w_w2T", i["attn_w_w2"].T)
    put("wa", "v_wT", i["attn_v_w"].T)
    put("wa", "g_wT", i["attn_g_w"].T)
    put("wa", "w_b", np.concatenate([i["attn_w_b"]] * 2)[:, None])
    put("wa", "bonus", np.concatenate([i["attn_bonus"].reshape(-1)] * 2)[:, None])
    put("wa", "hm4", (part[:, None] % 64 // DK == np.arange(NH)).astype(f32))
    put("wb", "ident", np.eye(P, dtype=f32))
    put("wb", "o_wT", i["attn_o_w"].T)
    put("wb", "gnw", np.broadcast_to(i["attn_gn_weight"], (P, D)))
    put("wb", "gnb", np.broadcast_to(i["attn_gn_bias"], (P, D)))
    put("wb", "W_Q", i["xattn_W_Q"])
    put("wb", "W_K", i["xattn_W_K"])
    even_odd = lambda a: a.reshape(-1, XH // 2, 2, XD).transpose(0, 2, 1, 3).reshape(-1, D)
    put("wb", "W_V2", even_odd(i["xattn_W_V"]))
    put("wb", "W_O", i["xattn_W_O"])
    put("wb", "b_Q", np.tile(i["xattn_b_Q"].reshape(2, 64), (1, 2)).T)
    put("wb", "b_K", np.tile(i["xattn_b_K"].reshape(2, 64), (1, 2)).T)
    put("wb", "b_V", np.repeat(even_odd(i["xattn_b_V"]).reshape(2, 64), 64, axis=0))
    put("wb", "b_O", np.broadcast_to(i["xattn_b_O"], (P, D)))
    put("wb", "hm8", (part[:, None] % 64 // XD == np.arange(8)).astype(f32))
    put("wb", "router_w1", i["ffn_router_w1"])
    rw2 = np.zeros((P, 15 * E), f32)
    rw2[:, 7 * E:8 * E] = i["ffn_router_w2"]
    put("wb", "router_w2", rw2)
    put("wb", "hme", (part[:, None] % E == np.arange(E)).astype(f32))
    put("wb", "bsel8", (part[:, None] // E == np.arange(8)).astype(f32))
    put("wb", "tcol", tok[:, None].astype(f32))
    put("wb", "trow", np.broadcast_to(np.arange(S).astype(f32), (P, S)))
    put("cb", "bsel8b", (part[:, None] // E == np.arange(8)).astype(bf))
    put("cb", "bsel", np.stack([part[:, None] // E == 2 * q + part[None, :] // S for q in range(HP)], 1).astype(bf))
    put("cb", "parsel", (np.arange(2)[:, None] == part[None, :] // S).astype(bf))
    masks = []
    t = np.arange(S)
    for step in range(7):
        n = LEVELS[max(step - 1, 0)]
        ts = t.reshape(-1, 2, n)[:, min(step, 1), :].reshape(-1)
        src = tok[:, None]
        if step == 0:
            m = src == ts
        elif step == 1:
            m = (src == ts) | (src == ts - 1)
        else:
            m = src // n == ts // n - 1
        masks.append(m)
    put("wb", "masks", np.concatenate(masks, 1).astype(f32))

    arrays = {k: np.ascontiguousarray(np.concatenate(v, 1)) for k, v in packs.items()}
    arrays["x"] = np.ascontiguousarray(i["x"])
    arrays["xT"] = np.ascontiguousarray(i["x"].reshape(B * S, D).T)
    arrays["ctxT"] = np.ascontiguousarray(i["ctx_1024"].reshape(B * S, D).T)
    arrays["key_mask"] = np.ascontiguousarray(i["mask_BxS2_bk0"].reshape(NPAIR, 2, S).transpose(1, 0, 2))
    w3 = i["ffn_w3"].reshape(E, 2, P, D).transpose(2, 0, 1, 3).reshape(P, E, DFF)
    ew = np.stack([i["ffn_w1"].transpose(1, 0, 2), i["ffn_w2"].transpose(1, 0, 2), w3], 2)
    arrays["ew"] = np.ascontiguousarray(ew.reshape(P, E * 3 * DFF))

    nc = bacc.Bacc("TRN2", target_bir_lowering=False, num_devices=1)
    ap = {k: nc.dram_tensor("in_" + k, v.shape, mybir.dt.from_np(v.dtype), kind="ExternalInput").ap() for k, v in arrays.items()}
    out = nc.dram_tensor("out_0", (B, S, D), F32, kind="ExternalOutput").ap()
    decoder_kernel(nc, ap, cols, out)
    r = run_bass_kernel_spmd(nc, [{"in_" + k: v for k, v in arrays.items()}], core_ids=[0])
    return r.results[0]["out_0"]
```

```python
from contextlib import ExitStack

import concourse.bass as bass
from concourse import mybir

F32 = mybir.dt.float32
BF16 = mybir.dt.bfloat16
U8 = mybir.dt.uint8
U32 = mybir.dt.uint32
F32R = mybir.dt.float32r
ALU = mybir.AluOpType
ACT = mybir.ActivationFunctionType
AX_X = mybir.AxisListType.X

P = 128
B, S, D = 16, 64, 128
NPAIR = B // 2
HP = NPAIR // 2
HT = HP * P
NH, DK, DV = 4, 16, 32
XH, XD = 16, 8
R = 32
E, DFF, CAP = 16, 256, 32
EG = 4
EPS = 1e-5
MASKED = -1e30
KRING = 2
WRING = 4
ROWS = [0, 1]
GATHER = [(0, 0), (1, 0), (0, 1), (1, 1)]
GBANK = [2, 3, 4, 5]
GACT = [4] * 3 + [3] * 5
AFTER = [dict(oT=6, proj=7, x2T=6, hr=7, lg=6), dict(oT=4, proj=5, x2T=4, hr=5, lg=7)]
TAIL = [dict(o=3, oT=2, proj=3, x1T=2, q=3), dict(o=7, oT=6, proj=7, x1T=6, q=7)]
TURN = [5] * 12 + [0, 1, 2, 3]
LEVELS = [1, 2, 4, 8, 16, 32]


def decoder_kernel(nc, ap, cols, out):
    with ExitStack() as ctx:
        def sb(name, shape, dt=F32):
            return ctx.enter_context(nc.sbuf_tensor(name, shape, dt))

        def sem(name):
            return ctx.enter_context(nc.semaphore(name))

        def sbuf(stack):
            return lambda name, shape, dt=F32: stack.enter_context(nc.sbuf_tensor(name, shape, dt))

        wb = sb("wb", [P, ap["wb"].shape[1]])
        cb = sb("cb", [P, ap["cb"].shape[1]], BF16)
        zeros = sb("zeros", [P, 512], BF16)
        minus_half = sb("minus_half", [P, HP])
        eps = sb("eps", [P, 1])
        table_call = sb("table_call", [P, 1])
        res = sb("res", [P, 2, HP, D])
        stats = sb("stats", [P, 2, HP, 6])
        mv = sb("mv", [P, 2, HP, 2])
        veps = sb("veps", [P, 2, HP])
        std = sb("std", [P, 2, HP])
        rstd = sb("rstd", [P, 2, HP])
        shift = sb("shift", [P, HP])
        x1 = sb("x1", [P, 2, HP, D])
        x2 = sb("x2", [P, 2, HP, D])
        x3 = x1
        ew = sb("ew", [P, WRING, 3, DFF])
        topf = sb("topf", [P, 2, CAP])
        topw = sb("topw", [P, 2, CAP])
        didx = sb("didx", [P, 2, E, CAP], BF16)
        pcol = sb("pcol", [P, 2, 2, 4, 8])

        with ExitStack() as attention:
            sa = sbuf(attention)
            oatt = sa("oatt", [P, NPAIR, XH, XD])
            oT = sa("oT", [P, 2, HT])
            xTn = sa("xTn", [P, 2, HT])
            hr = sa("hr", [P, 2, HT])
            lmax = sa("lmax", [P, 2])
            lexp = sa("lexp", [P, 2, S])
            lsum = sa("lsum", [P, 2])
            lrec = sa("lrec", [P, 2])
            pr = sa("pr", [P, 2, 2, S])
            topv = sa("topv", [P, 2, CAP])
            topi = sa("topi", [P, 2, CAP], U32)
            tsum = sa("tsum", [P, 2])
            dwgt = sa("dwgt", [P, 2, E, CAP])
            w0 = sa("w0", [P, ap["w0"].shape[1]])
            wa = sa("wa", [P, ap["wa"].shape[1]])
            key_mask = sa("key_mask", [2, NPAIR, S], U8)
            mask_row = sa("mask_row", [2, NPAIR, S], BF16)
            bqs = sa("bqs", [P, 2])
            khead_h = sa("khead_h", [P, 2, KRING, XH // 2, S], F32R)
            khead_l = sa("khead_l", [P, 2, KRING, XH // 2, S], F32R)
            vhead = sa("vhead", [P, NPAIR, 2, XH // 2, 2, XD + 1])
            x_tm = sa("x_tm", [P, NPAIR, D])
            with ExitStack() as recurrent:
                se = sbuf(recurrent)
                shiftd = se("shiftd", [P, 2, 5, HT])
                xT = se("xT", [P, B, S])
                ctxT = se("ctxT", [P, NPAIR, 2, S])
                delta = se("delta", [P, B, S])
                lerp = se("lerp", [P, 2, HT])
                low1 = se("low1", [P, 2, HT])
                mixA = se("mixA", [P, 2, HT])
                mixB = se("mixB", [P, 2, HT])
                wlow = se("wlow", [64, 2, HT])
                expw = se("expw", [P, 2, HP * S])
                v_tm = se("v_tm", [P, 2, HP, D])
                gate_t = se("gate_t", [P, 2, HT])
                gate = se("gate", [P, 2, HT])
                kbonus = se("kbonus", [P, 2, HP, P])
                kdecay = se("kdecay", [P, 2, HP, P])
                rdecay = se("rdecay", [P, 2, HP * NH, S])
                total = [se(f"total{n}", [P, 2, HP * NH, S // n]) for n in LEVELS[:5]]
                attT = se("attT", [P, 2, HP * NH, S])
                gsum = se("gsum", [P, 2, HP * NH])
                gvar = se("gvar", [P, 2, HP * NH])
                gstd = se("gstd", [P, 2, HP * NH])
                grstd = se("grstd", [P, 2, HP * NH])
                gcen = se("gcen", [P, 2, HP * NH, DV])
                gsq = mixA[:].rearrange("p f (g v) -> p f g v", v=DV)
                gout = lerp[:].rearrange("p f (q d) -> p f q d", d=D)
                kc = mixB[:].rearrange("p f (g q s) -> p f g q s", g=2, q=HP)
                kc_h = kbonus[:].rearrange("p f q t -> p f (q t)").rearrange("p f (g q s) -> p f g q s", g=2, q=HP)
                kc_l = low1[:].rearrange("p f (g q s) -> p f g q s", g=2, q=HP)
            qdiag_h = sa("qdiag_h", [P, 2, NPAIR, P], F32R)
            qdiag_l = sa("qdiag_l", [P, 2, NPAIR, P], F32R)
            smax = sa("smax", [P, 2, 8])
            scen = sa("scen", [P, 2, 8, S])
            prob = sa("prob", [P, 2, 512])
            probT = sa("probT", [P, 2, 4, P])
            oden = sa("oden", [P, 2, XH])
            query = sa("query", [P, 2, 2, HP * S])

        place = sb("place", [P, E // EG, B, S])
        y = sb("y", [P, 4, 4, D])
        yT = sb("yT", [P, 2, B, EG, CAP])
        sg = sb("sg", [P, 2, 512])
        hid = sb("hid", [P, 2, 512])
        hid_h = sb("hid_h", [P, 2, 2, 512], F32R)
        hid_l = sb("hid_l", [P, 2, 2, 512], F32R)
        ident_r = sb("ident_r", [P, P], F32R)
        x2h = sb("x2h", [P, 2, HP, D], F32R)
        x2l = sb("x2l", [P, 2, HP, D], F32R)
        pick = sb("pick", [P, 2, E * CAP], F32R)
        xh = sb("xh", [P, E, B, CAP], F32R)
        xl = sb("xl", [P, E, B, CAP], F32R)
        wh = sb("wh", [P, 3, 3, DFF], F32R)
        wl = sb("wl", [P, 3, 3, DFF], F32R)

        def const(name):
            pack, rows, at, n = cols[name]
            return {"w0": w0, "wa": wa, "wb": wb, "cb": cb}[pack][0:rows, at:at + n]

        ident = const("ident")

        ps = ctx.enter_context(nc.psum_tensor("ps", [P, 8, 512], F32))

        def bank(hf, i):
            return ps[:, 4 * hf + i, :]

        ld_x, ld_w0, ld_wa, ld_xtm, ld_ctx, ld_wb = [sem(f"ld_x{hf}") for hf in range(2)], sem("ld_w0"), sem("ld_wa"), sem("ld_xtm"), sem("ld_ctx"), sem("ld_wb")
        ld_c, ld_e = sem("ld_c"), [sem(f"ld_e{q}") for q in range(2)]
        stored = sem("stored")
        dve_chain, pool_chain, act_chain = sem("dve_chain"), sem("pool_chain"), sem("act_chain")
        names = """zeros_done zeroed lerp_done low1_mm low1_done mix_mm mixA_done mixB_done x2_mm muls_done
            r_mm k_mm w1_mm wlow_done w2_mm expw_done tot_ready v_mm g_mm v_done gate_t_done gate_done
            kbonus_done kmix_done kdecay_done rx_ready lvl_mm eps_done ident_done att_done upd_r upd_k upd_t o_mm gcen_done gsq_done gvar_done
            gstd_done ghalf_done gw_done gb_done gcw_done gout_done oT_mm oT_done proj_mm var_done std_done veps_done rstd_done x1_done x1b_done x1T_mm x1T_done
            kv_mm kc_done vhead_done khead_done const_done q_mm qdiag_done query_done qrest_done kch_done s_mm scen_done smax_done prob_done pT_mm
            pT_done pv_mm oatt_done x2_done x2T_mm x2T_done hr_mm th_done hr_done lg_mm lmax_done lexp_done
            didx_done topw_done dwgt_done row_mm pick_done xg_mm col_mm pcol_done eq_done place_done
            gate_mm wh_done wl_done hh_done hl_done x2h_done x2l_done y_act xg_act xg_dve up_mm sg_done hid_done y_mm yT_done yTT_mm y_done moe_mm shift_done x3_done x3_act""".split()
        s = {n: sem(n) for n in names}
        delta_done = [sem(f"delta_done{hf}") for hf in range(2)]
        shifted = [sem(f"shifted{hf}") for hf in range(2)]
        block = ctx.enter_context(nc.Block())

        @block.sync
        def _(sp):
            for hf in range(2):
                sp.dma_start(xT[:, 8 * hf:8 * hf + 8].rearrange("p b s -> p (b s)"), ap["xT"][:, HT * hf:HT * hf + HT]).then_inc(ld_x[hf], 16)
            sp.dma_start(ctxT[:].rearrange("p a b s -> p (a b s)"), ap["ctxT"]).then_inc(ld_ctx, 16)
            sp.dma_start(wb[:], ap["wb"]).then_inc(ld_wb, 16)
            sp.dma_start(cb[:], ap["cb"]).then_inc(ld_c, 16)
            sp.dma_start(key_mask[:], ap["key_mask"]).then_inc(ld_c, 16)
            sp.dma_start(x_tm[:], ap["x"].rearrange("(n a) s d -> (a s) n d", a=2)).then_inc(ld_xtm, 16)
            for k in range(E // 2):
                if 2 * k >= WRING:
                    sp.wait_ge(s["wl_done"], 2 * k - WRING + 2)
                at = 2 * k % WRING
                sp.dma_start(ew[:, at:at + 2].rearrange("p e w f -> p (e w f)"), ap["ew"][:, 2 * k * 3 * DFF:(2 * k + 2) * 3 * DFF]).then_inc(ld_e[k % 2], 16)
            for u in range(4):
                if u < 2:
                    sp.wait_ge(s["x3_act"], 2 * u + 2)
                else:
                    sp.wait_ge(s["x3_done"], 2 * (u - 2) + 2)
                sp.dma_start(out[4 * u:4 * u + 4].rearrange("(n a) s d -> (a s) n d", a=2),
                             x3[:, u // 2, 2 * (u % 2):2 * (u % 2) + 2]).then_inc(stored, 16)
            sp.wait_ge(stored, 64)

        def token_delta(engine, hf):
            engine.wait_ge(ld_x[hf], 16)
            bs = slice(8 * hf, 8 * hf + 8)
            engine.tensor_tensor(delta[:, bs, 1:S], xT[:, bs, 0:S - 1], xT[:, bs, 1:S], ALU.subtract).then_inc(delta_done[hf], 1)
            engine.tensor_scalar(delta[:, bs, 0:1], xT[:, bs, 0:1], -1.0, None, ALU.mult).then_inc(delta_done[hf], 1)

        @block.tensor
        def _(pe):
            def stay_warm(n, b):
                for _ in range(n):
                    pe.matmul(ps[:, b, :], zeros[:, 0:P], zeros[:], start=True, stop=True)

            pe.wait_ge(s["zeros_done"], 1)
            stay_warm(9, 7)
            pe.wait_ge(ld_w0, 16)
            for hf in range(2):
                pe.wait_ge(s["lerp_done"], hf + 1)
                pe.matmul(bank(hf, 0), const("xl_w1T"), lerp[:, hf, :], start=True, stop=True).then_inc(s["low1_mm"], 1)
            for hf in range(2):
                pe.wait_ge(s["low1_done"], hf + 1)
                pe.matmul(bank(hf, 1), const("xl_w2T")[:, 0:P], low1[:, hf, :], start=True, stop=True).then_inc(s["mix_mm"], 1)
                pe.matmul(bank(hf, 2), const("xl_w2T")[:, P:], low1[:, hf, :], start=True, stop=True).then_inc(s["mix_mm"], 1)
            slot = [0, 3, 1, 2, 0]
            pe.wait_ge(ld_wa, 16)
            for n in range(5):
                for hf in range(2):
                    if n == 0:
                        pe.wait_ge(s["mixA_done"], hf + 1)
                    if n == 3:
                        pe.wait_ge(s["mixB_done"], hf + 1)
                    if n == 4:
                        pe.wait_ge(s["muls_done"], hf + 1)
                    pe.matmul(bank(hf, slot[n]), const("xout")[:, n * D:(n + 1) * D], (mixA if n < 4 else mixB)[:, hf, :],
                              start=True, stop=True).then_inc(s["x2_mm"], 1)

            def split(n, hf, w, b, at):
                src = shiftd[:, hf, n, :].rearrange("p (n a s) -> p a n s", a=2, s=S)
                for par in range(2):
                    mm = pe.matmul(bank(hf, b)[64 * par:64 * par + 64, at:at + HP * S], w, src[:, par],
                                   start=True, stop=True)
                return mm

            for hf in range(2):
                pe.wait_ge(shifted[hf], 1)
                pe.wait_ge(s["muls_done"], 2 + hf + 1)
                split(0, hf, const("r_wT"), 3, 0).then_inc(s["r_mm"], 1)
            for hf in range(2):
                pe.wait_ge(shifted[hf], 2)
                pe.wait_ge(s["muls_done"], 4 + hf + 1)
                pe.matmul(bank(hf, 1)[0:64, :], const("w_w1T"), shiftd[:, hf, 1, :], start=True, stop=True).then_inc(s["w1_mm"], 1)
            for hf in range(2):
                pe.wait_ge(shifted[hf], 4)
                pe.wait_ge(s["muls_done"], 6 + hf + 1)
                for n in range(HP):
                    mm = pe.matmul(bank(hf, 2)[:, n * D:(n + 1) * D], shiftd[:, hf, 3, n * P:(n + 1) * P], const("v_wT"),
                                   start=True, stop=True)
                mm.then_inc(s["v_mm"], 1)
                pe.wait_ge(shifted[hf], 3)
                pe.wait_ge(s["rx_ready"], hf + 1)
                split(2, hf, const("k_wT"), 3, HP * S).then_inc(s["k_mm"], 1)
            for hf in range(2):
                pe.wait_ge(s["wlow_done"], hf + 1)
                src = wlow[:, hf, :].rearrange("p (n a s) -> p a n s", a=2, s=S)
                for par in range(2):
                    mm = pe.matmul(bank(hf, 1)[64 * par:64 * par + 64, 0:HP * S], const("w_w2T"), src[:, par],
                                   start=True, stop=True)
                mm.then_inc(s["w2_mm"], 1)

            def gates(hf):
                pe.wait_ge(shifted[hf], 5)
                for n in range(HP):
                    mm = pe.matmul(bank(hf, 0)[:, n * D:(n + 1) * D], shiftd[:, hf, 4, n * P:(n + 1) * P], const("g_wT"),
                                   start=True, stop=True)
                mm.then_inc(s["g_mm"], 1)

            def context_keys(hf):
                if hf == 0:
                    pe.wait_ge(ld_ctx, 16)
                    pe.wait_ge(ld_wb, 16)
                pe.wait_ge(s["expw_done"], hf + 1)
                for g in range(2):
                    for par in range(2):
                        mm = pe.matmul(bank(hf, 1)[64 * par:64 * par + 64, g * 256:(g + 1) * 256], const("W_K")[:, 64 * g:64 * g + 64],
                                       ctxT[:, HP * hf:HP * hf + HP, par, :], start=True, stop=True)
                mm.then_inc(s["kv_mm"], 1)

            def context_values(hf):
                pe.wait_ge(s["gate_done"], hf + 1)
                for b in range(8):
                    for hh in range(2):
                        mm = pe.matmul(bank(hf, 0)[64 * hh:64 * hh + 64, b * 64:b * 64 + 64], ctxT[:, HP * hf + b // 2, b % 2, :],
                                       const("W_V2")[:, hh * 64:hh * 64 + 64], start=True, stop=True)
                mm.then_inc(s["kv_mm"], 1)

            def level(step, hf):
                n = LEVELS[max(step - 1, 0)]
                if step == 0:
                    pe.wait_ge(s["kbonus_done"], hf + 1)
                    pe.wait_ge(s["rx_ready"], hf + 1)
                    pe.wait_ge(s["v_done"], hf + 1)
                elif step == 1:
                    pe.wait_ge(s["kmix_done"], hf + 1)
                    pe.wait_ge(s["kdecay_done"], hf + 1)
                else:
                    pe.wait_ge(s["upd_r"], 2 * (step - 2) + hf + 1)
                    pe.wait_ge(s["upd_k"], 2 * (step - 2) + hf + 1)
                    pe.wait_ge(s["att_done"], 2 * (step - 2) + hf + 1)
                stat = kbonus if step < 2 else kdecay
                for q in range(HP):
                    rd = rdecay[:, hf, q * NH:(q + 1) * NH, :].rearrange("p h (b two n) -> p h b two n", two=2, n=n)[:, :, :, min(step, 1), :]
                    mm = pe.matmul(bank(hf, 2 + step % 2)[:, q * P:(q + 1) * P], stat[:, hf, q, :], rd, start=True, stop=True)
                mm.then_inc(s["lvl_mm"], 1)

            for step in range(7):
                for hf in range(2):
                    level(step, hf)
                if step == 0:
                    gates(0)
                    gates(1)
                if step in (2, 3):
                    context_keys(step - 2)
                if step in (4, 5):
                    context_values(step - 4)
            pe.wait_ge(s["kc_done"], 2)
            for hf in range(2):
                pe.wait_ge(s["att_done"], 12 + hf + 1)
                for q in range(HP):
                    stay_warm(1, 1)
                    for h in range(NH):
                        for par in range(2):
                            rows = slice(64 * par, 64 * par + 64)
                            mm = pe.matmul(ps[:, TAIL[hf]["o"]][rows, q * D + h * DV:q * D + (h + 1) * DV], attT[rows, hf, q * NH + h, :],
                                           v_tm[rows, hf, q, h * DV:(h + 1) * DV], start=True, stop=True)
                mm.then_inc(s["o_mm"], 1)

            def transposes(b, src, signal, pairs_of=None, before=0):
                for q in range(HP):
                    if pairs_of:
                        pe.wait_ge(s[pairs_of], before + q + 1)
                    mm = pe.transpose(ps[:, b, q * P:(q + 1) * P], src[:, q, :], ident)
                mm.then_inc(s[signal], 1)

            def project(hf, b, w):
                for q in range(HP):
                    mm = pe.matmul(ps[:, b, q * P:(q + 1) * P], oT[:, hf, q * P:(q + 1) * P], w, start=True, stop=True)
                mm.then_inc(s["proj_mm"], 1)

            for hf in range(2):
                if hf == 0:
                    stay_warm(14, 1)
                pe.wait_ge(s["gout_done"], hf + 1)
                transposes(TAIL[hf]["oT"], gout[:, hf], "oT_mm")
                stay_warm(3, 1)
                pe.wait_ge(s["oT_done"], hf + 1)
                project(hf, TAIL[hf]["proj"], const("o_wT"))
            def turn_x1(hf):
                transposes(TAIL[hf]["x1T"], x1[:, hf], "x1T_mm", "x1_done", HP * hf)

            def project_queries(hf):
                pe.wait_ge(s["x1T_done"], hf + 1)
                src = xTn[:, hf, :].rearrange("p (n a s) -> p a n s", a=2, s=S)
                for g in range(2):
                    for par in range(2):
                        mm = pe.matmul(ps[64 * par:64 * par + 64, TAIL[hf]["q"], g * 256:(g + 1) * 256], const("W_Q")[:, 64 * g:64 * g + 64],
                                       src[:, par], start=True, stop=True)
                mm.then_inc(s["q_mm"], 1)

            stay_warm(2, 1)
            turn_x1(0)
            stay_warm(3, 1)
            project_queries(0)
            stay_warm(4, 1)
            pe.wait_ge(s["vhead_done"], 2)
            N2 = 2 * NPAIR

            def scores(i):
                q, g = i // 2, i % 2
                if i % NPAIR < 2:
                    pe.wait_ge(s["qdiag_done"], 2 * (i // NPAIR) + g + 1)
                if g == 0:
                    pe.wait_ge(s["khead_done"], q + 1)
                if i >= 2:
                    pe.wait_ge(s["scen_done"], i - 1)
                k_h, k_l = khead_h[:, g, q % KRING], khead_l[:, g, q % KRING]
                pe.matmul(ps[:, i % 2, :], qdiag_h[:, g, q, :], k_h, start=True, stop=False)
                pe.matmul(ps[:, i % 2, :], qdiag_h[:, g, q, :], k_l, start=False, stop=False)
                if i % NPAIR < 2:
                    pe.wait_ge(s["qrest_done"], 2 * (i // NPAIR) + g + 1)
                pe.matmul(ps[:, i % 2, :], qdiag_l[:, g, q, :], k_h, start=False, stop=False)
                pe.matmul(ps[:, i % 2, :], const("parsel"), mask_row[:, q, None, :].broadcast_to([2, 8, S]),
                          start=False, stop=True).then_inc(s["s_mm"], 1)

            def weigh(i):
                q, g = i // 2, i % 2
                if i >= 2:
                    pe.wait_ge(s["pT_done"], i - 1)
                pe.wait_ge(s["prob_done"], i + 1)
                for c in range(4):
                    mm = pe.transpose(ps[:, 2 + i % 2, c * P:(c + 1) * P], prob[:, i % 2, c * P:(c + 1) * P], ident)
                mm.then_inc(s["pT_mm"], 1)

            def values(i):
                q, g = i // 2, i % 2
                pe.wait_ge(s["pT_done"], i + 1)
                if q >= 2 and g == 0:
                    pe.wait_ge(s["oatt_done"], q - 1)
                o = ps[:, 4 + q % 2, 0:288].rearrange("p (a c x) -> p a c x", a=2, c=8)
                for c in range(4):
                    mm = pe.matmul(o[:, :, 4 * g + c, :], probT[:, i % 2, c, :],
                                   vhead[:, q, :, 4 * g + c].rearrange("p a h x -> p a (h x)"), start=True, stop=True)
                mm.then_inc(s["pv_mm"], 1)

            def turn_outputs(hf):
                pe.wait_ge(s["oatt_done"], HP * hf + HP)
                transposes(AFTER[hf]["oT"], oatt[:, HP * hf:HP * hf + HP].rearrange("p n h d -> p n (h d)"), "oT_mm")

            def project_outputs(hf):
                pe.wait_ge(s["oT_done"], 2 + hf + 1)
                project(hf, AFTER[hf]["proj"], const("W_O"))

            def turn_x2(hf):
                transposes(AFTER[hf]["x2T"], x2[:, hf], "x2T_mm", "x2_done", HP * hf)

            def router_hidden(hf):
                pe.wait_ge(s["x2T_done"], hf + 1)
                pe.matmul(ps[:, AFTER[hf]["hr"], :], const("router_w1"), xTn[:, hf, :], start=True, stop=True).then_inc(s["hr_mm"], 1)

            def router_logits(hf):
                pe.wait_ge(s["hr_done"], hf + 1)
                for second in range(2):
                    for g in range(4):
                        b = 2 * g + second
                        mm = pe.matmul(ps[2 * E * g:2 * E * g + 2 * E, AFTER[hf]["lg"], 0:S], const("router_w2")[:, (1 - second) * E:(3 - second) * E],
                                       hr[:, hf, b * S:(b + 1) * S], start=(second == 0), stop=(second == 1), skip_group_check=True)
                mm.then_inc(s["lg_mm"], 1)

            for i in range(N2 + 3):
                if i < N2:
                    scores(i)
                if i == 1:
                    turn_x1(1)
                if i == 13:
                    project_outputs(0)
                if 2 <= i < N2 + 2:
                    if i >= 16:
                        stay_warm(2, 6)
                    weigh(i - 2)
                if i == 2:
                    project_queries(1)
                if i >= 3:
                    values(i - 3)
                if i == 11:
                    turn_outputs(0)
                if i == 17:
                    turn_x2(0)
                if i == 18:
                    router_hidden(0)
            turn_outputs(1)
            stay_warm(3, 2)
            project_outputs(1)
            router_logits(0)
            stay_warm(18, 2)
            turn_x2(1)
            stay_warm(3, 2)
            router_hidden(1)
            def columns(hf):
                pe.wait_ge(s["lexp_done"], hf + 1)
                pe.wait_ge(s["dwgt_done"], hf + 1)
                b = AFTER[hf]["lg"]
                for eg in range(4):
                    pe.matmul(ps[:, b, 128 + eg * 8:136 + eg * 8], didx[:, hf, EG * eg:EG * eg + EG, :].rearrange("p e j -> p (e j)"),
                              const("bsel8b"), start=True, stop=True)
                    mm = pe.matmul(ps[:, b, 192 + eg * 8:200 + eg * 8], dwgt[:, hf, EG * eg:EG * eg + EG, :].rearrange("p e j -> p (e j)"),
                                   const("bsel8"), start=True, stop=True)
                mm.then_inc(s["col_mm"], 1)

            def row(q):
                if q % HP == 0:
                    pe.wait_ge(s["didx_done"], q // HP + 1)
                if q >= 2:
                    pe.wait_ge(s["pick_done"], q - 1)
                pe.matmul(ps[:, ROWS[q % 2], :], const("bsel")[:, (q % HP) * P:(q % HP + 1) * P],
                          didx[:, q // HP].rearrange("p e j -> p (e j)"), start=True, stop=True).then_inc(s["row_mm"], 1)

            def gather(q):
                hf = q // HP
                if q % HP == 0:
                    pe.wait_ge(s["x2l_done"], hf + 1)
                pe.wait_ge(s["pick_done"], q + 1)
                for k, (par, part) in enumerate(GATHER):
                    rows = slice(64 * par, 64 * par + 64)
                    if q >= 1:
                        if k < GACT[q - 1]:
                            pe.wait_ge(s["xg_act"], sum(GACT[:q - 1]) + k + 1)
                        else:
                            pe.wait_ge(s["xg_dve"], sum(4 - n for n in GACT[:q]))
                    if k == 0:
                        stay_warm(2, GBANK[0])
                    pe.matmul(ps[:, GBANK[k], :], (x2h, x2l)[part][rows, hf, q % HP, :], pick[rows, q % 2, :],
                              start=True, stop=True).then_inc(s["xg_mm"], 1)

            stay_warm(6, 2)
            row(0)
            row(1)
            router_logits(1)
            stay_warm(3, 2)
            gather(0)
            row(2)
            gather(1)
            row(3)
            gather(2)
            gather(3)
            row(4)
            row(5)
            columns(0)
            gather(4)
            row(6)
            gather(5)
            row(7)
            gather(6)
            gather(7)
            stay_warm(4, ROWS[0])
            pe.wait_ge(s["xg_act"], sum(GACT))
            pe.wait_ge(s["xg_dve"], 4 * NPAIR - sum(GACT))

            def three(out_ps, w_at, rhs_h, rhs_l, first, last):
                w_h, w_l = wh[:, w_at[0], w_at[1], w_at[2]], wl[:, w_at[0], w_at[1], w_at[2]]
                pe.matmul(out_ps, w_h, rhs_h, start=first, stop=False)
                pe.matmul(out_ps, w_h, rhs_l, start=False, stop=False)
                return pe.matmul(out_ps, w_l, rhs_h, start=False, stop=last)

            def up(e):
                pe.wait_ge(s["wl_done"], e + 1)
                for f in range(2):
                    fs = slice(f * P, (f + 1) * P)
                    r_h, r_l = (x[:, e].rearrange("p b j -> p (b j)") for x in (xh, xl))
                    if e >= 1:
                        pe.wait_ge(s["sg_done"], 2 * (e - 1) + f + 1)
                    three(ps[:, 2 * f, :], (e % 3, 0, fs), r_h, r_l, True, True).then_inc(s["gate_mm"], 1)
                    if e >= 1:
                        pe.wait_ge(s["hid_done"], 2 * (e - 1) + f + 1)
                    three(ps[:, 2 * f + 1, :], (e % 3, 1, fs), r_h, r_l, True, True).then_inc(s["up_mm"], 1)

            def down(e):
                if e >= 1:
                    pe.wait_ge(s["yT_done"], e)
                for f in range(2):
                    pe.wait_ge(s["hl_done"], 2 * e + f + 1)
                    mm = three(ps[:, 4, :], (e % 3, 2, slice(f * P, (f + 1) * P)), hid_h[:, e % 2, f, :], hid_l[:, e % 2, f, :], f == 0, f == 1)
                mm.then_inc(s["y_mm"], 1)

            def turn(k):
                eg, t = k // 4, k % 4
                pe.wait_ge(s["yT_done"], EG * eg + EG)
                if 1 <= k < 12:
                    pe.wait_ge(s["y_done"], k)
                for b in range(4):
                    mm = pe.transpose(ps[:, TURN[k], b * P:(b + 1) * P],
                                      yT[:, eg % 2, 4 * t + b].rearrange("p e j -> p (e j)"), ident)
                mm.then_inc(s["yTT_mm"], 1)

            def put(k):
                eg, t = k // 4, k % 4
                if k < 12:
                    pe.wait_ge(s["y_done"], k + 1)
                elif k % 2 == 0:
                    pe.wait_ge(s["y_done"], 13 + (k - 12) // 2)
                else:
                    pe.wait_ge(s["y_act"], 1 + (k - 12) // 2)
                if k == 0:
                    pe.wait_ge(s["pcol_done"], 2)
                if k % 2 == 0:
                    pe.wait_ge(s["place_done"], k // 2 + 1)
                for b in range(4):
                    bb = 4 * t + b
                    q, par = bb // 2, bb % 2
                    mm = pe.matmul(ps[64 * par:64 * par + 64, 6 + q // HP, (q % HP) * D:(q % HP + 1) * D], place[:, eg, bb, :], y[:, k % 4, b, :],
                                   start=(eg == 0 and q % HP == 0), stop=(eg == 3), skip_group_check=True)
                mm.then_inc(s["moe_mm"], 1)

            def add_x2(hf):
                for x in (x2h, x2l):
                    pe.matmul(ps[:, 6 + hf, :], ident_r[:], x[:, hf].rearrange("p q d -> p (q d)"), start=False, stop=False, skip_group_check=True)

            for e in range(E):
                up(e)
                if e >= 6:
                    put(e - 6)
                if e >= 5:
                    turn(e - 5)
                if e >= 1:
                    down(e - 1)
                if e == 1:
                    columns(1)
            pe.wait_ge(s["ident_done"], 1)
            for hf in range(2):
                add_x2(hf)
            down(E - 1)
            put(10)
            turn(11)
            turn(12)
            turn(13)
            put(11)
            turn(14)
            turn(15)
            for k in range(12, 16):
                put(k)

        @block.gpsimd
        def _(pool):
            done = [0]

            def link(ins):
                done[0] += 1
                ins.then_inc(pool_chain, 1)
                pool.wait_ge(pool_chain, done[0])

            pool.memset(minus_half[:], -0.5).then_inc(s["eps_done"], 1)
            pool.memset(eps[:], EPS).then_inc(s["eps_done"], 1)
            for t in (kbonus, kdecay):
                pool.memset(t[:], 0.0).then_inc(s["zeroed"], 1)
            token_delta(pool, 1)
            xh = xT[:].rearrange("p (f b) s -> p f (b s)", f=2)
            for n in range(5):
                pool.wait_ge(s["muls_done"], 2 * n + 2)
                pool.tensor_tensor(shiftd[:, 1, n, :], shiftd[:, 1, n, :], xh[:, 1, :], ALU.add).then_inc(shifted[1], 1)
            pool.memset(vhead[:], 0.0).then_inc(s["zeroed"], 1)
            pool.wait_ge(s["zeroed"], 3)
            for hh in range(2):
                link(pool.memset(vhead[64 * hh:64 * hh + 64, :, :, :, hh, XD:XD + 1].rearrange("p n a c x -> p (n a c) x"), 1.0))
            pool.wait_ge(s["kdecay_done"], 2)
            for lv in range(5):
                n = LEVELS[lv]
                for hf in range(2):
                    if lv == 0:
                        pool.wait_ge(s["tot_ready"], hf + 1)
                    if lv >= 1:
                        pool.wait_ge(s["upd_t"], 2 * (lv - 1) + hf + 1)
                        pool.wait_ge(s["lvl_mm"], 2 * (lv + 1) + hf + 1)
                        pool.wait_ge(s["upd_k"], 2 * (lv - 1) + hf + 1)
                    if 2 * lv + hf >= 1:
                        pool.wait_ge(s["upd_k"], 2 * lv + hf)
                    tot = total[lv][:, hf].rearrange("p g (b two) -> p g b two", two=2)
                    for par in range(2):
                        rows = slice(64 * par, 64 * par + 64)
                        kd = kdecay[rows, hf, :, 64 * par:64 * par + 64].rearrange("p q (b two n) -> p q b two n", two=2, n=n)[:, :, :, 0, :]
                        tk = tot[rows].rearrange("p (q h) b two -> p q h b two", h=NH)[:, :, 0, :, 1]
                        mm = pool.tensor_tensor(kd, kd, tk[:, :, :, None].broadcast_to([64, HP, S // (2 * n), n]), ALU.mult)
                        if par == 0:
                            link(mm)
                    mm.then_inc(s["upd_k"], 1)
            pool.wait_ge(s["upd_k"], 10)
            pool.wait_ge(s["g_mm"], 2)
            pool.memset(qdiag_h[:].bitcast(F32), 0.0).then_inc(s["zeroed"], 1)
            pool.memset(qdiag_l[:].bitcast(F32), 0.0).then_inc(s["zeroed"], 1)
            pool.wait_ge(ld_wb, 16)
            for hf in range(2):
                half_gate = gate_t[:, hf].rearrange("p (q d) -> p q d", d=D)
                pool.wait_ge(s["ghalf_done"], hf + 1)
                pool.tensor_tensor(gate[:, hf].rearrange("p (q d) -> p q d", d=D), half_gate,
                                   const("gnw")[:, None, :].broadcast_to([P, HP, D]), ALU.mult).then_inc(s["gw_done"], 1)
                pool.wait_ge(s["gw_done"], hf + 1)
                pool.tensor_tensor(half_gate, half_gate, const("gnb")[:, None, :].broadcast_to([P, HP, D]), ALU.mult).then_inc(s["gb_done"], 1)
            pool.wait_ge(s["eps_done"], 2)

            def inverse_deviation(k, hf):
                pool.wait_ge(s["veps_done"], 2 * (k - 1) + hf + 1)
                pool.tensor_tensor(rstd[:, hf], veps[:, hf], minus_half[:], ALU.pow).then_inc(s["rstd_done"], 1)

            for hf in range(2):
                pool.wait_ge(s["kch_done"], hf + 1)
                link(pool.tensor_tensor(kc_l[:, hf], kc[:, hf], kc_h[:, hf], ALU.subtract))
            for hf in range(2):
                for q in range(HP):
                    if hf == 0 and q >= 2:
                        h2 = q - 2
                        pool.wait_ge(s["x1T_mm"], h2 + 1)
                        pool.tensor_tensor(x1[:, h2], x1[:, h2], const("b_O")[:, None, :].broadcast_to([P, HP, D]), ALU.add).then_inc(s["x1b_done"], 1)
                    if HP * hf + q >= KRING:
                        pool.wait_ge(s["s_mm"], 2 * (HP * hf + q - KRING) + 2)
                    for g in range(2):
                        for keys, spread in ((kc_h, khead_h), (kc_l, khead_l)):
                            kq = keys[:, hf, g, q, None, :].broadcast_to([P, 8, S])
                            mm = pool.tensor_tensor(spread[:, g, q % KRING], kq, const("hm8")[:, :, None].broadcast_to([P, 8, S]), ALU.mult)
                    mm.then_inc(s["khead_done"], 1)
            for hf in range(2):
                inverse_deviation(1, hf)
                pool.wait_ge(s["x2h_done"], hf + 1)
                pool.tensor_tensor(x2l[:, hf], x2[:, hf], x2h[:, hf].bitcast(F32), ALU.subtract).then_inc(s["x2l_done"], 1)

            def rest_of_weights(e):
                pool.wait_ge(s["wh_done"], e + 1)
                pool.tensor_tensor(wl[:, e % 3], ew[:, e % WRING], wh[:, e % 3].bitcast(F32), ALU.subtract).then_inc(s["wl_done"], 1)

            for e in range(2):
                rest_of_weights(e)
            for hf in range(2):
                pool.wait_ge(s["topw_done"], hf + 1)
                pool.tensor_tensor(dwgt[:, hf], topw[:, hf, None, :].broadcast_to([P, E, CAP]),
                                   const("hme")[:, :, None].broadcast_to([P, E, CAP]), ALU.mult).then_inc(s["dwgt_done"], 1)
            for e in range(2, E):
                rest_of_weights(e)
                if 5 <= e < 13:
                    eg, hf = (e - 5) // 2, (e - 5) % 2
                    pool.wait_ge(s["eq_done"], e - 4)
                    pl = place[:, eg, 8 * hf:8 * hf + 8, :]
                    pool.tensor_tensor(pl, pl, pcol[:, hf, 1, eg, :, None].broadcast_to([P, 8, S]), ALU.mult).then_inc(s["place_done"], 1)
            for hf in range(2):
                inverse_deviation(2, hf)

        @block.scalar
        def _(act):
            done = [0]

            def link(ins):
                done[0] += 1
                ins.then_inc(act_chain, 1)
                act.wait_ge(act_chain, done[0])

            def bring_table(function):
                act.activation(table_call[:], eps[:], function)

            act.dma_start(w0[:], ap["w0"]).then_inc(ld_w0, 16)
            act.dma_start(wa[:], ap["wa"]).then_inc(ld_wa, 16)
            act.wait_ge(s["eps_done"], 2)
            bring_table(ACT.Tanh)
            act.wait_ge(ld_w0, 16)
            for hf in range(2):
                act.wait_ge(s["low1_mm"], hf + 1)
                act.activation(low1[:, hf, :], bank(hf, 0), ACT.Tanh).then_inc(s["low1_done"], 1)
            for hf in range(2):
                act.wait_ge(s["mix_mm"], 2 * hf + 1)
                act.activation(mixA[:, hf, :], bank(hf, 1), ACT.Tanh, bias=const("xl_b2")).then_inc(s["mixA_done"], 1)
                act.wait_ge(s["mix_mm"], 2 * hf + 2)
                act.activation(mixB[:, hf, :], bank(hf, 2), ACT.Tanh, bias=const("xl_b24")).then_inc(s["mixB_done"], 1)
            act.wait_ge(ld_wa, 16)
            for hf in range(2):
                act.wait_ge(s["w1_mm"], hf + 1)
                act.activation(wlow[:, hf, :], bank(hf, 1)[0:64, :], ACT.Tanh).then_inc(s["wlow_done"], 1)
            for hf in range(2):
                act.wait_ge(s["v_mm"], hf + 1)
                act.activation(v_tm[:, hf].rearrange("p q d -> p (q d)"), bank(hf, 2), ACT.Copy).then_inc(s["v_done"], 1)
                act.wait_ge(s["k_mm"], hf + 1)
                if hf == 0:
                    act.wait_ge(s["zeroed"], 2)
                kps = bank(hf, 3)[:, HP * S:].rearrange("p (q s) -> p q s", s=S)
                for par in range(2):
                    rows = slice(64 * par, 64 * par + 64)
                    mm = act.activation(kbonus[rows, hf, :, 64 * par:64 * par + 64], kps[rows], ACT.Copy, scale=const("bonus")[rows])
                mm.then_inc(s["kbonus_done"], 1)
            for hf in range(2):
                kps = bank(hf, 3)[:, HP * S:].rearrange("p (q s) -> p q s", s=S)
                for par in range(2):
                    rows = slice(64 * par, 64 * par + 64)
                    mm = act.activation(kdecay[rows, hf, :, 64 * par:64 * par + 64], kps[rows], ACT.Copy)
                mm.then_inc(s["kdecay_done"], 1)

            def decays(hf):
                act.wait_ge(s["w2_mm"], hf + 1)
                act.activation(expw[:, hf, :], bank(hf, 1)[:, 0:HP * S], ACT.Exp, bias=const("w_b")).then_inc(s["expw_done"], 1)
                act.wait_ge(s["expw_done"], hf + 1)
                for h in range(NH):
                    tt = total[0][:, hf].rearrange("p (q h) s -> p q h s", h=NH)[:, :, h, :]
                    mm = act.activation(tt, expw[:, hf, :].rearrange("p (q s) -> p q s", s=S), ACT.Exp, scale=-1.0)
                mm.then_inc(s["tot_ready"], 1)

            decays(0)
            for hf in range(2):
                act.wait_ge(s["lvl_mm"], hf + 1)
                kps = bank(hf, 3)[:, HP * S:].rearrange("p (q s two) -> p q s two", two=2, q=HP)
                for par in range(2):
                    rows = slice(64 * par, 64 * par + 64)
                    ke = kbonus[rows, hf, :, 64 * par:64 * par + 64].rearrange("p q (s two) -> p q s two", two=2)
                    mm = act.activation(ke[:, :, :, 0], kps[rows][:, :, :, 0], ACT.Copy)
                mm.then_inc(s["kmix_done"], 1)
            decays(1)
            for hf in range(2):
                act.wait_ge(s["g_mm"], hf + 1)
                act.activation(gate_t[:, hf, :], bank(hf, 0), ACT.Tanh, scale=0.5).then_inc(s["gate_t_done"], 1)
            for hf in range(2):
                act.wait_ge(s["gate_done"], hf + 1)
                act.activation(gate_t[:, hf, :], gate[:, hf, :], ACT.Copy, scale=0.5).then_inc(s["ghalf_done"], 1)
            act.wait_ge(ld_wb, 16)
            for hf in range(2):
                act.wait_ge(s["kv_mm"], hf + 1)
                for g in range(2):
                    mm = act.activation(mixB[:, hf, 256 * g:256 * g + 256], bank(hf, 1)[:, 256 * g:256 * g + 256], ACT.Identity,
                                        bias=const("b_K")[:, g:g + 1])
                mm.then_inc(s["kc_done"], 1)
                act.wait_ge(s["kc_done"], hf + 1)
                act.activation(kc_h[:, hf].bitcast(F32R), kc[:, hf], ACT.Copy).then_inc(s["kch_done"], 1)
            for g in range(2):
                mm = act.activation(bqs[:, g:g + 1], const("b_Q")[:, g:g + 1], ACT.Copy, scale=XD ** -0.5)
            mm.then_inc(s["const_done"], 1)
            bring_table(ACT.Sqrt)
            for hf in range(2):
                act.wait_ge(s["gcen_done"], hf + 1)
                act.activation(gsq[:, hf], gcen[:, hf], ACT.Square).then_inc(s["gsq_done"], 1)
                act.wait_ge(s["gvar_done"], hf + 1)
                act.activation(gstd[:, hf], gvar[:, hf], ACT.Sqrt, bias=eps[:], scale=1.0 / DV).then_inc(s["gstd_done"], 1)

            def copy_T(dst, hf, b, mm_sem, k, done_sem):
                act.wait_ge(s[mm_sem], k)
                act.activation(dst[:, hf, :], ps[:, b, :], ACT.Copy).then_inc(s[done_sem], 1)

            for hf in range(2):
                copy_T(oT, hf, TAIL[hf]["oT"], "oT_mm", hf + 1, "oT_done")

            def deviation(hf):
                act.wait_ge(s["var_done"], hf + 1)
                act.activation(std[:, hf], mv[:, hf, :, 1], ACT.Sqrt, bias=eps[:]).then_inc(s["std_done"], 1)

            deviation(0)
            copy_T(xTn, 0, TAIL[0]["x1T"], "x1T_mm", 1, "x1T_done")
            deviation(1)
            bring_table(ACT.Exp)
            act.wait_ge(s["zeroed"], 5)

            def queries(hf, g):
                act.wait_ge(s["query_done"], 2 * hf + g + 1)
                for par in range(2):
                    rows = slice(64 * par, 64 * par + 64)
                    mm = act.activation(qdiag_h[rows, g, HP * hf:HP * hf + HP, 64 * par:64 * par + 64],
                                        query[rows, hf, g].rearrange("p (q s) -> p q s", s=S), ACT.Copy)
                mm.then_inc(s["qdiag_done"], 1)

            queries(0, 0)
            queries(0, 1)
            N2 = 2 * NPAIR
            for i in range(N2 + 1):
                if i == 12:
                    copy_T(oT, 0, AFTER[0]["oT"], "oT_mm", 3, "oT_done")
                if i < N2:
                    act.wait_ge(s["scen_done"], i + 1)
                    if i >= 2:
                        act.wait_ge(s["pT_mm"], i - 1)
                    act.activation(prob[:, i % 2, :], scen[:, i % 2].rearrange("p h s -> p (h s)"), ACT.Exp).then_inc(s["prob_done"], 1)
                if i == 0:
                    copy_T(xTn, 1, TAIL[1]["x1T"], "x1T_mm", 2, "x1T_done")
                if i in (4, 6):
                    queries(1, i // 2 - 2)
                if i >= 1:
                    act.wait_ge(s["pT_mm"], i)
                    if i >= 3:
                        act.wait_ge(s["pv_mm"], i - 2)
                    act.activation(probT[:, (i - 1) % 2].rearrange("p c q -> p (c q)"), ps[:, 2 + (i - 1) % 2, :], ACT.Copy).then_inc(s["pT_done"], 1)

            def router_tanh(hf):
                act.wait_ge(s["hr_mm"], hf + 1)
                act.activation(hr[:, hf, :], ps[:, AFTER[hf]["hr"], :], ACT.Tanh, scale=0.5).then_inc(s["th_done"], 1)

            def round_x2(hf):
                act.wait_ge(s["x2_done"], HP * hf + HP)
                act.activation(x2h[:, hf], x2[:, hf], ACT.Copy).then_inc(s["x2h_done"], 1)

            def router_exp(hf):
                act.wait_ge(s["lmax_done"], hf + 1)
                act.activation(lexp[:, hf, :], ps[:, AFTER[hf]["lg"], 0:S], ACT.Exp, bias=lmax[:, hf:hf + 1], scale=0.5,
                               accum_out=lsum[:, hf:hf + 1]).then_inc(s["lexp_done"], 1)

            def round_weights(e):
                act.wait_ge(ld_e[e // 2 % 2], 16 * (e // 4 + 1))
                if e >= 3:
                    act.wait_ge(s["y_mm"], e - 2)
                act.activation(wh[:, e % 3], ew[:, e % WRING], ACT.Copy).then_inc(s["wh_done"], 1)

            def gathered(q):
                for k in range(GACT[q]):
                    par, part = GATHER[k]
                    act.wait_ge(s["xg_mm"], 4 * q + k + 1)
                    act.activation((xh, xl)[part][:, :, 2 * q + par, :], ps[:, GBANK[k], :].rearrange("p (e j) -> p e j", e=E),
                                   ACT.Copy).then_inc(s["xg_act"], 1)

            copy_T(xTn, 0, AFTER[0]["x2T"], "x2T_mm", 1, "x2T_done")
            router_tanh(0)
            copy_T(oT, 1, AFTER[1]["oT"], "oT_mm", 4, "oT_done")
            round_x2(0)
            router_exp(0)
            round_weights(0)
            copy_T(xTn, 1, AFTER[1]["x2T"], "x2T_mm", 2, "x2T_done")
            round_weights(1)
            router_tanh(1)
            round_x2(1)
            router_exp(1)
            act.activation(ident_r[:], ident, ACT.Copy).then_inc(s["ident_done"], 1)
            for q in range(NPAIR):
                gathered(q)
                if q == 3:
                    bring_table(ACT.Silu)
            for e in range(E + 1):
                if e < E:
                    for f in range(2):
                        k = 2 * e + f
                        act.wait_ge(s["gate_mm"], k + 1)
                        if k >= 2:
                            act.wait_ge(s["hid_done"], k - 1)
                        act.activation(sg[:, f, :], ps[:, 2 * f, :], ACT.Silu).then_inc(s["sg_done"], 1)
                    for f in range(2):
                        act.wait_ge(s["hid_done"], 2 * e + f + 1)
                        if e >= 2:
                            act.wait_ge(s["y_mm"], e - 1)
                        act.activation(hid_h[:, e % 2, f, :], hid[:, f, :], ACT.Copy).then_inc(s["hh_done"], 1)
                if e >= 1:
                    d = e - 1
                    act.wait_ge(s["y_mm"], d + 1)
                    if d >= 8 and d % 4 == 0:
                        act.wait_ge(s["yTT_mm"], 4 * (d // 4 - 1))
                    act.activation(yT[:, (d // 4) % 2, :, d % 4, :], ps[:, 4, :].rearrange("p (b j) -> p b j", b=B), ACT.Copy).then_inc(s["yT_done"], 1)
                if e + 2 < E:
                    round_weights(e + 2)
            act.wait_ge(s["yTT_mm"], 14)
            act.wait_ge(s["moe_mm"], 10)
            act.activation(y[:, 1].rearrange("p b d -> p (b d)"), ps[:, TURN[13], :], ACT.Copy).then_inc(s["y_act"], 1)
            act.wait_ge(s["yTT_mm"], 16)
            act.wait_ge(s["moe_mm"], 12)
            act.activation(y[:, 3].rearrange("p b d -> p (b d)"), ps[:, TURN[15], :], ACT.Copy).then_inc(s["y_act"], 1)
            act.wait_ge(s["moe_mm"], 14)
            act.wait_ge(s["rstd_done"], 3)
            act.wait_ge(s["shift_done"], 1)
            for q in range(HP):
                act.activation(x3[:, 0, q, :], ps[:, 6, q * D:(q + 1) * D], ACT.Identity, bias=shift[:, q:q + 1],
                               scale=rstd[:, 0, q:q + 1]).then_inc(s["x3_act"], 1)

        @block.vector
        def _(dve):
            done = [0]

            def link(ins):
                done[0] += 1
                ins.then_inc(dve_chain, 1)
                dve.wait_ge(dve_chain, done[0])

            dve.memset(zeros[:], 0.0).then_inc(s["zeros_done"], 1)
            token_delta(dve, 0)
            dve.wait_ge(ld_w0, 16)
            xh = xT[:].rearrange("p (f b) s -> p f (b s)", f=2)
            dh = delta[:].rearrange("p (f b) s -> p f (b s)", f=2)
            for hf in range(2):
                dve.wait_ge(delta_done[hf], 2)
                dve.scalar_tensor_tensor(lerp[:, hf, :], dh[:, hf], const("mu"), xh[:, hf], ALU.mult, ALU.add).then_inc(s["lerp_done"], 1)
            link(dve.memset(attT[:], 0.0))
            dve.wait_ge(ld_c, 32)
            link(dve.tensor_scalar(mask_row[:], key_mask[:], MASKED, None, ALU.mult))
            slot = [0, 3, 1, 2, 0]
            dve.wait_ge(ld_wa, 16)
            for n in range(5):
                for hf in range(2):
                    dve.wait_ge(s["x2_mm"], 2 * n + hf + 1)
                    dve.scalar_tensor_tensor(shiftd[:, hf, n, :], bank(hf, slot[n]), const("x_bias")[:, n:n + 1], dh[:, hf],
                                             ALU.add, ALU.mult).then_inc(s["muls_done"], 1)
                dve.wait_ge(s["muls_done"], 2 * n + 1)
                dve.tensor_tensor(shiftd[:, 0, n, :], shiftd[:, 0, n, :], xh[:, 0], ALU.add).then_inc(shifted[0], 1)
            for hf in range(2):
                dve.wait_ge(s["r_mm"], hf + 1)
                rps = bank(hf, 3)[:, 0:HP * S].rearrange("p (q s) -> p q s", s=S)
                dve.tensor_tensor(rdecay[:, hf].rearrange("p (q h) s -> p q h s", h=NH), rps[:, :, None, :].broadcast_to([P, HP, NH, S]),
                                  const("hm4")[:, None, :, None].broadcast_to([P, HP, NH, S]), ALU.mult).then_inc(s["rx_ready"], 1)

            def gate_of(hf):
                dve.wait_ge(s["gate_t_done"], hf + 1)
                dve.scalar_tensor_tensor(gate[:, hf, :], gate_t[:, hf, :], 1.0, bank(hf, 0), ALU.add, ALU.mult).then_inc(s["gate_done"], 1)

            def context_values(hf):
                if hf == 0:
                    dve.wait_ge(pool_chain, 2)
                dve.wait_ge(s["kv_mm"], 2 + hf + 1)
                for hh in range(2):
                    rows = slice(64 * hh, 64 * hh + 64)
                    dst = vhead[rows, HP * hf:HP * hf + HP, :, :, hh, 0:XD].rearrange("p n a c x -> p (n a) c x")
                    mm = dve.tensor_tensor(dst, bank(hf, 0)[rows].rearrange("p (b c x) -> p b c x", c=8, x=XD),
                                           const("b_V")[rows].rearrange("p (c x) -> p c x", c=8)[:, None].broadcast_to([64, 8, 8, XD]), ALU.add)
                mm.then_inc(s["vhead_done"], 1)

            def double_decays(lv, hf):
                if lv == 0:
                    dve.wait_ge(s["tot_ready"], hf + 1)
                else:
                    dve.wait_ge(s["upd_t"], 2 * (lv - 1) + hf + 1)
                tot = total[lv][:, hf].rearrange("p g (b two) -> p g b two", two=2)
                dve.tensor_tensor(total[lv + 1][:, hf], tot[:, :, :, 0], tot[:, :, :, 1], ALU.mult).then_inc(s["upd_t"], 1)

            dve.wait_ge(ld_wb, 16)
            masks = const("masks").bitcast(U32).rearrange("p (l n) -> p l n", l=7)
            for step in range(7):
                n = LEVELS[max(step - 1, 0)]
                for hf in range(2):
                    if 1 <= step <= 4:
                        double_decays(step - 1, hf)
                    dve.wait_ge(s["lvl_mm"], 2 * step + hf + 1)
                    if 1 <= step <= 5:
                        lv = step - 1
                        if lv == 0:
                            dve.wait_ge(s["tot_ready"], hf + 1)
                            dve.wait_ge(s["rx_ready"], hf + 1)
                        else:
                            dve.wait_ge(s["upd_t"], 2 * (lv - 1) + hf + 1)
                            dve.wait_ge(s["upd_r"], 2 * (lv - 1) + hf + 1)
                        rd = rdecay[:, hf].rearrange("p g (b two n) -> p g b two n", two=2, n=n)[:, :, :, 1, :]
                        tt = total[lv][:, hf].rearrange("p g (b two) -> p g b two", two=2)[:, :, :, 0]
                        dve.tensor_tensor(rd, rd, tt[:, :, :, None].broadcast_to([P, HP * NH, S // (2 * n), n]), ALU.mult).then_inc(s["upd_r"], 1)
                    if step >= 1:
                        dve.wait_ge(s["att_done"], 2 * (step - 1) + hf + 1)
                    dst = attT[:, hf].rearrange("p g (b two n) -> p g b two n", two=2, n=n)[:, :, :, min(step, 1), :]
                    msk = masks[:, step].rearrange("p (b n) -> p b n", n=n)[:, None].broadcast_to([P, HP * NH, S // (2 * n), n])
                    src = bank(hf, 2 + step % 2).rearrange("p (g b n) -> p g b n", g=HP * NH, n=n)
                    dve.copy_predicated(dst, msk, src).then_inc(s["att_done"], 1)
                if step == 2:
                    gate_of(0)
                    gate_of(1)
            for hf in range(2):
                context_values(hf)
            def centre(hf):
                dve.wait_ge(s["o_mm"], hf + 1)
                o = ps[:, TAIL[hf]["o"]].rearrange("p (g v) -> p g v", v=DV)
                link(dve.reduce_sum(gsum[:, hf], o, AX_X))
                dve.scalar_tensor_tensor(gcen[:, hf], gsum[:, hf, :, None].broadcast_to([P, HP * NH, DV]), -1.0 / DV, o,
                                         ALU.mult, ALU.add).then_inc(s["gcen_done"], 1)

            def square_sum_and_weight(hf):
                dve.wait_ge(s["gsq_done"], hf + 1)
                dve.reduce_sum(gvar[:, hf], gsq[:, hf], AX_X).then_inc(s["gvar_done"], 1)
                dve.wait_ge(s["gw_done"], hf + 1)
                gc = gcen[:, hf].rearrange("p g v -> p (g v)")
                dve.tensor_tensor(gc, gc, gate[:, hf, :], ALU.mult).then_inc(s["gcw_done"], 1)

            def gated_norm(hf):
                dve.wait_ge(s["gstd_done"], hf + 1)
                link(dve.reciprocal(grstd[:, hf], gstd[:, hf]))
                dve.wait_ge(s["gcw_done"], hf + 1)
                dve.wait_ge(s["gb_done"], hf + 1)
                link(dve.tensor_tensor(gout[:, hf].rearrange("p q (h v) -> p (q h) v", v=DV), gcen[:, hf],
                                       grstd[:, hf, :, None].broadcast_to([P, HP * NH, DV]), ALU.mult))
                g2 = gout[:, hf].rearrange("p q d -> p (q d)")
                dve.tensor_tensor(g2, g2, gate_t[:, hf, :], ALU.add).then_inc(s["gout_done"], 1)

            centre(0)
            square_sum_and_weight(0)
            centre(1)
            gated_norm(0)
            square_sum_and_weight(1)
            gated_norm(1)

            def residual(k, hf, b, other):
                link(dve.tensor_tensor(res[:, hf], ps[:, b].rearrange("p (q d) -> p q d", q=HP), other, ALU.add))
                for q in range(HP):
                    mm = dve.bn_stats(stats[:, hf, q, :], res[:, hf, q, :])
                link(mm)
                variances(k, hf)

            def variances(k, hf):
                for q in range(HP):
                    mm = dve.bn_aggr(mv[:, hf, q, :], stats[:, hf, q, :])
                if k == 0:
                    mm.then_inc(s["var_done"], 1)
                    return
                link(mm)
                dve.tensor_scalar(veps[:, hf], mv[:, hf, :, 1], EPS, None, ALU.add).then_inc(s["veps_done"], 1)

            def normalise(k, hf, dst, signal):
                if k == 0:
                    dve.wait_ge(s["std_done"], hf + 1)
                    link(dve.reciprocal(rstd[:, hf], std[:, hf]))
                else:
                    dve.wait_ge(s["rstd_done"], 2 * (k - 1) + hf + 1)
                for q in range(HP):
                    dve.tensor_scalar(dst[:, hf, q, :], res[:, hf, q, :], mv[:, hf, q, 0:1], rstd[:, hf, q:q + 1],
                                      ALU.subtract, ALU.mult).then_inc(s[signal], 1)

            dve.wait_ge(ld_xtm, 16)
            for hf in range(2):
                dve.wait_ge(s["proj_mm"], hf + 1)
                residual(0, hf, TAIL[hf]["proj"], x_tm[:, HP * hf:HP * hf + HP, :])
                if hf == 0:
                    normalise(0, 0, x1, "x1_done")

            def divide(q):
                dve.wait_ge(s["pv_mm"], 2 * q + 2)
                for par in range(2):
                    rows = slice(64 * par, 64 * par + 64)
                    o = ps[rows, 4 + q % 2, 144 * par:144 * par + 144].rearrange("p (h x) -> p h x", x=XD + 1)
                    mm = dve.reciprocal(oden[rows, q % 2], o[:, :, XD])
                link(mm)
                for par in range(2):
                    rows = slice(64 * par, 64 * par + 64)
                    o = ps[rows, 4 + q % 2, 144 * par:144 * par + 144].rearrange("p (h x) -> p h x", x=XD + 1)
                    mm = dve.tensor_tensor(oatt[rows, q], o[:, :, 0:XD], oden[rows, q % 2, :, None].broadcast_to([64, XH, XD]), ALU.mult)
                mm.then_inc(s["oatt_done"], 1)

            def residual_x1(hf):
                dve.wait_ge(s["proj_mm"], 2 + hf + 1)
                dve.wait_ge(s["x1b_done"], hf + 1)
                residual(1, hf, AFTER[hf]["proj"], x1[:, hf])

            def full_queries(hf):
                dve.wait_ge(s["q_mm"], hf + 1)
                for g in range(2):
                    dve.tensor_scalar(query[:, hf, g], ps[:, TAIL[hf]["q"], 256 * g:256 * g + 256], XD ** -0.5, bqs[:, g:g + 1],
                                      ALU.mult, ALU.add).then_inc(s["query_done"], 1)

            def rest_of_queries(hf, g):
                dve.wait_ge(s["qdiag_done"], 2 * hf + g + 1)
                for par in range(2):
                    rows = slice(64 * par, 64 * par + 64)
                    block = (rows, g, slice(HP * hf, HP * hf + HP), slice(64 * par, 64 * par + 64))
                    mm = dve.tensor_tensor(qdiag_l[block], query[rows, hf, g].rearrange("p (q s) -> p q s", s=S),
                                           qdiag_h[block].bitcast(F32), ALU.subtract)
                mm.then_inc(s["qrest_done"], 1)

            dve.wait_ge(s["const_done"], 1)
            dve.wait_ge(s["zeroed"], 5)
            full_queries(0)
            normalise(0, 1, x1, "x1_done")
            rest_of_queries(0, 0)
            rest_of_queries(0, 1)

            for i in range(2 * NPAIR):
                if i == 3:
                    full_queries(1)
                if i in (5, 7):
                    rest_of_queries(1, (i - 5) // 2)
                q = i // 2
                dve.wait_ge(s["s_mm"], i + 1)
                sc = ps[:, i % 2, :].rearrange("p (h s) -> p h s", s=S)
                dve.tensor_reduce(smax[:, i % 2], sc, AX_X, ALU.max).then_inc(s["smax_done"], 1)
                dve.wait_ge(s["smax_done"], i + 1)
                if i >= 2:
                    dve.wait_ge(s["prob_done"], i - 1)
                dve.tensor_tensor(scen[:, i % 2], sc, smax[:, i % 2, :, None].broadcast_to([P, 8, S]), ALU.subtract).then_inc(s["scen_done"], 1)
                if i >= 4 and i % 2 == 0:
                    divide(i // 2 - 2)
                if i == 13:
                    residual_x1(0)
                if i == 15:
                    normalise(1, 0, x2, "x2_done")

            def router_gate(hf):
                dve.wait_ge(s["th_done"], hf + 1)
                dve.scalar_tensor_tensor(hr[:, hf, :], hr[:, hf, :], 1.0, ps[:, AFTER[hf]["hr"], :], ALU.add, ALU.mult).then_inc(s["hr_done"], 1)

            def router_max(hf):
                dve.wait_ge(s["lg_mm"], hf + 1)
                link(dve.tensor_reduce(lmax[:, hf:hf + 1], ps[:, AFTER[hf]["lg"], 0:S], AX_X, ALU.max))
                dve.tensor_scalar(lmax[:, hf:hf + 1], lmax[:, hf:hf + 1], -0.5, None, ALU.mult).then_inc(s["lmax_done"], 1)

            def router_softmax(hf):
                dve.wait_ge(s["lexp_done"], hf + 1)
                link(dve.reciprocal(lrec[:, hf:hf + 1], lsum[:, hf:hf + 1]))
                link(dve.tensor_scalar(pr[:, hf, 0], lexp[:, hf, :], lrec[:, hf:hf + 1], None, ALU.mult))

            def best_eight(hf, k):
                k8 = slice(8 * k, 8 * k + 8)
                link(dve.max(topv[:, hf, k8], pr[:, hf, k % 2]))
                link(dve.max_index(topi[:, hf, k8], topv[:, hf, k8], pr[:, hf, k % 2]))
                if k < CAP // 8 - 1:
                    link(dve.match_replace(pr[:, hf, (k + 1) % 2], topv[:, hf, k8], pr[:, hf, k % 2], -1.0))

            def positions(hf):
                link(dve.tensor_copy(topf[:, hf], topi[:, hf]))
                dve.tensor_tensor(didx[:, hf], topf[:, hf, None, :].broadcast_to([P, E, CAP]),
                                  const("hme")[:, :, None].broadcast_to([P, E, CAP]), ALU.mult).then_inc(s["didx_done"], 1)

            def weight_sum(hf):
                return dve.reduce_sum(tsum[:, hf:hf + 1], topv[:, hf], AX_X)

            def weight_sum_guard(hf):
                return dve.tensor_scalar(tsum[:, hf:hf + 1], tsum[:, hf:hf + 1], 1e-9, None, ALU.add)

            def weight_sum_inverse(hf):
                return dve.reciprocal(tsum[:, hf:hf + 1], tsum[:, hf:hf + 1])

            def normalised_weights(hf):
                dve.tensor_scalar(topw[:, hf], topv[:, hf], tsum[:, hf:hf + 1], None, ALU.mult).then_inc(s["topw_done"], 1)

            def columns(hf):
                dve.wait_ge(s["col_mm"], hf + 1)
                dve.tensor_copy(pcol[:, hf].rearrange("p a g b -> p a (g b)"),
                                ps[:, AFTER[hf]["lg"], 128:256].rearrange("p (a x) -> p a x", a=2)[:, :, 0:32]).then_inc(s["pcol_done"], 1)

            def gathered(q):
                par, part = GATHER[3]
                dve.wait_ge(s["xg_mm"], 4 * q + 4)
                dve.tensor_copy((xh, xl)[part][:, :, 2 * q + par, :], ps[:, GBANK[3], :].rearrange("p (e j) -> p e j", e=E)).then_inc(s["xg_dve"], 1)

            def make_pick(q):
                dve.wait_ge(s["row_mm"], q + 1)
                if q >= 2:
                    dve.wait_ge(s["xg_mm"], 4 * (q - 1))
                dve.tensor_scalar(pick[:, q % 2, :], ps[:, ROWS[q % 2], :], const("tcol"), None, ALU.is_equal).then_inc(s["pick_done"], 1)

            divide(6)
            divide(7)
            router_gate(0)
            residual_x1(1)
            router_max(0)
            router_softmax(0)
            best_eight(0, 0)
            normalise(1, 1, x2, "x2_done")
            for k in range(1, CAP // 8):
                best_eight(0, k)
            positions(0)
            router_gate(1)
            make_pick(0)
            router_max(1)
            make_pick(1)
            router_softmax(1)
            weight_sum(0)
            best_eight(1, 0)
            weight_sum_guard(0)
            make_pick(2)
            best_eight(1, 1)
            weight_sum_inverse(0)
            make_pick(3)
            best_eight(1, 2)
            normalised_weights(0)
            best_eight(1, 3)
            positions(1)
            make_pick(4)
            gathered(3)
            for step in (weight_sum, weight_sum_guard, weight_sum_inverse):
                link(step(1))
            normalised_weights(1)
            for q in range(4, NPAIR):
                if q + 1 < NPAIR:
                    make_pick(q + 1)
                gathered(q)

            def copy_y(k):
                dve.wait_ge(s["yTT_mm"], k + 1)
                if k >= 4:
                    dve.wait_ge(s["moe_mm"], k - 3)
                dve.tensor_copy(y[:, k % 4].rearrange("p b d -> p (b d)"), ps[:, TURN[k], :]).then_inc(s["y_done"], 1)

            for e in range(E):
                for f in range(2):
                    dve.wait_ge(s["sg_done"], 2 * e + f + 1)
                    dve.wait_ge(s["up_mm"], 2 * e + f + 1)
                    if e >= 1:
                        dve.wait_ge(s["hl_done"], 2 * (e - 1) + f + 1)
                    dve.tensor_tensor(hid[:, f, :], sg[:, f, :], ps[:, 2 * f + 1, :], ALU.mult).then_inc(s["hid_done"], 1)
                for f in range(2):
                    dve.wait_ge(s["hh_done"], 2 * e + f + 1)
                    dve.tensor_tensor(hid_l[:, e % 2, f, :], hid[:, f, :], hid_h[:, e % 2, f, :].bitcast(F32), ALU.subtract).then_inc(s["hl_done"], 1)
                if e == 2:
                    for hf in range(2):
                        columns(hf)
                    dve.wait_ge(s["pcol_done"], 2)
                if 3 <= e < 11:
                    eg, hf = (e - 3) // 2, (e - 3) % 2
                    dve.tensor_tensor(place[:, eg, 8 * hf:8 * hf + 8, :], const("trow")[:, None, :].broadcast_to([P, 8, S]),
                                      pcol[:, hf, 0, eg, :, None].broadcast_to([P, 8, S]), ALU.is_equal).then_inc(s["eq_done"], 1)
                if e >= 5:
                    copy_y(e - 5)
            copy_y(11)
            copy_y(12)
            copy_y(14)

            for hf in range(2):
                dve.wait_ge(s["moe_mm"], 12 + 2 * hf + 2)
                for q in range(HP):
                    mm = dve.bn_stats(stats[:, hf, q, :], ps[:, 6 + hf, q * D:(q + 1) * D])
                link(mm)
                variances(2, hf)
            dve.wait_ge(s["rstd_done"], 3)
            dve.scalar_tensor_tensor(shift[:], mv[:, 0, :, 0], -1.0, rstd[:, 0], ALU.mult, ALU.mult).then_inc(s["shift_done"], 1)
            dve.wait_ge(s["rstd_done"], 4)
            for q in range(HP):
                dve.tensor_scalar(x3[:, 1, q, :], ps[:, 7, q * D:(q + 1) * D], mv[:, 1, q, 0:1], rstd[:, 1, q:q + 1],
                                  ALU.subtract, ALU.mult).then_inc(s["x3_done"], 1)


def kernel(**inputs):
    import numpy as np
    import concourse.bacc as bacc
    from concourse.bass_utils import run_bass_kernel_spmd

    i = {k.removeprefix("L0_"): np.asarray(v) for k, v in inputs.items()}
    packs = {"w0": [], "wa": [], "wb": [], "cb": []}
    cols = {}

    def put(pack, name, a):
        a = np.asarray(a)
        a = a.reshape(a.shape[0], -1)
        full = np.zeros((P, a.shape[1]), a.dtype)
        full[:a.shape[0]] = a
        cols[name] = (pack, a.shape[0], sum(x.shape[1] for x in packs[pack]), a.shape[1])
        packs[pack].append(full)

    f32 = np.float32
    import ml_dtypes
    bf = ml_dtypes.bfloat16
    part = np.arange(P)
    tok = part % S
    put("w0", "mu", i["attn_x_proj_mu"][:, None])
    padded = lambda a, rows, columns: np.pad(a, ((0, rows - a.shape[0]), (0, columns - a.shape[1])))
    put("w0", "xl_w1T", padded(i["attn_xl_w1"].T, P, P))
    put("w0", "xl_w2T", padded(i["attn_xl_w2"].T, P, 2 * P))
    put("w0", "xl_b2", i["attn_xl_b2"][:P, None])
    put("w0", "xl_b24", padded(i["attn_xl_b2"][P:, None], P, 1))
    mixers = np.zeros((P, 5, D), f32)
    for n in range(5):
        mixers[n % 4 * R:(n % 4 + 1) * R, n] = i["attn_x_out_w"].T[n * R:(n + 1) * R]
    put("wa", "xout", mixers)
    put("wa", "x_bias", i["attn_x_bias"].T)
    put("wa", "r_wT", i["attn_r_w"].T)
    put("wa", "k_wT", i["attn_k_w"].T)
    put("wa", "w_w1T", i["attn_w_w1"].T)
    put("wa", "w_w2T", i["attn_w_w2"].T)
    put("wa", "v_wT", i["attn_v_w"].T)
    put("wa", "g_wT", i["attn_g_w"].T)
    put("wa", "w_b", np.concatenate([i["attn_w_b"]] * 2)[:, None])
    put("wa", "bonus", np.concatenate([i["attn_bonus"].reshape(-1)] * 2)[:, None])
    put("wa", "hm4", (part[:, None] % 64 // DK == np.arange(NH)).astype(f32))
    put("wb", "ident", np.eye(P, dtype=f32))
    put("wb", "o_wT", i["attn_o_w"].T)
    put("wb", "gnw", np.broadcast_to(i["attn_gn_weight"], (P, D)))
    put("wb", "gnb", np.broadcast_to(i["attn_gn_bias"], (P, D)))
    put("wb", "W_Q", i["xattn_W_Q"])
    put("wb", "W_K", i["xattn_W_K"])
    even_odd = lambda a: a.reshape(-1, XH // 2, 2, XD).transpose(0, 2, 1, 3).reshape(-1, D)
    put("wb", "W_V2", even_odd(i["xattn_W_V"]))
    put("wb", "W_O", i["xattn_W_O"])
    put("wb", "b_Q", np.tile(i["xattn_b_Q"].reshape(2, 64), (1, 2)).T)
    put("wb", "b_K", np.tile(i["xattn_b_K"].reshape(2, 64), (1, 2)).T)
    put("wb", "b_V", np.repeat(even_odd(i["xattn_b_V"]).reshape(2, 64), 64, axis=0))
    put("wb", "b_O", np.broadcast_to(i["xattn_b_O"], (P, D)))
    put("wb", "hm8", (part[:, None] % 64 // XD == np.arange(8)).astype(f32))
    put("wb", "router_w1", i["ffn_router_w1"])
    rw2 = np.zeros((P, 3 * E), f32)
    rw2[:, E:2 * E] = i["ffn_router_w2"]
    put("wb", "router_w2", rw2)
    put("wb", "hme", (part[:, None] % E == np.arange(E)).astype(f32))
    put("wb", "bsel8", (part[:, None] // E == np.arange(8)).astype(f32))
    put("wb", "tcol", tok[:, None].astype(f32))
    put("wb", "trow", np.broadcast_to(np.arange(S).astype(f32), (P, S)))
    put("cb", "bsel8b", (part[:, None] // E == np.arange(8)).astype(bf))
    put("cb", "bsel", np.stack([part[:, None] // E == 2 * q + part[None, :] // S for q in range(HP)], 1).astype(bf))
    put("cb", "parsel", (np.arange(2)[:, None] == part[None, :] // S).astype(bf))
    masks = []
    t = np.arange(S)
    for step in range(7):
        n = LEVELS[max(step - 1, 0)]
        ts = t.reshape(-1, 2, n)[:, min(step, 1), :].reshape(-1)
        src = tok[:, None]
        if step == 0:
            m = src == ts
        elif step == 1:
            m = (src == ts) | (src == ts - 1)
        else:
            m = src // n == ts // n - 1
        masks.append(m)
    put("wb", "masks", np.concatenate(masks, 1).astype(f32))

    arrays = {k: np.ascontiguousarray(np.concatenate(v, 1)) for k, v in packs.items()}
    arrays["x"] = np.ascontiguousarray(i["x"])
    arrays["xT"] = np.ascontiguousarray(i["x"].reshape(B * S, D).T)
    arrays["ctxT"] = np.ascontiguousarray(i["ctx_1024"].reshape(B * S, D).T)
    arrays["key_mask"] = np.ascontiguousarray(i["mask_BxS2_bk0"].reshape(NPAIR, 2, S).transpose(1, 0, 2))
    w3 = i["ffn_w3"].reshape(E, 2, P, D).transpose(2, 0, 1, 3).reshape(P, E, DFF)
    ew = np.stack([i["ffn_w1"].transpose(1, 0, 2), i["ffn_w2"].transpose(1, 0, 2), w3], 2)
    arrays["ew"] = np.ascontiguousarray(ew.reshape(P, E * 3 * DFF))

    nc = bacc.Bacc("TRN2", target_bir_lowering=False, num_devices=1)
    ap = {k: nc.dram_tensor("in_" + k, v.shape, mybir.dt.from_np(v.dtype), kind="ExternalInput").ap() for k, v in arrays.items()}
    out = nc.dram_tensor("out_0", (B, S, D), F32, kind="ExternalOutput").ap()
    decoder_kernel(nc, ap, cols, out)
    r = run_bass_kernel_spmd(nc, [{"in_" + k: v for k, v in arrays.items()}], core_ids=[0])
    return r.results[0]["out_0"]
```
